# Optimizing a Trainium2 kernel written in Bass

```python
import numpy as np
import jax
import jax.numpy as jnp

def _softmax(x, axis=-1):
    return jax.nn.softmax(x, axis=axis)

def _gelu(x):
    return jax.nn.gelu(x, approximate=True)

def _silu(x):
    return jax.nn.silu(x)

def _sigmoid(x):
    return jax.nn.sigmoid(x)

def _layernorm(x, axis=-1, eps=1e-05):
    m = jnp.mean(x, axis=axis, keepdims=True)
    v = jnp.var(x, axis=axis, keepdims=True)
    return (x - m) / jnp.sqrt(v + eps)

def _scatter_add(tgt, idx, src, axis=0):
    return tgt.at[idx].add(src)

def _segment_sum(src, seg, n):
    return jax.ops.segment_sum(src, seg, n)
kernel_name = 'mk_hybrid_d2_jaxref_r8_ef9804'

def setup_inputs(seed: int=0):
    np.random.seed(seed)
    _w = jnp.asarray

    def _L0_attn_a_setup():
        import jax, jax.numpy as jnp
        import numpy as np
        HIDDEN = 512
        N_HEADS = 32
        N_KV = 8
        HEAD_DIM = HIDDEN // N_HEADS
        Q_PER_KV = N_HEADS // N_KV
        SEQ = 256
        ROPE_BASE = 1000000.0
        POS_SCALE = 1.0
        SM_SCALE = 1.0 / HEAD_DIM
        BLOCK = 64
        LOCAL_BLOCKS = 16
        VERT_STRIDE = 8

        def _blocksparse_mask(seq_len):
            nb = seq_len // BLOCK
            qb = np.arange(nb)[:, None]
            kb = np.arange(nb)[None, :]
            bmask = (kb <= qb) & ((qb - kb < LOCAL_BLOCKS) | ((kb + 1) % VERT_STRIDE == 0))
            emask = np.kron(bmask, np.ones((BLOCK, BLOCK), dtype=bool))
            i = np.arange(seq_len)
            emask &= i[:, None] >= i[None, :]
            return jnp.asarray(emask)

        def _rope(x, cos, sin):
            x1, x2 = jnp.split(x, 2, axis=-1)
            rot = jnp.concatenate([-x2, x1], axis=-1)
            return x * cos[None, :, None, :] + rot * sin[None, :, None, :]
        key = jax.random.key(seed)
        k1, k2, k3, k4, k5 = jax.random.split(key, 5)
        qkv_out = (N_HEADS + 2 * N_KV) * HEAD_DIM
        return {'hidden_states': jax.random.normal(k1, (1, SEQ, HIDDEN), dtype=jnp.float32), 'w_qkv': jax.random.normal(k2, (qkv_out, HIDDEN), dtype=jnp.float32) * 0.02, 'b_qkv': jnp.zeros((qkv_out,), dtype=jnp.float32), 'w_dense': jax.random.normal(k3, (HIDDEN, HIDDEN), dtype=jnp.float32) * 0.02, 'b_dense': jnp.zeros((HIDDEN,), dtype=jnp.float32)}
    _L0_attn_a_in = _L0_attn_a_setup()

    def _L0_attn_b_setup():
        import jax, jax.numpy as jnp
        import numpy as np
        H = 512
        D = H // 4
        key = jax.random.key(seed)
        k1, k2, k3, k4, k5 = jax.random.split(key, 5)
        x = jax.random.normal(k1, (4, 512, H), dtype=jnp.float32)
        s_in = 1.0 / np.sqrt(H)
        Wqkv = jax.random.normal(k2, (H, 3 * D), dtype=jnp.float32) * s_in
        bqkv = jax.random.normal(k3, (3 * D,), dtype=jnp.float32) * 0.01
        Wo = jax.random.normal(k4, (D, H), dtype=jnp.float32) * (1.0 / np.sqrt(D))
        bo = jax.random.normal(k5, (H,), dtype=jnp.float32) * 0.01
        return {'x': x, 'Wqkv': Wqkv, 'bqkv': bqkv, 'Wo': Wo, 'bo': bo}
    _L0_attn_b_in = _L0_attn_b_setup()

    def _L0_ffn_setup():
        import jax, jax.numpy as jnp
        import numpy as np
        NUM_EXPERTS = 4
        HIDDEN = 512
        RANK = 8
        ALPHA = 8.0
        SCALE = ALPHA / RANK
        key = jax.random.key(seed)
        ks = jax.random.split(key, 6)
        B, T, H, E, R = (4, 512, HIDDEN, NUM_EXPERTS, RANK)
        x = jax.random.normal(ks[0], (B, T, H), dtype=jnp.float32)
        W_up = jax.random.normal(ks[1], (H, H), dtype=jnp.float32) / np.sqrt(H)
        gate_w = jax.random.normal(ks[2], (E, H), dtype=jnp.float32) / np.sqrt(H)
        expert_bias = jnp.zeros((E,), dtype=jnp.float32)
        lora_A = jax.random.normal(ks[3], (E, R, H), dtype=jnp.float32) / np.sqrt(H)
        lora_B = jax.random.normal(ks[4], (E, H, R), dtype=jnp.float32) * 0.01
        return {'x': x, 'W_up': W_up, 'gate_w': gate_w, 'expert_bias': expert_bias, 'lora_A': lora_A, 'lora_B': lora_B}
    _L0_ffn_in = _L0_ffn_setup()

    def _L1_attn_a_setup():
        import jax, jax.numpy as jnp
        import numpy as np
        H = 32
        G = 8
        D = 128
        HID = 512
        THETA = 10000.0

        def _rope(x, pos):
            half = D // 2
            inv_freq = 1.0 / THETA ** (jnp.arange(0, half, dtype=jnp.float32) / half)
            ang = pos[:, None].astype(jnp.float32) * inv_freq[None, :]
            cos = jnp.cos(ang)[None, None]
            sin = jnp.sin(ang)[None, None]
            x1, x2 = (x[..., :half], x[..., half:])
            return jnp.concatenate([x1 * cos - x2 * sin, x1 * sin + x2 * cos], axis=-1)
        key = jax.random.key(seed)
        ks = jax.random.split(key, 9)
        s = 0.02
        return {'hidden_states': jax.random.normal(ks[0], (1, 256, HID), jnp.float32), 'Wq': jax.random.normal(ks[1], (HID, H * D), jnp.float32) * s, 'bq': jnp.zeros((H * D,), jnp.float32), 'Wk': jax.random.normal(ks[2], (HID, G * D), jnp.float32) * s, 'bk': jnp.zeros((G * D,), jnp.float32), 'Wv': jax.random.normal(ks[3], (HID, G * D), jnp.float32) * s, 'bv': jnp.zeros((G * D,), jnp.float32), 'Wo': jax.random.normal(ks[4], (H * D, HID), jnp.float32) * s, 'bo': jnp.zeros((HID,), jnp.float32)}
    _L1_attn_a_in = _L1_attn_a_setup()

    def _L1_attn_b_setup():
        import jax, jax.numpy as jnp
        import numpy as np
        HIDDEN = 512
        N_HEADS = 32
        N_KV = 8
        HEAD_DIM = HIDDEN // N_HEADS
        Q_PER_KV = N_HEADS // N_KV
        SEQ = 256
        ROPE_BASE = 1000000.0
        POS_SCALE = 1.0
        SM_SCALE = 1.0 / HEAD_DIM
        BLOCK = 64
        LOCAL_BLOCKS = 16
        VERT_STRIDE = 8

        def _blocksparse_mask(seq_len):
            nb = seq_len // BLOCK
            qb = np.arange(nb)[:, None]
            kb = np.arange(nb)[None, :]
            bmask = (kb <= qb) & ((qb - kb < LOCAL_BLOCKS) | ((kb + 1) % VERT_STRIDE == 0))
            emask = np.kron(bmask, np.ones((BLOCK, BLOCK), dtype=bool))
            i = np.arange(seq_len)
            emask &= i[:, None] >= i[None, :]
            return jnp.asarray(emask)

        def _rope(x, cos, sin):
            x1, x2 = jnp.split(x, 2, axis=-1)
            rot = jnp.concatenate([-x2, x1], axis=-1)
            return x * cos[None, :, None, :] + rot * sin[None, :, None, :]
        key = jax.random.key(seed)
        k1, k2, k3, k4, k5 = jax.random.split(key, 5)
        qkv_out = (N_HEADS + 2 * N_KV) * HEAD_DIM
        return {'hidden_states': jax.random.normal(k1, (1, SEQ, HIDDEN), dtype=jnp.float32), 'w_qkv': jax.random.normal(k2, (qkv_out, HIDDEN), dtype=jnp.float32) * 0.02, 'b_qkv': jnp.zeros((qkv_out,), dtype=jnp.float32), 'w_dense': jax.random.normal(k3, (HIDDEN, HIDDEN), dtype=jnp.float32) * 0.02, 'b_dense': jnp.zeros((HIDDEN,), dtype=jnp.float32)}
    _L1_attn_b_in = _L1_attn_b_setup()

    def _L1_ffn_setup():
        import jax, jax.numpy as jnp
        import numpy as np
        H = 512
        I = 256
        E = 16
        TOPK = 4
        SI = 256
        key = jax.random.key(seed)
        ks = jax.random.split(key, 9)
        s = 0.02
        return {'hidden_states': jax.random.normal(ks[0], (2, 256, H), dtype=jnp.float32), 'gate_w': jax.random.normal(ks[1], (E, H), dtype=jnp.float32) * s, 'bias': jnp.zeros((E,), dtype=jnp.float32), 'Wg': jax.random.normal(ks[2], (E, I, H), dtype=jnp.float32) * s, 'Wu': jax.random.normal(ks[3], (E, I, H), dtype=jnp.float32) * s, 'Wd': jax.random.normal(ks[4], (E, H, I), dtype=jnp.float32) * s, 'Sg': jax.random.normal(ks[5], (SI, H), dtype=jnp.float32) * s, 'Su': jax.random.normal(ks[6], (SI, H), dtype=jnp.float32) * s, 'Sd': jax.random.normal(ks[7], (H, SI), dtype=jnp.float32) * s}
    _L1_ffn_in = _L1_ffn_setup()
    _d = {'L0_attn_a_hidden_states': _L0_attn_a_in['hidden_states'], 'L0_attn_a_w_qkv': _L0_attn_a_in['w_qkv'], 'L0_attn_a_b_qkv': _L0_attn_a_in['b_qkv'], 'L0_attn_a_w_dense': _L0_attn_a_in['w_dense'], 'L0_attn_a_b_dense': _L0_attn_a_in['b_dense'], 'L0_attn_b_Wqkv': _L0_attn_b_in['Wqkv'], 'L0_attn_b_bqkv': _L0_attn_b_in['bqkv'], 'L0_attn_b_Wo': _L0_attn_b_in['Wo'], 'L0_attn_b_bo': _L0_attn_b_in['bo'], 'L0_ffn_W_up': _L0_ffn_in['W_up'], 'L0_ffn_gate_w': _L0_ffn_in['gate_w'], 'L0_ffn_expert_bias': _L0_ffn_in['expert_bias'], 'L0_ffn_lora_A': _L0_ffn_in['lora_A'], 'L0_ffn_lora_B': _L0_ffn_in['lora_B'], 'L1_attn_a_Wq': _L1_attn_a_in['Wq'], 'L1_attn_a_bq': _L1_attn_a_in['bq'], 'L1_attn_a_Wk': _L1_attn_a_in['Wk'], 'L1_attn_a_bk': _L1_attn_a_in['bk'], 'L1_attn_a_Wv': _L1_attn_a_in['Wv'], 'L1_attn_a_bv': _L1_attn_a_in['bv'], 'L1_attn_a_Wo': _L1_attn_a_in['Wo'], 'L1_attn_a_bo': _L1_attn_a_in['bo'], 'L1_attn_b_w_qkv': _L1_attn_b_in['w_qkv'], 'L1_attn_b_b_qkv': _L1_attn_b_in['b_qkv'], 'L1_attn_b_w_dense': _L1_attn_b_in['w_dense'], 'L1_attn_b_b_dense': _L1_attn_b_in['b_dense'], 'L1_ffn_gate_w': _L1_ffn_in['gate_w'], 'L1_ffn_bias': _L1_ffn_in['bias'], 'L1_ffn_Wg': _L1_ffn_in['Wg'], 'L1_ffn_Wu': _L1_ffn_in['Wu'], 'L1_ffn_Wd': _L1_ffn_in['Wd'], 'L1_ffn_Sg': _L1_ffn_in['Sg'], 'L1_ffn_Su': _L1_ffn_in['Su'], 'L1_ffn_Sd': _L1_ffn_in['Sd']}
    _x0 = _d['L0_attn_a_hidden_states']
    _d['L0_attn_a_hidden_states'] = jax.random.normal(jax.random.fold_in(jax.random.key(seed), 1), (1, 1024, 512), dtype=_x0.dtype)
    del _x0
    return _d

def reference(L0_attn_a_hidden_states, L0_attn_a_w_qkv, L0_attn_a_b_qkv, L0_attn_a_w_dense, L0_attn_a_b_dense, L0_attn_b_Wqkv, L0_attn_b_bqkv, L0_attn_b_Wo, L0_attn_b_bo, L0_ffn_W_up, L0_ffn_gate_w, L0_ffn_expert_bias, L0_ffn_lora_A, L0_ffn_lora_B, L1_attn_a_Wq, L1_attn_a_bq, L1_attn_a_Wk, L1_attn_a_bk, L1_attn_a_Wv, L1_attn_a_bv, L1_attn_a_Wo, L1_attn_a_bo, L1_attn_b_w_qkv, L1_attn_b_b_qkv, L1_attn_b_w_dense, L1_attn_b_b_dense, L1_ffn_gate_w, L1_ffn_bias, L1_ffn_Wg, L1_ffn_Wu, L1_ffn_Wd, L1_ffn_Sg, L1_ffn_Su, L1_ffn_Sd):

    def _L0_attn_a_ref(hidden_states, w_qkv, b_qkv, w_dense, b_dense):
        import jax, jax.numpy as jnp
        import numpy as np
        HIDDEN = 512
        N_HEADS = 32
        N_KV = 8
        HEAD_DIM = HIDDEN // N_HEADS
        Q_PER_KV = N_HEADS // N_KV
        SEQ = 256
        ROPE_BASE = 1000000.0
        POS_SCALE = 1.0
        SM_SCALE = 1.0 / HEAD_DIM
        BLOCK = 64
        LOCAL_BLOCKS = 16
        VERT_STRIDE = 8

        def _blocksparse_mask(seq_len):
            nb = seq_len // BLOCK
            qb = np.arange(nb)[:, None]
            kb = np.arange(nb)[None, :]
            bmask = (kb <= qb) & ((qb - kb < LOCAL_BLOCKS) | ((kb + 1) % VERT_STRIDE == 0))
            emask = np.kron(bmask, np.ones((BLOCK, BLOCK), dtype=bool))
            i = np.arange(seq_len)
            emask &= i[:, None] >= i[None, :]
            return jnp.asarray(emask)

        def _rope(x, cos, sin):
            x1, x2 = jnp.split(x, 2, axis=-1)
            rot = jnp.concatenate([-x2, x1], axis=-1)
            return x * cos[None, :, None, :] + rot * sin[None, :, None, :]
        B, S, _ = hidden_states.shape
        qkv = jnp.einsum('bsh,oh->bso', hidden_states, w_qkv) + b_qkv
        qkv = qkv.reshape(B, S, N_KV, Q_PER_KV + 2, HEAD_DIM)
        q = qkv[:, :, :, :Q_PER_KV].reshape(B, S, N_HEADS, HEAD_DIM)
        k = qkv[:, :, :, Q_PER_KV]
        v = qkv[:, :, :, Q_PER_KV + 1]
        inv_freq = 1.0 / ROPE_BASE ** (jnp.arange(0, HEAD_DIM, 2, dtype=jnp.float32) / HEAD_DIM)
        t = jnp.arange(S, dtype=jnp.float32) * POS_SCALE
        freqs = jnp.outer(t, inv_freq)
        emb = jnp.concatenate([freqs, freqs], axis=-1)
        cos, sin = (jnp.cos(emb), jnp.sin(emb))
        q = _rope(q, cos, sin)
        k = _rope(k, cos, sin)
        k = jnp.repeat(k, Q_PER_KV, axis=2)
        v = jnp.repeat(v, Q_PER_KV, axis=2)
        mask = _blocksparse_mask(S)
        scores = jnp.einsum('bqhd,bkhd->bhqk', q, k) * SM_SCALE
        scores = jnp.where(mask[None, None], scores, jnp.finfo(scores.dtype).min)
        probs = jax.nn.softmax(scores, axis=-1)
        ctx = jnp.einsum('bhqk,bkhd->bqhd', probs, v).reshape(B, S, HIDDEN)
        out = jnp.einsum('bsh,oh->bso', ctx, w_dense) + b_dense
        return out

    def _L0_attn_b_ref(x, Wqkv, bqkv, Wo, bo):
        import jax, jax.numpy as jnp
        import numpy as np
        H = 512
        D = H // 4
        B, S, C = x.shape
        d = C // 4
        qkv = jnp.einsum('bsc,cf->bsf', x, Wqkv) + bqkv
        qkv = qkv.reshape(B, S, 3, d)
        q, k, v = (qkv[:, :, 0], qkv[:, :, 1], qkv[:, :, 2])
        scale = 1.0 / jnp.sqrt(jnp.float32(d)).astype(x.dtype)
        attn = jnp.einsum('bqd,bkd->bqk', q, k) * scale
        attn = jax.nn.softmax(attn, axis=-1)
        out = jnp.einsum('bqk,bkd->bqd', attn, v)
        return jnp.einsum('bqd,dc->bqc', out, Wo) + bo

    def _L0_ffn_ref(x, W_up, gate_w, expert_bias, lora_A, lora_B):
        import jax, jax.numpy as jnp
        import numpy as np
        NUM_EXPERTS = 4
        HIDDEN = 512
        RANK = 8
        ALPHA = 8.0
        SCALE = ALPHA / RANK
        B, T, H = x.shape
        E = gate_w.shape[0]
        x_flat = x.reshape(-1, H)
        logits = x_flat @ gate_w.T + expert_bias
        top1 = jnp.argmax(logits, axis=-1)
        one_hot = jax.nn.one_hot(top1, E, dtype=x_flat.dtype)
        base_out = jnp.einsum('bth,oh->bto', x, W_up)
        z = jnp.einsum('nh,erh->ner', x_flat, lora_A)
        d = jnp.einsum('ner,ehr->neh', z, lora_B) * SCALE
        delta = jnp.einsum('neh,ne->nh', d, one_hot)
        return base_out + delta.reshape(B, T, H)

    def _L1_attn_a_ref(hidden_states, Wq, bq, Wk, bk, Wv, bv, Wo, bo):
        import jax, jax.numpy as jnp
        import numpy as np
        H = 32
        G = 8
        D = 128
        HID = 512
        THETA = 10000.0

        def _rope(x, pos):
            half = D // 2
            inv_freq = 1.0 / THETA ** (jnp.arange(0, half, dtype=jnp.float32) / half)
            ang = pos[:, None].astype(jnp.float32) * inv_freq[None, :]
            cos = jnp.cos(ang)[None, None]
            sin = jnp.sin(ang)[None, None]
            x1, x2 = (x[..., :half], x[..., half:])
            return jnp.concatenate([x1 * cos - x2 * sin, x1 * sin + x2 * cos], axis=-1)
        B, S, _ = hidden_states.shape
        R = H // G
        q = hidden_states @ Wq + bq
        k = hidden_states @ Wk + bk
        v = hidden_states @ Wv + bv
        q = q.reshape(B, S, H, D).transpose(0, 2, 1, 3)
        k = k.reshape(B, S, G, D).transpose(0, 2, 1, 3)
        v = v.reshape(B, S, G, D).transpose(0, 2, 1, 3)
        pos = jnp.arange(S)
        q = _rope(q, pos)
        k = _rope(k, pos)
        qg = q.reshape(B, G, R, S, D)
        scores = jnp.einsum('bgrsd,bgtd->bgrst', qg, k) / jnp.sqrt(jnp.float32(D))
        causal = jnp.tril(jnp.ones((S, S), dtype=bool))
        scores = jnp.where(causal[None, None, None], scores, jnp.finfo(scores.dtype).min)
        probs = jax.nn.softmax(scores, axis=-1)
        ctx = jnp.einsum('bgrst,bgtd->bgrsd', probs, v)
        ctx = ctx.reshape(B, H, S, D).transpose(0, 2, 1, 3).reshape(B, S, H * D)
        return ctx @ Wo + bo

    def _L1_attn_b_ref(hidden_states, w_qkv, b_qkv, w_dense, b_dense):
        import jax, jax.numpy as jnp
        import numpy as np
        HIDDEN = 512
        N_HEADS = 32
        N_KV = 8
        HEAD_DIM = HIDDEN // N_HEADS
        Q_PER_KV = N_HEADS // N_KV
        SEQ = 256
        ROPE_BASE = 1000000.0
        POS_SCALE = 1.0
        SM_SCALE = 1.0 / HEAD_DIM
        BLOCK = 64
        LOCAL_BLOCKS = 16
        VERT_STRIDE = 8

        def _blocksparse_mask(seq_len):
            nb = seq_len // BLOCK
            qb = np.arange(nb)[:, None]
            kb = np.arange(nb)[None, :]
            bmask = (kb <= qb) & ((qb - kb < LOCAL_BLOCKS) | ((kb + 1) % VERT_STRIDE == 0))
            emask = np.kron(bmask, np.ones((BLOCK, BLOCK), dtype=bool))
            i = np.arange(seq_len)
            emask &= i[:, None] >= i[None, :]
            return jnp.asarray(emask)

        def _rope(x, cos, sin):
            x1, x2 = jnp.split(x, 2, axis=-1)
            rot = jnp.concatenate([-x2, x1], axis=-1)
            return x * cos[None, :, None, :] + rot * sin[None, :, None, :]
        B, S, _ = hidden_states.shape
        qkv = jnp.einsum('bsh,oh->bso', hidden_states, w_qkv) + b_qkv
        qkv = qkv.reshape(B, S, N_KV, Q_PER_KV + 2, HEAD_DIM)
        q = qkv[:, :, :, :Q_PER_KV].reshape(B, S, N_HEADS, HEAD_DIM)
        k = qkv[:, :, :, Q_PER_KV]
        v = qkv[:, :, :, Q_PER_KV + 1]
        inv_freq = 1.0 / ROPE_BASE ** (jnp.arange(0, HEAD_DIM, 2, dtype=jnp.float32) / HEAD_DIM)
        t = jnp.arange(S, dtype=jnp.float32) * POS_SCALE
        freqs = jnp.outer(t, inv_freq)
        emb = jnp.concatenate([freqs, freqs], axis=-1)
        cos, sin = (jnp.cos(emb), jnp.sin(emb))
        q = _rope(q, cos, sin)
        k = _rope(k, cos, sin)
        k = jnp.repeat(k, Q_PER_KV, axis=2)
        v = jnp.repeat(v, Q_PER_KV, axis=2)
        mask = _blocksparse_mask(S)
        scores = jnp.einsum('bqhd,bkhd->bhqk', q, k) * SM_SCALE
        scores = jnp.where(mask[None, None], scores, jnp.finfo(scores.dtype).min)
        probs = jax.nn.softmax(scores, axis=-1)
        ctx = jnp.einsum('bhqk,bkhd->bqhd', probs, v).reshape(B, S, HIDDEN)
        out = jnp.einsum('bsh,oh->bso', ctx, w_dense) + b_dense
        return out

    def _L1_ffn_ref(hidden_states, gate_w, bias, Wg, Wu, Wd, Sg, Su, Sd):
        import jax, jax.numpy as jnp
        import numpy as np
        H = 512
        I = 256
        E = 16
        TOPK = 4
        SI = 256
        orig_shape = hidden_states.shape
        x = hidden_states.reshape(-1, orig_shape[-1])
        scores = jax.nn.sigmoid(x @ gate_w.T) + bias
        topk_w, topk_idx = jax.lax.top_k(scores, TOPK)
        topk_w = topk_w / (jnp.sum(topk_w, axis=-1, keepdims=True) + 1e-20)
        cw = jnp.sum(jax.nn.one_hot(topk_idx, E, dtype=x.dtype) * topk_w[..., None], axis=1)
        g = jnp.einsum('th,eih->eti', x, Wg)
        u = jnp.einsum('th,eih->eti', x, Wu)
        z = jax.nn.silu(g) * u
        zw = z * cw.T[:, :, None]
        out = jnp.einsum('eti,ehi->th', zw, Wd)
        out = out + jax.nn.silu(x @ Sg.T) * (x @ Su.T) @ Sd.T
        return out.reshape(orig_shape)
    x = L0_attn_a_hidden_states
    x = x + _L0_attn_a_ref(_layernorm(x, axis=-1), L0_attn_a_w_qkv, L0_attn_a_b_qkv, L0_attn_a_w_dense, L0_attn_a_b_dense)
    x = x + _L0_ffn_ref(_layernorm(x, axis=-1), L0_ffn_W_up, L0_ffn_gate_w, L0_ffn_expert_bias, L0_ffn_lora_A, L0_ffn_lora_B)
    x = x + _L0_attn_b_ref(_layernorm(x, axis=-1), L0_attn_b_Wqkv, L0_attn_b_bqkv, L0_attn_b_Wo, L0_attn_b_bo)
    x = x + _L0_ffn_ref(_layernorm(x, axis=-1), L0_ffn_W_up, L0_ffn_gate_w, L0_ffn_expert_bias, L0_ffn_lora_A, L0_ffn_lora_B)
    x = x + _L1_attn_a_ref(_layernorm(x, axis=-1), L1_attn_a_Wq, L1_attn_a_bq, L1_attn_a_Wk, L1_attn_a_bk, L1_attn_a_Wv, L1_attn_a_bv, L1_attn_a_Wo, L1_attn_a_bo)
    x = x + _L1_ffn_ref(_layernorm(x, axis=-1), L1_ffn_gate_w, L1_ffn_bias, L1_ffn_Wg, L1_ffn_Wu, L1_ffn_Wd, L1_ffn_Sg, L1_ffn_Su, L1_ffn_Sd)
    x = x + _L1_attn_b_ref(_layernorm(x, axis=-1), L1_attn_b_w_qkv, L1_attn_b_b_qkv, L1_attn_b_w_dense, L1_attn_b_b_dense)
    x = x + _L1_ffn_ref(_layernorm(x, axis=-1), L1_ffn_gate_w, L1_ffn_bias, L1_ffn_Wg, L1_ffn_Wu, L1_ffn_Wd, L1_ffn_Sg, L1_ffn_Su, L1_ffn_Sd)
    return x

_drawn_inputs = setup_inputs


def setup_inputs(seed=0):
    import zlib

    import numpy as np

    out = dict(_drawn_inputs(seed))
    spreads = {'L0_attn_a_b_qkv': (0.0, 0.1),
     'L0_attn_a_b_dense': (0.0, 0.1),
     'L0_ffn_expert_bias': (0.0, 0.8),
     'L1_attn_a_bq': (0.0, 0.8),
     'L1_attn_a_bk': (0.0, 0.8),
     'L1_attn_a_bv': (0.0, 0.1),
     'L1_attn_a_bo': (0.0, 0.1),
     'L1_attn_b_b_qkv': (0.0, 0.469),
     'L1_attn_b_b_dense': (0.0, 0.1),
     'L1_ffn_bias': (0.0, 0.732)}
    factors = {'L0_attn_a_w_qkv': 3.741,
     'L0_attn_b_bqkv': 8.0,
     'L0_attn_b_bo': 8.0,
     'L0_ffn_gate_w': 3.063,
     'L1_attn_a_Wq': 8.0,
     'L1_attn_a_Wk': 8.0,
     'L1_attn_b_w_qkv': 4.937,
     'L1_attn_b_w_dense': 2.823,
     'L1_ffn_gate_w': 4.935,
     'L1_ffn_Wg': 3.918,
     'L1_ffn_Wu': 3.84,
     'L1_ffn_Wd': 3.837}
    for name, (base, spread) in spreads.items():
        noise = np.random.default_rng([zlib.crc32(name.encode()), seed]).standard_normal(out[name].shape)
        drawn = base * np.exp(spread * noise) if base else spread * noise
        out[name] = jnp.asarray(drawn.astype(out[name].dtype))
    for name, factor in factors.items():
        out[name] = (out[name] * factor).astype(out[name].dtype)
    return out
```

```python
from contextlib import ExitStack, contextmanager

import concourse.bass as bass
from concourse import mybir

ALU = mybir.AluOpType
ACT = mybir.ActivationFunctionType
F32 = mybir.dt.float32
F32R = mybir.dt.float32r
BF16 = mybir.dt.bfloat16
U32 = mybir.dt.uint32
AX_X = mybir.AxisListType.X

P = 128
T = 1024
NT = T // P
H = 512
KC = H // P
HALF = T // 2
BLK = HALF // P
EPS = 1e-5
BIG = 1e30
LOWEST = -3e38

NH, NKV, HD = 32, 8, 16
GH = NH // NKV
QKV = (NH + 2 * NKV) * HD
NQK = NH + NKV
SLOTS = P // HD

D = 128
SCALE = float(D) ** -0.5

NE0, RANK = 4, 8
ZR = NE0 * RANK

NE, INNER, TOPK = 16, 256, 4
IC = INNER // P


def banks_of(qt):
    return qt // BLK + 1


BANKS_BEFORE = [sum(banks_of(q) for q in range(qt)) for qt in range(NT + 1)]


@contextmanager
def stage(nc, name):
    sems = []
    with ExitStack() as scope:
        def sb(n, shape, dt=F32, at=scope):
            return at.enter_context(nc.sbuf_tensor(f"{name}_{n}", shape, dt))

        def sem(n):
            sems.append(nc.alloc_semaphore(f"{name}_{n}"))
            return sems[-1]

        yield sb, sem
    nc.clear_and_free_semaphores(sems)
    nc.all_engine_barrier()


class Shared:

    def __init__(self, nc, ctx):
        def sb(name, shape, dt=F32):
            return ctx.enter_context(nc.sbuf_tensor(name, shape, dt))

        self.x = sb("x", [P, NT, H])
        self.ident, self.ident_b = sb("ident", [P, P]), sb("ident_b", [P, P], BF16)
        self.ones = sb("ones", [P, H])
        self.mask_b = sb("mask_b", [P, P], BF16)
        self.pair = [ctx.enter_context(nc.psum_tensor(f"pair{i}", [P, 2 * HALF], F32)) for i in range(2)]
        self.single = [ctx.enter_context(nc.psum_tensor(f"single{i}", [P, HALF], F32)) for i in range(4)]

    def bank(self, i):
        return self.pair[i // 2][:, (i % 2) * HALF:(i % 2 + 1) * HALF] if i < 4 else self.single[i - 4][:, :]


class Normalisation:

    def __init__(self, sb, sem):
        self.xn = sb("xn", [P, 2, H])
        self.stats, self.mv = sb("stats", [P, NT, 6]), sb("mv", [P, NT, 2])
        self.veps, self.std, self.rstd = sb("veps", [P, NT]), sb("std", [P, NT]), sb("rstd", [P, NT])
        self.step, self.std_ready = sem("ln_step"), sem("std_ready")
        self.row_ready, self.turned = sem("row_ready"), sem("row_turned")


def ln_stats(dve, g, n):
    for t in range(NT):
        dve.bn_stats(n.stats[:, t, :], g.x[:, t, :]).then_inc(n.step, 1)
    for t in range(NT):
        dve.wait_ge(n.step, NT)
        dve.bn_aggr(n.mv[:, t, :], n.stats[:, t, :]).then_inc(n.step, 1)
    dve.wait_ge(n.step, 2 * NT)
    dve.tensor_scalar_add(n.veps[:, :], n.mv[:, :, 1], EPS).then_inc(n.step, 1)
    dve.wait_ge(n.std_ready, 1)
    dve.reciprocal(n.rstd[:, :], n.std[:, :]).then_inc(n.step, 1)
    dve.wait_ge(n.step, 2 * NT + 2)


def ln_root(act, n):
    act.wait_ge(n.step, 2 * NT + 1)
    act.activation(n.std[:, :], n.veps[:, :], ACT.Sqrt).then_inc(n.std_ready, 1)


def ln_row(dve, g, n, t):
    if t >= 2:
        dve.wait_ge(n.turned, t - 1)
    dve.tensor_scalar(n.xn[:, t % 2, :], g.x[:, t, :], n.mv[:, t, 0:1], n.rstd[:, t:t + 1],
                      ALU.subtract, ALU.mult).then_inc(n.row_ready, 1)


def ln_turn(pe, g, n, t):
    pe.wait_ge(n.row_ready, t + 1)
    for k in range(KC):
        mm = pe.transpose(g.bank(4 + t % 2)[:, k * P:(k + 1) * P], n.xn[:, t % 2, k * P:(k + 1) * P], g.ident[:, :])
    mm.then_inc(n.turned, 1)


def turned_row(g, t):
    return g.bank(4 + t % 2).rearrange("p (k t) -> p k t", k=KC)


def output_bias(pool, g, n, bd, loaded, count, biased):
    pool.wait_ge(loaded, count)
    for t in range(NT):
        pool.wait_ge(n.row_ready, t + 1)
        pool.tensor_tensor(g.x[:, t, :], g.x[:, t, :], bd[:, :], ALU.add).then_inc(biased, 1)


def constants(nc, g, d):
    with stage(nc, "const") as (sb, sem):
        done = sem("done")
        loaded = sem("loaded")
        with nc.Block() as block:
            @block.sync
            def _(sp):
                sp.dma_start(g.x[:, :, :], d["x"]).then_inc(loaded, 16)
                sp.wait_ge(loaded, 16)

            @block.gpsimd
            def _(pool):
                pool.memset(g.ident[:, :], 0.0).then_inc(done, 1)
                pool.memset(g.mask_b[:, :], 0.0).then_inc(done, 1)
                pool.memset(g.ones[:, :], 1.0).then_inc(done, 1)
                pool.wait_ge(done, 3)
                pool.affine_select(out=g.ident[:, :], in_=g.ident[:, :], compare_op=ALU.not_equal, fill=1.0,
                                   base=0, pattern=[[-1, P]], channel_multiplier=1).then_inc(done, 1)
                pool.affine_select(out=g.mask_b[:, :], in_=g.mask_b[:, :], compare_op=ALU.is_ge, fill=BIG,
                                   base=0, pattern=[[-1, P]], channel_multiplier=1).then_inc(done, 1)
                pool.wait_ge(done, 5)
                pool.tensor_copy(g.ident_b[:, :], g.ident[:, :]).then_inc(done, 1)
                pool.wait_ge(done, 6)


def store(nc, g, out):
    with stage(nc, "store") as (sb, sem):
        stored = sem("stored")
        with nc.Block() as block:
            @block.sync
            def _(sp):
                sp.dma_start(out, g.x[:, :, :]).then_inc(stored, 16)
                sp.wait_ge(stored, 16)


BANKS = GH * BANKS_BEFORE[NT]


def turned_before(u):
    if u < 0:
        return -banks_of(NT - 1)
    qt, j = divmod(u, GH)
    return GH * BANKS_BEFORE[qt] + j * banks_of(qt)


class Heads16:

    def __init__(self, sb, sem):
        self.xT = sb("xT", [P, KC, T])
        self.w = sb("w", [P, KC, QKV])
        self.bias = sb("bias", [P, QKV])
        self.cos = sb("cos", [P, NT, 2, HD])
        self.sin = sb("sin", [P, NT, 2, HD])
        self.wd = sb("wd", [P, KC, H])
        self.bd = sb("bd", [P, H])
        self.v = sb("v", [P, NT, NKV, HD])
        self.vg = sb("vg", [P, NT, 32])
        self.qkT = sb("qkT", [P, NQK, T], BF16)
        with ExitStack() as proj:
            def c(n, shape, dt=F32):
                return sb(n, shape, dt, proj)
            self.qk = c("qk", [P, NQK, HD])
            self.rc = c("rc", [P, NQK, HD])
            self.rs = c("rs", [P, NQK, HD])
            self.rest1 = c("rest1", [P, NQK, HD])
            self.rest2 = c("rest2", [P, NQK, HD])
            self.stack = c("stack", [P, NQK, SLOTS, HD], BF16)
        self.probs = sb("probs", [P, 2, T])
        self.probsT = sb("probsT", [P, 2, GH, NT, P])
        self.least = sb("least", [P, 4])
        self.ctxT = sb("ctxT", [P, P])
        self.rsum = sb("rsum", [P, GH])
        self.oT = sb("oT", [P, KC, P])
        self.ctx = self.xT[:, :, :].rearrange("p k t -> p (k t)").rearrange("p (n h) -> p n h", n=NT)
        self.w_loaded, self.xT_ready, self.qkv_ready = sem("w_loaded"), sem("xT_ready"), sem("qkv_ready")
        self.qkv_read, self.rope_step, self.split1 = sem("qkv_read"), sem("rope_step"), sem("split1")
        self.rest1_ready, self.rest2_ready, self.stack_ready = sem("rest1_ready"), sem("rest2_ready"), sem("stack_ready")
        self.stackT_ready, self.stackT_copied, self.vg_ready = sem("stackT_ready"), sem("stackT_copied"), sem("vg_ready")
        self.scores_ready, self.least_ready, self.probs_ready = sem("scores_ready"), sem("least_ready"), sem("probs_ready")
        self.probsT_ready, self.evac_dve, self.evac_act = sem("probsT_ready"), sem("evac_dve"), sem("evac_act")
        self.pv_ready, self.ctxT_ready, self.ctx_turned = sem("pv_ready"), sem("ctxT_ready"), sem("ctx_turned")
        self.rsum_ready, self.ctx_ready, self.ctxT2_ready = sem("rsum_ready"), sem("ctx_ready"), sem("ctxT2_ready")
        self.oT_ready, self.out_ready, self.biased = sem("oT_ready"), sem("out_ready"), sem("biased")
        self.added = sem("added")


def attention16(nc, g, d, name):
    with stage(nc, name) as (sb, sem):
        ln = Normalisation(sb, sem)
        a = Heads16(sb, sem)

        with nc.Block() as block:
            @block.sync
            def _(sp):
                sp.dma_start(a.w[:, :, :], d[name + "_wqkv"]).then_inc(a.w_loaded, 16)
                sp.dma_start(a.bias[:, :], d[name + "_bqkv"].partition_broadcast(P)).then_inc(a.w_loaded, 16)
                sp.dma_start(a.cos[:, :, :, :], d["cos16"]).then_inc(a.w_loaded, 16)
                sp.dma_start(a.sin[:, :, :, :], d["sin16"]).then_inc(a.w_loaded, 16)
                sp.dma_start(a.wd[:, :, :], d[name + "_wd"]).then_inc(a.w_loaded, 16)
                sp.dma_start(a.bd[:, :], d[name + "_bd"].partition_broadcast(P)).then_inc(a.w_loaded, 16)

            @block.gpsimd
            def _(pool):
                pool.memset(a.vg[:, :, :], 0.0).then_inc(a.vg_ready, 1)
                pool.wait_ge(a.vg_ready, 1)
                pool.memset(a.vg[:, :, HD:HD + 1], 1.0).then_inc(a.vg_ready, 1)
                for t in range(NT):
                    pool.wait_ge(a.split1, t + 1)
                    if t >= 1:
                        pool.wait_ge(a.stack_ready, 2 * t)
                    pool.tensor_tensor(a.rest1[:, :, :], a.rc[:, :, :], a.stack[:, :, 0, :],
                                       ALU.subtract).then_inc(a.rest1_ready, 1)
                output_bias(pool, g, ln, a.bd, a.w_loaded, 96, a.biased)


            @block.scalar
            def _(act):
                def row_copy(t):
                    act.wait_ge(ln.turned, t + 1)
                    act.activation(a.xT[:, :, t * P:(t + 1) * P], turned_row(g, t), ACT.Copy).then_inc(a.xT_ready, 1)

                def evac_odd(kv, qt, j):
                    first = GH * BANKS_BEFORE[qt] + j * banks_of(qt)
                    for n in range(banks_of(qt)):
                        b = first + n
                        if b % 2:
                            k = min(4, qt + 1 - 4 * n)
                            act.wait_ge(a.probsT_ready, kv * BANKS + b + 4)
                            act.wait_ge(a.pv_ready, kv * NT + qt + 1)
                            act.activation(a.probsT[:, qt % 2, j, 4 * n:4 * n + k, :],
                                           g.bank(5)[:, 0:k * P].rearrange("p (k q) -> p k q", k=k),
                                           ACT.Copy).then_inc(a.evac_act, 1)

                def ctx_evac(kv, qt):
                    act.wait_ge(a.pv_ready, kv * NT + qt + 3)
                    act.wait_ge(a.ctx_turned, kv * NT + qt + 1)
                    act.activation(a.ctxT[:, :], g.bank(6)[:, 0:P], ACT.Copy).then_inc(a.ctxT_ready, 1)

                ln_root(act, ln)
                row_copy(0)
                for t in range(NT):
                    if t + 1 < NT:
                        row_copy(t + 1)
                    act.wait_ge(a.rope_step, 4 * t + 4)
                    if t >= 1:
                        act.wait_ge(a.stackT_ready, 5 * t)
                    act.activation(a.stack[:, 0:NH, 0:3, :],
                                   a.rc[:, 0:NH, :].unsqueeze(2).to_broadcast([P, NH, 3, HD]), ACT.Copy)
                    act.activation(a.stack[:, NH:NQK, 0:7:3, :],
                                   a.rc[:, NH:NQK, :].unsqueeze(2).to_broadcast([P, NKV, 3, HD]), ACT.Copy)\
                        .then_inc(a.split1, 1)
                    for n in range(5):
                        act.wait_ge(a.stackT_ready, 5 * t + n + 1)
                        act.activation(a.qkT[:, 8 * n:8 * n + 8, t * P:(t + 1) * P],
                                       g.bank(6 + n % 2).bitcast(BF16).rearrange("p (h t) -> p h t", h=8),
                                       ACT.Copy).then_inc(a.stackT_copied, 1)
                act.sem_inc(a.ctxT_ready, 1)
                act.sem_inc(a.probs_ready, 2)
                act.sem_inc(a.evac_act, 1)
                with act.Fori(0, NKV) as kv:
                    unit = 0
                    prev = None
                    for qt in range(NT):
                        for j in range(GH):
                            n = (qt + 1) * P
                            act.wait_ge(a.least_ready, kv * (NT * GH) + unit + 1)
                            act.wait_ge(a.probsT_ready, kv * BANKS + turned_before(unit - 1) + 3)
                            act.activation(a.probs[:, unit % 2, 0:n], g.pair[unit % 2][:, 0:n], ACT.Exp,
                                           bias=a.least[:, unit % 4:unit % 4 + 1], scale=-1.0)\
                                .then_inc(a.probs_ready, 1)
                            if prev is not None:
                                evac_odd(kv, *prev)
                            prev = (qt, j)
                            unit += 1
                            if qt >= 1 and j == 1:
                                ctx_evac(kv, qt - 1)
                    evac_odd(kv, *prev)
                    ctx_evac(kv, NT - 1)
                for t in range(NT):
                    act.wait_ge(a.ctxT2_ready, t + 1)
                    if t >= 1:
                        act.wait_ge(a.out_ready, t)
                    act.activation(a.oT[:, :, :], g.bank(4 + t % 2).rearrange("p (k t) -> p k t", k=KC),
                                   ACT.Copy).then_inc(a.oT_ready, 1)


            @block.tensor
            def _(pe):
                def qkv(t):
                    pe.wait_ge(a.xT_ready, t + 1)
                    if t >= 2:
                        pe.wait_ge(a.qkv_read, 2 * (t - 1))
                    for lo, hi, b in ((0, H, 0), (H, QKV, 1)):
                        for k in range(KC):
                            mm = pe.matmul(g.bank(2 * (t % 2) + b)[:, 0:hi - lo], a.xT[:, k, t * P:(t + 1) * P],
                                           a.w[:, k, lo:hi], start=(k == 0), stop=(k == KC - 1))
                    mm.then_inc(a.qkv_ready, 1)

                def turn_stack(t):
                    pe.wait_ge(a.stack_ready, 2 * t + 2)
                    for n in range(5):
                        if 5 * t + n >= 2:
                            pe.wait_ge(a.stackT_copied, 5 * t + n - 1)
                        for i in range(8):
                            mm = pe.transpose(g.bank(6 + n % 2).bitcast(BF16)[:, i * P:(i + 1) * P],
                                              a.stack[:, 8 * n + i, :, :].rearrange("p s d -> p (s d)"),
                                              g.ident_b[:, :])
                        mm.then_inc(a.stackT_ready, 1)

                ln_turn(pe, g, ln, 0)
                pe.wait_ge(a.w_loaded, 96)
                for t in range(NT):
                    if t + 1 < NT:
                        ln_turn(pe, g, ln, t + 1)
                    qkv(t)
                    if t >= 1:
                        turn_stack(t - 1)
                turn_stack(NT - 1)
                pe.wait_ge(a.stackT_copied, 5 * NT)
                pe.wait_ge(a.qkv_read, 2 * NT)

                pe.sem_inc(a.probsT_ready, 3)
                pe.sem_inc(a.pv_ready, 2)
                pe.sem_inc(a.ctx_turned, 1)
                with pe.Fori(0, NKV) as kv:
                    units = NT * GH

                    def scores(u):
                        qt, j = divmod(u, GH)
                        n = (qt + 1) * P
                        pe.wait_ge(a.probs_ready, kv * units + u + 1)
                        for c in range(0, n, HALF):
                            w = min(HALF, n - c)
                            last = c + w == n
                            mm = pe.matmul(g.pair[u % 2][:, c:c + w],
                                           a.qkT[:, bass.ds(kv * GH + j, 1), qt * P:(qt + 1) * P].squeeze(1),
                                           a.qkT[:, bass.ds(kv + NH, 1), c:c + w].squeeze(1),
                                           start=True, stop=not last)
                        mm = pe.matmul(g.pair[u % 2][:, n - P:n], g.ident_b[:, :], g.mask_b[:, :], start=False, stop=True)
                        mm.then_inc(a.scores_ready, 1)

                    def turn_probs(u):
                        qt, j = divmod(u, GH)
                        pe.wait_ge(a.probs_ready, kv * units + u + 3)
                        for n in range(banks_of(qt)):
                            b = GH * BANKS_BEFORE[qt] + j * banks_of(qt) + n
                            if b % 2:
                                pe.wait_ge(a.evac_act, kv * (BANKS // 2) + b // 2 + 1)
                            else:
                                pe.wait_ge(a.evac_dve, kv * (BANKS // 2) + b // 2 + 1)
                            for i in range(min(4, qt + 1 - 4 * n)):
                                kt = 4 * n + i
                                mm = pe.transpose(g.bank(4 + b % 2)[:, i * P:(i + 1) * P],
                                                  a.probs[:, u % 2, kt * P:(kt + 1) * P], g.ident[:, :])
                            mm.then_inc(a.probsT_ready, 1)

                    def weigh(qt):
                        done = GH * BANKS_BEFORE[qt + 1]
                        pe.wait_ge(a.evac_act, kv * (BANKS // 2) + done // 2 + 1)
                        pe.wait_ge(a.evac_dve, kv * (BANKS // 2) + done // 2 + 1)
                        pe.wait_ge(a.ctxT_ready, kv * NT + qt + 1)
                        if qt == 0:
                            pe.wait_ge(a.vg_ready, kv + 3)
                        for kt in range(qt + 1):
                            for j in range(GH):
                                mm = pe.matmul(g.bank(6)[32 * j:32 * j + 32, 0:P], a.vg[:, kt, :],
                                               a.probsT[:, qt % 2, j, kt, :], start=(kt == 0), stop=(kt == qt))
                        mm.then_inc(a.pv_ready, 1)

                    def turn_ctx(qt):
                        pe.wait_ge(a.ctxT_ready, kv * NT + qt + 2)
                        pe.wait_ge(a.ctx_ready, kv * NT + qt + 1)
                        pe.transpose(g.bank(7)[:, 0:P], a.ctxT[:, :], g.ident[:, :]).then_inc(a.ctx_turned, 1)

                    scores(0)
                    scores(1)
                    for u in range(units):
                        if u + 2 < units:
                            scores(u + 2)
                        turn_probs(u)
                        if u % GH == 0 and u:
                            weigh(u // GH - 1)
                        if u % GH == 2 and u > GH:
                            turn_ctx(u // GH - 1)
                    weigh(NT - 1)
                    turn_ctx(NT - 1)

                def turn_o(t):
                    pe.wait_ge(a.ctx_ready, NKV * NT + 1)
                    if t >= 2:
                        pe.wait_ge(a.oT_ready, t - 1)
                    for k in range(KC):
                        mm = pe.transpose(g.bank(4 + t % 2)[:, k * P:(k + 1) * P], a.ctx[:, t, k * P:(k + 1) * P],
                                          g.ident[:, :])
                    mm.then_inc(a.ctxT2_ready, 1)

                turn_o(0)
                for t in range(NT):
                    if t + 1 < NT:
                        turn_o(t + 1)
                    pe.wait_ge(a.oT_ready, t + 1)
                    if t >= 2:
                        pe.wait_ge(a.added, t - 1)
                    for k in range(KC):
                        mm = pe.matmul(g.bank(t % 2), a.oT[:, k, :], a.wd[:, k, :], start=(k == 0), stop=(k == KC - 1))
                    mm.then_inc(a.out_ready, 1)


            @block.vector
            def _(dve):
                ln_stats(dve, g, ln)
                ln_row(dve, g, ln, 0)
                ln_row(dve, g, ln, 1)
                dve.wait_ge(a.w_loaded, 96)
                for t in range(NT):
                    if t + 2 < NT:
                        ln_row(dve, g, ln, t + 2)
                    b = 2 * (t % 2)
                    dve.wait_ge(a.qkv_ready, t + 1)
                    if t >= 1:
                        dve.wait_ge(a.rope_step, 4 * t)
                    dve.tensor_tensor(a.qk[:, 0:NH, :].rearrange("p h d -> p (h d)"), g.bank(b), a.bias[:, 0:H],
                                      ALU.add).then_inc(a.qkv_read, 1)
                    dve.tensor_tensor(a.qk[:, NH:NQK, :].rearrange("p h d -> p (h d)"), g.bank(b + 1)[:, 0:P],
                                      a.bias[:, H:H + P], ALU.add).then_inc(a.rope_step, 1)
                    dve.tensor_tensor(a.v[:, t, :, :].rearrange("p h d -> p (h d)"), g.bank(b + 1)[:, P:2 * P],
                                      a.bias[:, H + P:QKV], ALU.add).then_inc(a.qkv_read, 1)
                    dve.wait_ge(a.qkv_read, 2 * t + 2)
                    dve.wait_ge(a.rope_step, 4 * t + 1)
                    if t >= 1:
                        dve.wait_ge(a.split1, t)
                        dve.wait_ge(a.rest1_ready, t)
                    for n, (lo, hi) in enumerate(((0, NH), (NH, NQK))):
                        m = hi - lo
                        dve.tensor_tensor(a.rc[:, lo:hi, :], a.qk[:, lo:hi, :],
                                          a.cos[:, t, n:n + 1, :].to_broadcast([P, m, HD]), ALU.mult)
                        for c in range(2):
                            o = c * HD // 2
                            q = HD // 2 - o
                            mm = dve.tensor_tensor(a.rs[:, lo:hi, o:o + HD // 2], a.qk[:, lo:hi, q:q + HD // 2],
                                                   a.sin[:, t, n:n + 1, o:o + HD // 2].to_broadcast([P, m, HD // 2]),
                                                   ALU.mult)
                    mm.then_inc(a.rope_step, 2)
                    dve.wait_ge(a.rope_step, 4 * t + 3)
                    dve.tensor_tensor(a.rc[:, :, :], a.rc[:, :, :], a.rs[:, :, :], ALU.add).then_inc(a.rope_step, 1)
                    dve.wait_ge(a.rest1_ready, t + 1)
                    dve.tensor_copy(a.stack[:, 0:NH, 3:6, :],
                                    a.rest1[:, 0:NH, :].unsqueeze(2).to_broadcast([P, NH, 3, HD])).then_inc(a.rest2_ready, 1)
                    dve.tensor_copy(a.stack[:, NH:NQK, 1:8:3, :],
                                    a.rest1[:, NH:NQK, :].unsqueeze(2).to_broadcast([P, NKV, 3, HD])).then_inc(a.rest2_ready, 1)
                    dve.wait_ge(a.rest2_ready, 5 * t + 2)
                    dve.tensor_tensor(a.rest2[:, 0:NH, :], a.rest1[:, 0:NH, :], a.stack[:, 0:NH, 3, :],
                                      ALU.subtract).then_inc(a.rest2_ready, 1)
                    dve.tensor_tensor(a.rest2[:, NH:NQK, :], a.rest1[:, NH:NQK, :], a.stack[:, NH:NQK, 1, :],
                                      ALU.subtract).then_inc(a.rest2_ready, 2)
                    dve.wait_ge(a.rest2_ready, 5 * t + 5)
                    dve.tensor_copy(a.stack[:, 0:NH, 6:8, :],
                                    a.rest2[:, 0:NH, :].unsqueeze(2).to_broadcast([P, NH, 2, HD])).then_inc(a.stack_ready, 1)
                    dve.tensor_copy(a.stack[:, NH:NQK, 2:6:3, :],
                                    a.rest2[:, NH:NQK, :].unsqueeze(2).to_broadcast([P, NKV, 2, HD])).then_inc(a.stack_ready, 1)

                dve.sem_inc(a.ctx_ready, 1)
                dve.sem_inc(a.evac_dve, 1)
                dve.wait_ge(a.vg_ready, 2)
                with dve.Fori(0, NKV) as kv:
                    dve.wait_ge(a.pv_ready, kv * NT + 2)
                    dve.tensor_scalar(a.vg[:, :, 0:HD].unsqueeze(2), a.v[:, :, bass.ds(kv, 1), :], 1.0, None,
                                      ALU.mult).then_inc(a.vg_ready, 1)

                    def least(u):
                        n = (u // GH + 1) * P
                        dve.wait_ge(a.scores_ready, kv * (NT * GH) + u + 1)
                        dve.tensor_reduce(a.least[:, u % 4:u % 4 + 1], g.pair[u % 2][:, 0:n], AX_X, ALU.min)\
                            .then_inc(a.least_ready, 1)

                    def evac_even(u):
                        qt, j = divmod(u, GH)
                        for n in range(banks_of(qt)):
                            b = GH * BANKS_BEFORE[qt] + j * banks_of(qt) + n
                            if b % 2 == 0:
                                k = min(4, qt + 1 - 4 * n)
                                dve.wait_ge(a.probsT_ready, kv * BANKS + b + 4)
                                dve.wait_ge(a.pv_ready, kv * NT + qt + 1)
                                dve.tensor_copy(a.probsT[:, qt % 2, j, 4 * n:4 * n + k, :],
                                                g.bank(4)[:, 0:k * P].rearrange("p (k q) -> p k q", k=k))\
                                    .then_inc(a.evac_dve, 1)

                    def normalise(qt):
                        dve.wait_ge(a.ctx_turned, kv * NT + qt + 2)
                        v = g.bank(7)[:, 0:P].rearrange("p (j d) -> p j d", j=GH)
                        dve.reciprocal(a.rsum[:, :], v[:, :, HD]).then_inc(a.rsum_ready, 1)
                        dve.wait_ge(a.rsum_ready, kv * NT + qt + 1)
                        o = a.ctx[:, qt, :].rearrange("p (g d) -> p g d", g=NKV)[:, bass.ds(kv, 1), :].squeeze(1)
                        dve.tensor_tensor(o.rearrange("p (j d) -> p j d", j=GH), v[:, :, 0:HD],
                                          a.rsum[:, :].unsqueeze(2).to_broadcast([P, GH, HD]), ALU.mult)\
                            .then_inc(a.ctx_ready, 1)

                    least(0)
                    least(1)
                    for u in range(NT * GH):
                        if u + 2 < NT * GH:
                            least(u + 2)
                        evac_even(u)
                        if u % GH == 3 and u > GH:
                            normalise(u // GH - 1)
                    normalise(NT - 1)
                for t in range(NT):
                    dve.wait_ge(a.out_ready, t + 1)
                    dve.wait_ge(a.biased, t + 1)
                    dve.tensor_tensor(g.x[:, t, :], g.bank(t % 2), g.x[:, t, :], ALU.add).then_inc(a.added, 1)



def lora_ffn(nc, g, d, name):
    with stage(nc, name) as (sb, sem):
        ln = Normalisation(sb, sem)
        xT = sb("xT", [P, KC, T])
        w = sb("w", [P, KC, H])
        ga = sb("ga", [P, KC, NE0 + ZR])
        bm = sb("bm", [P, H])
        ebias = sb("ebias", [P, NE0])
        number = sb("number", [P, ZR])
        logits = sb("logits", [P, NT, 8])
        top = sb("top", [P, NT, 8])
        at = sb("at", [P, NT, 8], U32)
        pick = sb("pick", [P, NT])
        z = sb("z", [P, 2, P])
        zT = sb("zT", [P, 2, P])
        loaded, b_loaded = sem("w_loaded"), sem("b_loaded")
        filled, b_filled, xT_ready = sem("filled"), sem("b_filled"), sem("xT_ready")
        gz_ready, pick_step, z_ready = sem("gz_ready"), sem("pick_step"), sem("z_ready")
        z_turned, zT_ready, out_ready, added = sem("z_turned"), sem("zT_ready"), sem("out_ready"), sem("added")

        with nc.Block() as block:
            @block.sync
            def _(sp):
                sp.dma_start(ga[:, :, :], d["L0f_ga"]).then_inc(loaded, 16)
                sp.dma_start(w[:, :, :], d["L0f_w"]).then_inc(loaded, 16)
                sp.dma_start(ebias[:, :], d["L0f_bias"].partition_broadcast(P)).then_inc(loaded, 16)
                sp.wait_ge(b_filled, 1)
                sp.dma_start(bm[0:ZR, :], d["L0f_b"]).then_inc(b_loaded, 16)

            @block.gpsimd
            def _(pool):
                pool.memset(bm[:, :], 0.0).then_inc(b_filled, 1)
                for e in range(NE0):
                    pool.memset(number[:, e * RANK:(e + 1) * RANK], float(e)).then_inc(filled, 1)
                pool.memset(z[:, :, :], 0.0).then_inc(filled, 1)
                pool.memset(logits[:, :, :], LOWEST).then_inc(filled, 1)

            @block.scalar
            def _(act):
                ln_root(act, ln)
                for t in range(NT + 2):
                    if t < NT:
                        act.wait_ge(ln.turned, t + 1)
                        act.activation(xT[:, :, t * P:(t + 1) * P], turned_row(g, t), ACT.Copy).then_inc(xT_ready, 1)
                    if t >= 2:
                        act.wait_ge(z_turned, t - 1)
                        if t >= 4:
                            act.wait_ge(out_ready, t - 3)
                        act.activation(zT[:, t % 2, :], g.bank(3)[:, 0:P], ACT.Copy).then_inc(zT_ready, 1)

            @block.tensor
            def _(pe):
                ln_turn(pe, g, ln, 0)
                pe.wait_ge(loaded, 48)
                for t in range(NT + 2):
                    if t + 1 < NT:
                        ln_turn(pe, g, ln, t + 1)
                    if t < NT:
                        pe.wait_ge(xT_ready, t + 1)
                        if t >= 2:
                            pe.wait_ge(z_ready, t - 1)
                        for k in range(KC):
                            mm = pe.matmul(g.bank(6 + t % 2)[:, 0:NE0 + ZR], xT[:, k, t * P:(t + 1) * P], ga[:, k, :],
                                           start=(k == 0), stop=(k == KC - 1))
                        mm.then_inc(gz_ready, 1)
                        if t >= 3:
                            pe.wait_ge(added, t - 2)
                        for k in range(KC):
                            pe.matmul(g.bank(t % 3), xT[:, k, t * P:(t + 1) * P], w[:, k, :],
                                      start=(k == 0), stop=False)
                    if t >= 2:
                        pe.wait_ge(zT_ready, t - 1)
                        pe.wait_ge(b_loaded, 16)
                        pe.matmul(g.bank((t - 2) % 3), zT[:, t % 2, :], bm[:, :], start=False, stop=True)\
                            .then_inc(out_ready, 1)
                    if 1 <= t <= NT:
                        pe.wait_ge(z_ready, t)
                        if t >= 2:
                            pe.wait_ge(zT_ready, t - 1)
                        pe.transpose(g.bank(3)[:, 0:P], z[:, (t - 1) % 2, :], g.ident[:, :]).then_inc(z_turned, 1)

            @block.vector
            def _(dve):
                ln_stats(dve, g, ln)
                ln_row(dve, g, ln, 0)
                ln_row(dve, g, ln, 1)
                dve.wait_ge(filled, NE0 + 2)
                dve.wait_ge(loaded, 48)
                for t in range(NT + 2):
                    if t + 2 < NT:
                        ln_row(dve, g, ln, t + 2)
                    if t < NT:
                        gz = g.bank(6 + t % 2)
                        dve.wait_ge(gz_ready, t + 1)
                        dve.tensor_tensor(logits[:, t, 0:NE0], gz[:, 0:NE0], ebias[:, :], ALU.add).then_inc(pick_step, 1)
                        dve.wait_ge(pick_step, 4 * t + 1)
                        dve.max(top[:, t, :], logits[:, t, :]).then_inc(pick_step, 1)
                        dve.wait_ge(pick_step, 4 * t + 2)
                        dve.max_index(at[:, t, :], top[:, t, :], logits[:, t, :]).then_inc(pick_step, 1)
                        dve.wait_ge(pick_step, 4 * t + 3)
                        dve.tensor_copy(pick[:, t:t + 1], at[:, t, 0:1]).then_inc(pick_step, 1)
                        dve.wait_ge(pick_step, 4 * t + 4)
                        if t >= 2:
                            dve.wait_ge(z_turned, t - 1)
                        dve.scalar_tensor_tensor(out=z[:, t % 2, 0:ZR], in0=number[:, :], scalar=pick[:, t:t + 1],
                                                 in1=gz[:, NE0:NE0 + ZR], op0=ALU.is_equal, op1=ALU.mult)\
                            .then_inc(z_ready, 1)
                    if t >= 2:
                        dve.wait_ge(out_ready, t - 1)
                        dve.tensor_tensor(g.x[:, t - 2, :], g.bank((t - 2) % 3), g.x[:, t - 2, :], ALU.add)\
                            .then_inc(added, 1)


def single_head(nc, g, d, name):
    with stage(nc, name) as (sb, sem):
        ln = Normalisation(sb, sem)
        xT = sb("xT", [P, KC, T])
        w = sb("w", [P, KC, 3 * D])
        wo = sb("wo", [P, H])
        bq = sb("bq", [P, 2])
        bqs = sb("bqs", [P, 1])
        bv = sb("bv", [P, D])
        bo = sb("bo", [P, H])
        qT, kT = sb("qT", [P, T]), sb("kT", [P, T])
        v = sb("v", [P, NT, D])
        probs, probsT = sb("probs", [P, 2, T]), sb("probsT", [P, 2, NT, P])
        least, rsum, rinv = sb("least", [P, NT]), sb("rsum", [P, NT]), sb("rinv", [P, NT])
        ctxT = sb("ctxT", [P, 2, P])
        loaded, xT_ready, bias_ready, biased = sem("loaded"), sem("xT_ready"), sem("bias_ready"), sem("biased")
        qk_ready, qk_copied = sem("qk_ready"), sem("qk_copied")
        v_ready, v_copied = sem("v_ready"), sem("v_copied")
        scores_ready, least_ready, probs_ready = sem("scores_ready"), sem("least_ready"), sem("probs_ready")
        turned, evac_dve, evac_act = sem("probs_turned"), sem("evac_dve"), sem("evac_act")
        pv_ready, ctxT_ready = sem("pv_ready"), sem("ctxT_ready")
        out_ready, rinv_ready, added = sem("out_ready"), sem("rinv_ready"), sem("added")

        with nc.Block() as block:
            @block.sync
            def _(sp):
                sp.dma_start(w[:, :, :], d["L0b_w"]).then_inc(loaded, 16)
                sp.dma_start(bq[:, :], d["L0b_bqk"]).then_inc(loaded, 16)
                sp.dma_start(bv[:, :], d["L0b_bv"].partition_broadcast(P)).then_inc(loaded, 16)
                sp.dma_start(wo[:, :], d["L0b_wo"]).then_inc(loaded, 16)
                sp.dma_start(bo[:, :], d["L0b_bo"].partition_broadcast(P)).then_inc(loaded, 16)

            @block.gpsimd
            def _(pool):
                output_bias(pool, g, ln, bo, loaded, 80, biased)

            @block.scalar
            def _(act):
                ln_root(act, ln)
                for t in range(NT):
                    act.wait_ge(ln.turned, t + 1)
                    act.activation(xT[:, :, t * P:(t + 1) * P], turned_row(g, t), ACT.Copy).then_inc(xT_ready, 1)
                act.wait_ge(bias_ready, 1)
                for h in range(2):
                    s = slice(h * HALF, (h + 1) * HALF)
                    act.wait_ge(qk_ready, 2 * h + 1)
                    act.activation(qT[:, s], g.bank(2 * h), ACT.Identity, bias=bqs[:, 0:1], scale=-SCALE)\
                        .then_inc(qk_copied, 1)
                    act.wait_ge(qk_ready, 2 * h + 2)
                    act.activation(kT[:, s], g.bank(2 * h + 1), ACT.Identity, bias=bq[:, 1:2]).then_inc(qk_copied, 1)

                def ctx_copy(qt):
                    act.wait_ge(pv_ready, qt + 1)
                    if qt >= 2:
                        act.wait_ge(out_ready, qt - 1)
                    act.activation(ctxT[:, qt % 2, :], g.bank(6)[:, 0:P], ACT.Copy).then_inc(ctxT_ready, 1)

                def exps(qt):
                    act.wait_ge(least_ready, qt + 1)
                    if qt >= 2:
                        act.wait_ge(turned, 2 * (qt - 1))
                    act.activation(probs[:, qt % 2, :], g.pair[qt % 2][:, :], ACT.Exp, bias=least[:, qt:qt + 1],
                                   scale=-1.0, accum_out=rsum[:, qt:qt + 1]).then_inc(probs_ready, 1)

                exps(0)
                for qt in range(NT):
                    if qt + 1 < NT:
                        exps(qt + 1)
                    act.wait_ge(turned, 2 * qt + 2)
                    if qt >= 2:
                        act.wait_ge(pv_ready, qt - 1)
                    act.activation(probsT[:, qt % 2, BLK:NT, :], g.bank(5).rearrange("p (k q) -> p k q", k=BLK),
                                   ACT.Copy).then_inc(evac_act, 1)
                    if qt >= 1:
                        ctx_copy(qt - 1)
                ctx_copy(NT - 1)

            @block.tensor
            def _(pe):
                pe.wait_ge(loaded, 80)
                for t in range(NT):
                    if t >= 2:
                        pe.wait_ge(xT_ready, t - 1)
                    ln_turn(pe, g, ln, t)
                for h in range(2):
                    pe.wait_ge(xT_ready, (h + 1) * BLK)
                    for c in range(2):
                        for k in range(KC):
                            mm = pe.matmul(g.bank(2 * h + c), w[:, k, c * D:(c + 1) * D],
                                           xT[:, k, h * HALF:(h + 1) * HALF], start=(k == 0), stop=(k == KC - 1))
                        mm.then_inc(qk_ready, 1)
                for t in range(NT):
                    if t >= 2:
                        pe.wait_ge(v_copied, t - 1)
                    for k in range(KC):
                        mm = pe.matmul(g.bank(6 + t % 2)[:, 0:D], xT[:, k, t * P:(t + 1) * P], w[:, k, 2 * D:3 * D],
                                       start=(k == 0), stop=(k == KC - 1))
                    mm.then_inc(v_ready, 1)

                def scores(qt):
                    pe.wait_ge(qk_copied, 4)
                    if qt >= 2:
                        pe.wait_ge(probs_ready, qt - 1)
                    for h in range(2):
                        mm = pe.matmul(g.pair[qt % 2][:, h * HALF:(h + 1) * HALF], qT[:, qt * P:(qt + 1) * P],
                                       kT[:, h * HALF:(h + 1) * HALF], start=True, stop=True)
                    mm.then_inc(scores_ready, 1)

                def weigh(qt):
                    pe.wait_ge(v_copied, NT)
                    pe.wait_ge(evac_dve, qt + 1)
                    pe.wait_ge(evac_act, qt + 1)
                    if qt >= 1:
                        pe.wait_ge(ctxT_ready, qt)
                    for kt in range(NT):
                        mm = pe.matmul(g.bank(6)[:, 0:P], v[:, kt, :], probsT[:, qt % 2, kt, :],
                                       start=(kt == 0), stop=(kt == NT - 1))
                    mm.then_inc(pv_ready, 1)

                def project(qt):
                    pe.wait_ge(ctxT_ready, qt + 1)
                    if qt >= 1:
                        pe.wait_ge(added, qt)
                    pe.matmul(g.bank(7), ctxT[:, qt % 2, :], wo[:, :], start=True, stop=True).then_inc(out_ready, 1)

                scores(0)
                scores(1)
                for qt in range(NT):
                    if qt + 2 < NT:
                        scores(qt + 2)
                    pe.wait_ge(probs_ready, qt + 1)
                    for b in range(2):
                        if qt >= 1:
                            pe.wait_ge((evac_dve, evac_act)[b], qt)
                        for i in range(BLK):
                            kt = BLK * b + i
                            mm = pe.transpose(g.bank(4 + b)[:, i * P:(i + 1) * P], probs[:, qt % 2, kt * P:(kt + 1) * P],
                                              g.ident[:, :])
                        mm.then_inc(turned, 1)
                    if qt >= 1:
                        weigh(qt - 1)
                    if qt >= 2:
                        project(qt - 2)
                weigh(NT - 1)
                project(NT - 2)
                project(NT - 1)

            @block.vector
            def _(dve):
                ln_stats(dve, g, ln)
                dve.wait_ge(loaded, 80)
                dve.tensor_scalar(bqs[:, :], bq[:, 0:1], -SCALE, None, ALU.mult).then_inc(bias_ready, 1)
                for t in range(NT):
                    ln_row(dve, g, ln, t)
                for t in range(NT):
                    dve.wait_ge(v_ready, t + 1)
                    dve.tensor_tensor(v[:, t, :], g.bank(6 + t % 2)[:, 0:D], bv[:, :], ALU.add).then_inc(v_copied, 1)

                def low(qt):
                    dve.wait_ge(scores_ready, qt + 1)
                    dve.tensor_reduce(least[:, qt:qt + 1], g.pair[qt % 2][:, :], AX_X, ALU.min).then_inc(least_ready, 1)

                def add(qt):
                    dve.wait_ge(probs_ready, qt + 1)
                    dve.reciprocal(rinv[:, qt:qt + 1], rsum[:, qt:qt + 1]).then_inc(rinv_ready, 1)
                    dve.wait_ge(rinv_ready, qt + 1)
                    dve.wait_ge(out_ready, qt + 1)
                    dve.wait_ge(biased, qt + 1)
                    dve.scalar_tensor_tensor(out=g.x[:, qt, :], in0=g.bank(7), scalar=rinv[:, qt:qt + 1],
                                             in1=g.x[:, qt, :], op0=ALU.mult, op1=ALU.add).then_inc(added, 1)

                low(0)
                low(1)
                for qt in range(NT):
                    if qt + 2 < NT:
                        low(qt + 2)
                    dve.wait_ge(turned, 2 * qt + 1)
                    if qt >= 2:
                        dve.wait_ge(pv_ready, qt - 1)
                    dve.tensor_copy(probsT[:, qt % 2, 0:BLK, :], g.bank(4).rearrange("p (k q) -> p k q", k=BLK))\
                        .then_inc(evac_dve, 1)
                    if qt >= 2:
                        add(qt - 2)
                add(NT - 2)
                add(NT - 1)


def turned_rows_high(act, g, ln, xh, ready):
    for t in range(NT):
        act.wait_ge(ln.turned, t + 1)
        act.activation(xh[:, :, t * P:(t + 1) * P], turned_row(g, t), ACT.Copy).then_inc(ready, 1)


def turned_rows_low(dve, g, t, xh, xl, ready, split):
    dve.wait_ge(ready, t + 1)
    s = slice(t * P, (t + 1) * P)
    dve.tensor_tensor(xl[:, :, s], turned_row(g, t), xh[:, :, s].bitcast(F32), ALU.subtract).then_inc(split, 1)


def product(pe, out, wh, wl, xh, xl, start, stop):
    pe.matmul(out, wh, xh, start=start, stop=False)
    pe.matmul(out, wh, xl, start=False, stop=False)
    return pe.matmul(out, wl, xh, start=False, stop=stop)


K_, V_, Q_, O_ = 0, 1, 2, 2 + GH
PIECES = 2 + 2 * GH
SPLIT_ORDER = [K_, Q_, V_, Q_ + 1, O_, Q_ + 2, O_ + 1, Q_ + 3, O_ + 2, O_ + 3]
SLOTS_RAW = PIECES // 2
UNITS = GH * NT
BANKS_G = GH * BANKS_BEFORE[NT]


def group_plan():
    plan = [("proj", K_, 0), ("proj", Q_, 0), ("proj", K_, 1), ("proj", Q_, 1), ("begin",), ("proj", V_, 0)]
    for j in range(GH):
        if j == 0:
            between = [[("turn_v", 0)], [("proj", V_, 1)], [("turn_v", 1)], [("proj", Q_ + 1, 0)],
                       [("weigh", 0, 0), ("proj", Q_ + 1, 1)]]
        else:
            more = [("proj", Q_ + j + 1, h) for h in range(2)] if j + 1 < GH else [None, None]
            between = [[], [("weigh", j - 1, 1), more[0]], [("out", j - 1, 4), ("out", j - 1, 5)], [("out", j - 1, 6), ("out", j - 1, 7)], [("weigh", j, 0), more[1]]]
        between += [[], [("out", j, 0), ("out", j, 1)], [("out", j, 2), ("out", j, 3)]]
        for qt in range(NT):
            plan += [("unit", j, qt)] + [s for s in between[qt] if s]
    plan.append(("weigh", GH - 1, 1))
    return plan + [("out", GH - 1, t) for t in range(BLK, NT)]


PLAN = group_plan()


def numbered(*kinds):
    return {s: n for n, s in enumerate(s for s in PLAN if s[0] in kinds)}


AUX = numbered("proj", "turn_v", "out")
IN_BANK = numbered("proj", "turn_v", "out", "weigh")
ORDER = list(IN_BANK)
NAUX = len(AUX)
OF_KIND = {k: numbered(k) for k in ("proj", "turn_v", "out", "weigh")}
ROPE = {s: n for n, s in enumerate(s for s in PLAN if s[0] == "proj" and s[1] != V_)}
NROPE = len(ROPE)
NPROJ = len(OF_KIND["proj"])


def aux_bank(s):
    return 6 + IN_BANK[s] % 2


def rotated_before(j, qt):
    need = [("proj", K_, h) for h in range(qt // BLK + 1)] + [("proj", Q_ + j, h) for h in range(qt // BLK + 1)]
    return max(ROPE[s] for s in need) + 1


def turned_of_group(u):
    if u < 0:
        return -banks_of(NT - 1)
    j, qt = divmod(u, NT)
    return j * BANKS_BEFORE[NT] + BANKS_BEFORE[qt]


def attention128(nc, g, d, name):
    with stage(nc, name) as (sb, sem):
        ln = Normalisation(sb, sem)
        xh, xl = sb("xh", [P, KC, T], F32R), sb("xl", [P, KC, T], F32R)
        raw = sb("raw", [P, SLOTS_RAW, H])
        wh, wl = sb("wh", [P, PIECES, H], F32R), sb("wl", [P, PIECES, H], F32R)
        cos, sin = sb("cos", [P, T]), sb("sin", [P, T])
        bias = sb("bias", [P, 2 + GH, NKV])
        own_bias = sb("own_bias", [P, 2 + GH])
        bo = sb("bo", [P, H])
        lin, swapped = sb("lin", [P, 2, HALF]), sb("swapped", [P, 2, HALF])
        by_cos, by_sin, rot = sb("by_cos", [P, HALF]), sb("by_sin", [P, HALF]), sb("rot", [P, HALF])
        kh, kl = sb("kh", [P, T], F32R), sb("kl", [P, T], F32R)
        qh, ql = sb("qh", [P, 2, T], F32R), sb("ql", [P, 2, T], F32R)
        vT = sb("vT", [P, HALF])
        vh, vl = sb("vh", [P, NT, D], F32R), sb("vl", [P, NT, D], F32R)
        probs = sb("probs", [P, 2, T])
        ph, pl = sb("ph", [P, NT, HALF], F32R), sb("pl", [P, NT, HALF], F32R)
        ch, cl = sb("ch", [P, HALF], F32R), sb("cl", [P, HALF], F32R)
        least = sb("least", [P, 4])
        rsum, rinv = sb("rsum", [P, 2, NT]), sb("rinv", [P, 2, NT])

        loaded, biased, scaled = sem("loaded"), sem("biased"), sem("scaled")
        own_bias_ready = sem("own_bias_ready")
        x_high, x_split = sem("x_high"), sem("x_split")
        raw_loaded = [sem(f"raw_loaded{i}") for i in range(SLOTS_RAW)]
        w_high, w_split = sem("w_high"), sem("w_split")
        aux_ready = sem("aux_ready")
        proj_read, v_split, added = sem("proj_read"), sem("v_split"), sem("added")
        by_cos_ready, by_sin_ready, summed = sem("by_cos_ready"), sem("by_sin_ready"), sem("summed")
        rot_high, rotated, v_high = sem("rot_high"), sem("rotated"), sem("v_high")
        scores_ready, least_ready, probs_ready = sem("scores_ready"), sem("least_ready"), sem("probs_ready")
        turned, p_high, p_split = sem("probs_turned"), sem("p_high"), sem("p_split")
        pv_ready, c_high, c_split, rinv_ready = sem("pv_ready"), sem("c_high"), sem("c_split"), sem("rinv_ready")

        with nc.Block() as block:
            @block.sync
            def _(sp):
                sp.dma_start(bias[:, :, :], d["L1a_bias"]).then_inc(loaded, 16)
                sp.dma_start(cos[:, :], d["cos128"]).then_inc(loaded, 16)
                sp.dma_start(sin[:, :], d["sin128"]).then_inc(loaded, 16)
                sp.dma_start(bo[:, :], d["L1a_bo"].partition_broadcast(P)).then_inc(loaded, 16)
                with sp.Fori(0, NKV) as kv:
                    for pos in range(PIECES):
                        sp.wait_ge(w_split, kv * PIECES + pos + 1)
                        sp.dma_start(raw[:, pos % SLOTS_RAW, :], d["L1a_w"][bass.ds(kv * PIECES + pos, 1), :, :].squeeze(0))\
                            .then_inc(raw_loaded[pos % SLOTS_RAW], 16)

            @block.gpsimd
            def _(pool):
                output_bias(pool, g, ln, bo, loaded, 64, biased)
                pool.sem_inc(w_split, SLOTS_RAW)
                pool.sem_inc(rotated, 2)
                with pool.Fori(0, NKV) as kv:
                    def split(pos):
                        piece = SPLIT_ORDER[pos]
                        if piece >= O_:
                            last = AUX["out", piece - O_, NT - 1]
                        else:
                            last = AUX["proj", piece, 1]
                        pool.wait_ge(raw_loaded[pos % SLOTS_RAW], kv * 32 + 16 * (pos // SLOTS_RAW) + 16)
                        pool.wait_ge(aux_ready, kv * NAUX + last + 1)
                        r = raw[:, pos % SLOTS_RAW, :]
                        pool.tensor_tensor(wh[:, piece, :], r, g.ones[:, :], ALU.mult).then_inc(w_high, 1)
                        pool.wait_ge(w_high, kv * PIECES + pos + 1)
                        pool.tensor_tensor(wl[:, piece, :], raw[:, pos % SLOTS_RAW, :], wh[:, piece, :].bitcast(F32),
                                           ALU.subtract).then_inc(w_split, 1)

                    def rotate(s):
                        _, piece, h = s
                        r, cols = ROPE[s], slice(h * HALF, (h + 1) * HALF)
                        pool.wait_ge(proj_read, (kv + 1) * NPROJ + OF_KIND["proj"][s] + 1)
                        pool.wait_ge(summed, kv * NROPE + r + 1)
                        pool.tensor_tensor(by_sin[:, :], swapped[:, r % 2, :], sin[:, cols], ALU.mult)\
                            .then_inc(by_sin_ready, 1)
                        to = kl[:, cols] if piece == K_ else ql[:, (piece - Q_) % 2, cols]
                        high = kh[:, cols] if piece == K_ else qh[:, (piece - Q_) % 2, cols]
                        pool.wait_ge(rot_high, kv * NROPE + r + 1)
                        pool.tensor_tensor(to, rot[:, :], high.bitcast(F32), ALU.subtract).then_inc(rotated, 1)

                    for pos in range(SLOTS_RAW):
                        split(pos)
                    for s, r in ROPE.items():
                        rotate(s)
                        if 3 <= r < 3 + SLOTS_RAW:
                            split(SLOTS_RAW + r - 3)

            @block.scalar
            def _(act):
                ln_root(act, ln)
                turned_rows_high(act, g, ln, xh, x_high)
                act.sem_inc(probs_ready, 2)
                act.sem_inc(proj_read, NPROJ)
                with act.Fori(0, NKV) as kv:
                    def exps(u):
                        j, qt = divmod(u, NT)
                        n = (qt + 1) * P
                        act.wait_ge(least_ready, kv * UNITS + u + 1)
                        act.wait_ge(turned, kv * BANKS_G + turned_of_group(u - 1) + 3)
                        act.activation(probs[:, u % 2, 0:n], g.pair[u % 2][:, 0:n], ACT.Exp,
                                       bias=least[:, u % 4:u % 4 + 1], scale=-1.0,
                                       accum_out=rsum[:, j % 2, qt:qt + 1]).then_inc(probs_ready, 1)

                    act.wait_ge(own_bias_ready, kv + 1)
                    for s in PLAN:
                        if s[0] == "proj":
                            piece, n = s[1], AUX[s]
                            act.wait_ge(aux_ready, (kv + 1) * NAUX + n + 1)
                            if piece == V_:
                                act.wait_ge(aux_ready, kv * NAUX + (AUX["turn_v", 1] + 1 if s[2] == 0 else
                                                                    NAUX + AUX["turn_v", 0] + 1))
                                act.activation(vT[:, :], g.bank(aux_bank(s)), ACT.Identity, bias=own_bias[:, 1:2])\
                                    .then_inc(proj_read, 1)
                                continue
                            r = ROPE[s]
                            act.wait_ge(rotated, kv * NROPE + r + 1)
                            b = own_bias[:, piece:piece + 1]
                            f = 1.0 if piece == K_ else -SCALE
                            act.activation(lin[:, r % 2, :], g.bank(aux_bank(s)), ACT.Identity, bias=b, scale=f)
                            for o in (0, P // 2):
                                q = P // 2 - o
                                mm = act.activation(swapped[o:o + P // 2, r % 2, :], g.bank(aux_bank(s))[q:q + P // 2, :],
                                                    ACT.Identity, bias=b[q:q + P // 2, :], scale=f)
                            mm.then_inc(proj_read, 1)
                        elif s[0] == "turn_v":
                            act.wait_ge(aux_ready, (kv + 1) * NAUX + AUX[s] + 1)
                            act.activation(vh[:, s[1] * BLK:(s[1] + 1) * BLK, :],
                                           g.bank(aux_bank(s)).rearrange("p (k e) -> p k e", k=BLK),
                                           ACT.Copy).then_inc(v_high, 1)
                        elif s[0] == "begin":
                            exps(0)
                        elif s[0] == "unit":
                            _, j, qt = s
                            u = j * NT + qt
                            if u + 1 < UNITS:
                                exps(u + 1)
                            for h in range(banks_of(qt)):
                                b = turned_of_group(u) + h
                                k = min(BLK, qt + 1 - BLK * h)
                                act.wait_ge(turned, kv * BANKS_G + b + 4)
                                act.wait_ge(pv_ready, kv * 2 * GH + 2 * j + qt // BLK + 1)
                                act.activation(ph[:, BLK * h:BLK * h + k, (qt % BLK) * P:(qt % BLK + 1) * P],
                                               g.bank(4 + b % 2)[:, 0:k * P].rearrange("p (k q) -> p k q", k=k),
                                               ACT.Copy).then_inc(p_high, 1)
                        elif s[0] == "weigh":
                            _, j, c = s
                            q = 2 * j + c
                            act.wait_ge(pv_ready, kv * 2 * GH + q + 2)
                            last = ("out", j, BLK - 1) if c else ("out", (j - 1) % GH, NT - 1)
                            act.wait_ge(aux_ready, kv * NAUX + AUX[last] + 1 + (NAUX if q else 0))
                            act.activation(ch[:, :], g.bank(aux_bank(s)), ACT.Copy).then_inc(c_high, 1)

            @block.tensor
            def _(pe):
                for t in range(NT):
                    if t >= 2:
                        pe.wait_ge(x_split, t - 1)
                    ln_turn(pe, g, ln, t)
                pe.wait_ge(x_split, NT)
                pe.sem_inc(turned, 3)
                pe.sem_inc(pv_ready, 1)
                pe.sem_inc(aux_ready, NAUX)
                with pe.Fori(0, NKV) as kv:
                    def scores(u):
                        j, qt = divmod(u, NT)
                        n = (qt + 1) * P
                        pe.wait_ge(rotated, kv * NROPE + rotated_before(j, qt) + 2)
                        pe.wait_ge(probs_ready, kv * UNITS + u + 1)
                        rows = slice(qt * P, (qt + 1) * P)
                        for c in range(0, n, HALF):
                            w = min(HALF, n - c)
                            product(pe, g.pair[u % 2][:, c:c + w], qh[:, j % 2, rows], ql[:, j % 2, rows],
                                    kh[:, c:c + w], kl[:, c:c + w], True, c + w < n)
                        pe.matmul(g.pair[u % 2][:, n - P:n], g.ident_b[:, :], g.mask_b[:, :], start=False, stop=True)\
                            .then_inc(scores_ready, 1)

                    for s in PLAN:
                        if s in IN_BANK:
                            n = IN_BANK[s] - 2
                            before = ORDER[n]
                            pe.wait_ge({"proj": proj_read, "turn_v": v_split, "out": added, "weigh": c_split}[before[0]],
                                       (kv + (n >= 0)) * len(OF_KIND[before[0]]) + OF_KIND[before[0]][before] + 1)
                        if s[0] == "proj":
                            _, piece, h = s
                            pe.wait_ge(w_split, kv * PIECES + SPLIT_ORDER.index(piece) + 1 + SLOTS_RAW)
                            for k in range(KC):
                                c, r = slice(k * P, (k + 1) * P), slice(h * HALF, (h + 1) * HALF)
                                mm = product(pe, g.bank(aux_bank(s)), wh[:, piece, c], wl[:, piece, c], xh[:, k, r], xl[:, k, r],
                                             k == 0, k == KC - 1)
                            mm.then_inc(aux_ready, 1)
                        elif s[0] == "turn_v":
                            pe.wait_ge(proj_read, (kv + 1) * NPROJ + OF_KIND["proj"]["proj", V_, s[1]] + 1)
                            for i in range(BLK):
                                mm = pe.transpose(g.bank(aux_bank(s))[:, i * P:(i + 1) * P], vT[:, i * P:(i + 1) * P], g.ident[:, :])
                            mm.then_inc(aux_ready, 1)
                        elif s[0] == "begin":
                            scores(0)
                            scores(1)
                        elif s[0] == "unit":
                            _, j, qt = s
                            u = j * NT + qt
                            if u + 2 < UNITS:
                                scores(u + 2)
                            pe.wait_ge(probs_ready, kv * UNITS + u + 3)
                            for h in range(banks_of(qt)):
                                b = turned_of_group(u) + h
                                pe.wait_ge(p_split, kv * BANKS_G + b + 1)
                                for i in range(min(BLK, qt + 1 - BLK * h)):
                                    kt = BLK * h + i
                                    mm = pe.transpose(g.bank(4 + b % 2)[:, i * P:(i + 1) * P],
                                                      probs[:, u % 2, kt * P:(kt + 1) * P], g.ident[:, :])
                                mm.then_inc(turned, 1)
                        elif s[0] == "weigh":
                            _, j, c = s
                            q = 2 * j + c
                            pe.wait_ge(p_split, kv * BANKS_G + j * BANKS_BEFORE[NT] + BANKS_BEFORE[BLK * (c + 1)] + 2)
                            pe.wait_ge(v_split, (kv + 1) * 2 + 2)
                            for kt in range(BLK * (c + 1)):
                                o = max(0, kt - BLK * c) * P
                                mm = product(pe, g.bank(aux_bank(s))[:, o:HALF], vh[:, kt, :], vl[:, kt, :],
                                             ph[:, kt, o:HALF], pl[:, kt, o:HALF], kt == 0, kt == BLK * (c + 1) - 1)
                            mm.then_inc(pv_ready, 1)
                        else:
                            _, j, t = s
                            pe.wait_ge(c_split, (kv + 1) * 2 * GH + 2 * j + t // BLK + 1)
                            pe.wait_ge(w_split, kv * PIECES + SPLIT_ORDER.index(O_ + j) + 1 + SLOTS_RAW)
                            c = slice((t % BLK) * P, (t % BLK + 1) * P)
                            product(pe, g.bank(aux_bank(s)), ch[:, c], cl[:, c], wh[:, O_ + j, :], wl[:, O_ + j, :], True, True)\
                                .then_inc(aux_ready, 1)

            @block.vector
            def _(dve):
                ln_stats(dve, g, ln)
                ln_row(dve, g, ln, 0)
                ln_row(dve, g, ln, 1)
                for t in range(NT):
                    if t + 2 < NT:
                        ln_row(dve, g, ln, t + 2)
                    turned_rows_low(dve, g, t, xh, xl, x_high, x_split)
                dve.wait_ge(loaded, 64)
                dve.tensor_scalar(bias[:, 2:2 + GH, :], bias[:, 2:2 + GH, :], -SCALE, None, ALU.mult).then_inc(scaled, 1)
                dve.wait_ge(biased, NT)
                dve.sem_inc(added, GH * NT)
                dve.sem_inc(v_split, 2)
                dve.sem_inc(summed, 1)
                dve.sem_inc(p_split, 2)
                dve.sem_inc(c_split, 2 * GH)
                dve.wait_ge(scaled, 1)
                with dve.Fori(0, NKV) as kv:
                    dve.wait_ge(proj_read, (kv + 1) * NPROJ)
                    dve.tensor_scalar(own_bias[:, :].unsqueeze(2), bias[:, :, bass.ds(kv, 1)], 1.0, None, ALU.mult)\
                        .then_inc(own_bias_ready, 1)

                    def low(u):
                        n = (u % NT + 1) * P
                        dve.wait_ge(scores_ready, kv * UNITS + u + 1)
                        dve.tensor_reduce(least[:, u % 4:u % 4 + 1], g.pair[u % 2][:, 0:n], AX_X, ALU.min)\
                            .then_inc(least_ready, 1)

                    def rotate(s):
                        _, piece, h = s
                        r, cols = ROPE[s], slice(h * HALF, (h + 1) * HALF)
                        dve.wait_ge(proj_read, (kv + 1) * NPROJ + OF_KIND["proj"][s] + 1)
                        dve.tensor_tensor(by_cos[:, :], lin[:, r % 2, :], cos[:, cols], ALU.mult).then_inc(by_cos_ready, 1)
                        dve.wait_ge(by_cos_ready, kv * NROPE + r + 1)
                        dve.wait_ge(by_sin_ready, kv * NROPE + r + 1)
                        dve.wait_ge(rotated, kv * NROPE + r + 2)
                        dve.tensor_tensor(rot[:, :], by_cos[:, :], by_sin[:, :], ALU.add).then_inc(summed, 1)
                        dve.wait_ge(summed, kv * NROPE + r + 2)
                        high = kh[:, cols] if piece == K_ else qh[:, (piece - Q_) % 2, cols]
                        dve.tensor_copy(high, rot[:, :]).then_inc(rot_high, 1)

                    started, projected = False, []
                    for s in PLAN:
                        if s in ROPE:
                            if started:
                                projected.append(s)
                            else:
                                rotate(s)
                        elif s[0] == "turn_v":
                            k = slice(s[1] * BLK, (s[1] + 1) * BLK)
                            dve.wait_ge(v_high, kv * 2 + s[1] + 1)
                            dve.tensor_tensor(vl[:, k, :], g.bank(aux_bank(s)).rearrange("p (k e) -> p k e", k=BLK),
                                              vh[:, k, :].bitcast(F32), ALU.subtract).then_inc(v_split, 1)
                        elif s[0] == "begin":
                            low(0)
                            low(1)
                        elif s[0] == "unit":
                            _, j, qt = s
                            u = j * NT + qt
                            if u + 2 < UNITS:
                                low(u + 2)
                            for h in range(banks_of(qt)):
                                b = turned_of_group(u) + h
                                k = min(BLK, qt + 1 - BLK * h)
                                to = (slice(None), slice(BLK * h, BLK * h + k), slice((qt % BLK) * P, (qt % BLK + 1) * P))
                                dve.wait_ge(p_high, kv * BANKS_G + b + 1)
                                dve.tensor_tensor(pl[to], g.bank(4 + b % 2)[:, 0:k * P].rearrange("p (k q) -> p k q", k=k),
                                                  ph[to].bitcast(F32), ALU.subtract).then_inc(p_split, 1)
                            for p in projected:
                                rotate(p)
                            started, projected = True, []
                        elif s[0] == "weigh":
                            _, j, c = s
                            q = 2 * j + c
                            tiles = slice(c * BLK, (c + 1) * BLK)
                            dve.wait_ge(probs_ready, kv * UNITS + j * NT + (c + 1) * BLK + 2)
                            dve.reciprocal(rinv[:, j % 2, tiles], rsum[:, j % 2, tiles]).then_inc(rinv_ready, 1)
                            dve.wait_ge(c_high, kv * 2 * GH + q + 1)
                            dve.tensor_tensor(cl[:, :], g.bank(aux_bank(s)), ch[:, :].bitcast(F32), ALU.subtract).then_inc(c_split, 1)
                        elif s[0] == "out":
                            _, j, t = s
                            dve.wait_ge(rinv_ready, kv * 2 * GH + 2 * j + t // BLK + 1)
                            dve.wait_ge(aux_ready, (kv + 1) * NAUX + AUX[s] + 1)
                            dve.scalar_tensor_tensor(out=g.x[:, t, :], in0=g.bank(aux_bank(s)), scalar=rinv[:, j % 2, t:t + 1],
                                                     in1=g.x[:, t, :], op0=ALU.mult, op1=ALU.add).then_inc(added, 1)


GU = KC
WP = GU + IC
ITEMS = 2 * IC


def routed_ffn(nc, g, d, name):
    with stage(nc, name) as (sb, sem):
        ln = Normalisation(sb, sem)
        xh, xl = sb("xh", [P, KC, T], F32R), sb("xl", [P, KC, T], F32R)
        gw = sb("gw", [P, KC, NE])
        gwh, gwl = sb("gwh", [P, KC, NE], F32R), sb("gwl", [P, KC, NE], F32R)
        gb = sb("gb", [P, NE])
        number = sb("number", [P, NE])
        score, top = sb("score", [P, NT, NE]), sb("top", [P, NT, 8])
        at, at_f = sb("at", [P, NT, 8], U32), sb("at_f", [P, NT, 8])
        wsum, winv = sb("wsum", [P, NT]), sb("winv", [P, NT])
        tw = sb("tw", [P, NT, TOPK])
        hit, cw = sb("hit", [P, NT, NE]), sb("cw", [P, NT, NE])
        cwe = sb("cwe", [P, 2, NT])
        raw = sb("raw", [P, WP, H])
        wh, wl = sb("wh", [P, 2, WP, H], F32R), sb("wl", [P, 2, WP, H], F32R)
        gate = sb("gate", [P, 2, HALF])
        z = sb("z", [P, 2, HALF])
        zh, zl = sb("zh", [P, IC, T], F32R), sb("zl", [P, IC, T], F32R)

        loaded, filled, gw_high, gw_split = sem("loaded"), sem("filled"), sem("gw_high"), sem("gw_split")
        x_high, x_split = sem("x_high"), sem("x_split")
        logits_ready, score_ready, pick_step, cwe_ready = sem("logits_ready"), sem("score_ready"), sem("pick_step"), sem("cwe_ready")
        raw_loaded = [sem(f"raw_loaded{i}") for i in range(WP)]
        w_high, w_split = sem("w_high"), sem("w_split")
        items_ready, gate_ready, z_ready = sem("items_ready"), sem("gate_ready"), sem("z_ready")
        z_high, z_split, out_ready, added = sem("z_high"), sem("z_split"), sem("out_ready"), sem("added")

        with nc.Block() as block:
            @block.sync
            def _(sp):
                sp.dma_start(gw[:, :, :], d["L1f_gate"]).then_inc(loaded, 16)
                sp.dma_start(gb[:, :], d["L1f_bias"].partition_broadcast(P)).then_inc(loaded, 16)

                def load(e):
                    for p in range(WP):
                        sp.wait_ge(w_split, e * WP + p + 1)
                        src = d["L1f_w"][e * WP + p] if isinstance(e, int) else \
                            d["L1f_w"][bass.ds(e * WP + p, 1), :, :].squeeze(0)
                        sp.dma_start(raw[:, p, :], src).then_inc(raw_loaded[p], 16)

                with sp.Fori(0, NE) as e:
                    load(e)
                load(NE)

            @block.gpsimd
            def _(pool):
                for e in range(NE):
                    pool.memset(number[:, e:e + 1], float(e)).then_inc(filled, 1)
                pool.sem_inc(w_split, WP)
                pool.sem_inc(z_split, 2)

                def split(e, par, p):
                    pool.wait_ge(raw_loaded[p], e * 16 + 16)
                    if not isinstance(e, int) or e:
                        if p < GU:
                            pool.wait_ge(items_ready, e * ITEMS)
                        else:
                            pool.wait_ge(out_ready, e * NT)
                    pool.tensor_tensor(wh[:, par, p, :], raw[:, p, :], g.ones[:, :], ALU.mult).then_inc(w_high, 1)
                    pool.wait_ge(w_high, e * WP + p + 1)
                    pool.tensor_tensor(wl[:, par, p, :], raw[:, p, :], wh[:, par, p, :].bitcast(F32), ALU.subtract)\
                        .then_inc(w_split, 1)

                def z_low(e, m):
                    c, h = m % IC, m // IC
                    s = slice(h * HALF, (h + 1) * HALF)
                    pool.wait_ge(z_high, e * ITEMS + m + 1)
                    pool.tensor_tensor(zl[:, c, s], z[:, m % 2, :], zh[:, c, s].bitcast(F32), ALU.subtract)\
                        .then_inc(z_split, 1)

                for p in range(WP):
                    split(0, 0, p)

                def expert(e, par, following):
                    for m in range(ITEMS):
                        z_low(e, m)
                        if following:
                            for p in ((0,), (1, 2), (3,), (4, 5))[m]:
                                split(e + 1, 1 - par, p)

                with pool.Fori(0, NE // 2) as pair:
                    for par in range(2):
                        expert(2 * pair + par, par, True)
                expert(NE, 0, False)

            @block.scalar
            def _(act):
                ln_root(act, ln)
                turned_rows_high(act, g, ln, xh, x_high)
                act.wait_ge(logits_ready, 1)
                act.activation(score[:, :, :].rearrange("p t e -> p (t e)"), g.bank(6)[:, 0:NT * NE], ACT.Sigmoid)\
                    .then_inc(score_ready, 1)

                def expert(e, par):
                    for m in range(ITEMS):
                        c, h = m % IC, m // IC
                        act.wait_ge(items_ready, e * ITEMS + m + 1 + ITEMS)
                        act.wait_ge(z_ready, e * ITEMS + m + 1)
                        act.activation(gate[:, m % 2, :], g.pair[m % 2][:, 0:HALF], ACT.Silu).then_inc(gate_ready, 1)
                        act.wait_ge(z_ready, e * ITEMS + m + 3)
                        act.activation(zh[:, c, h * HALF:(h + 1) * HALF], z[:, m % 2, :], ACT.Copy).then_inc(z_high, 1)

                with act.Fori(0, NE // 2) as pair:
                    for par in range(2):
                        expert(2 * pair + par, par)
                expert(NE, 0)

            @block.tensor
            def _(pe):
                for t in range(NT):
                    if t >= 2:
                        pe.wait_ge(x_split, t - 1)
                    ln_turn(pe, g, ln, t)
                pe.wait_ge(gw_split, 1)
                for t in range(NT):
                    pe.wait_ge(x_split, t + 1)
                    for k in range(KC):
                        s = slice(t * P, (t + 1) * P)
                        mm = product(pe, g.bank(6)[:, t * NE:(t + 1) * NE], xh[:, k, s], xl[:, k, s],
                                     gwh[:, k, :], gwl[:, k, :], k == 0, k == KC - 1)
                mm.then_inc(logits_ready, 1)
                pe.sem_inc(items_ready, ITEMS)
                pe.sem_inc(out_ready, NT)
                pe.wait_ge(score_ready, 1)

                def expert(e, par):
                    pe.wait_ge(w_split, e * WP + GU + WP)
                    for m in range(ITEMS):
                        c, h = m % IC, m // IC
                        pe.wait_ge(z_ready, e * ITEMS + m + 1)
                        for u in range(2):
                            cols = slice(u * INNER + c * P, u * INNER + (c + 1) * P)
                            toks = slice(h * HALF, (h + 1) * HALF)
                            for k in range(KC):
                                mm = product(pe, g.pair[m % 2][:, u * HALF:(u + 1) * HALF], wh[:, par, k, cols],
                                             wl[:, par, k, cols], xh[:, k, toks], xl[:, k, toks], k == 0, k == KC - 1)
                        mm.then_inc(items_ready, 1)
                    pe.wait_ge(w_split, e * WP + WP + WP)
                    for t in range(NT):
                        if t % BLK == 0:
                            pe.wait_ge(z_split, e * ITEMS + IC * (t // BLK + 1) + 2)
                        pe.wait_ge(added, e * NT + t + 1)
                        s = slice(t * P, (t + 1) * P)
                        for c in range(IC):
                            mm = product(pe, g.bank(4 + t % 4), zh[:, c, s], zl[:, c, s], wh[:, par, GU + c, :],
                                         wl[:, par, GU + c, :], c == 0, c == IC - 1)
                        mm.then_inc(out_ready, 1)

                with pe.Fori(0, NE // 2) as pair:
                    for par in range(2):
                        expert(2 * pair + par, par)
                expert(NE, 0)

            @block.vector
            def _(dve):
                ln_stats(dve, g, ln)
                ln_row(dve, g, ln, 0)
                ln_row(dve, g, ln, 1)
                dve.wait_ge(loaded, 32)
                dve.tensor_copy(gwh[:, :, :], gw[:, :, :]).then_inc(gw_high, 1)
                dve.wait_ge(gw_high, 1)
                dve.tensor_tensor(gwl[:, :, :], gw[:, :, :], gwh[:, :, :].bitcast(F32), ALU.subtract).then_inc(gw_split, 1)
                for t in range(NT):
                    if t + 2 < NT:
                        ln_row(dve, g, ln, t + 2)
                    turned_rows_low(dve, g, t, xh, xl, x_high, x_split)

                step = [0]

                def then(i):
                    i.then_inc(pick_step, 1)
                    step[0] += 1
                    dve.wait_ge(pick_step, step[0])

                def along(v, shape):
                    return v.to_broadcast([P] + shape)

                dve.wait_ge(filled, NE)
                dve.wait_ge(score_ready, 1)
                then(dve.tensor_tensor(score[:, :, :], score[:, :, :], along(gb[:, :].unsqueeze(1), [NT, NE]), ALU.add))
                for t in range(NT):
                    dve.max(top[:, t, :], score[:, t, :]).then_inc(pick_step, 1)
                step[0] += NT
                dve.wait_ge(pick_step, step[0])
                for t in range(NT):
                    dve.max_index(at[:, t, :], top[:, t, :], score[:, t, :]).then_inc(pick_step, 1)
                step[0] += NT
                dve.wait_ge(pick_step, step[0])
                then(dve.tensor_copy(at_f[:, :, :], at[:, :, :]))
                then(dve.tensor_reduce(wsum[:, :], top[:, :, 0:TOPK], AX_X, ALU.add))
                then(dve.tensor_scalar_add(wsum[:, :], wsum[:, :], 1e-20))
                then(dve.reciprocal(winv[:, :], wsum[:, :]))
                then(dve.tensor_tensor(tw[:, :, :], top[:, :, 0:TOPK], along(winv[:, :].unsqueeze(2), [NT, TOPK]), ALU.mult))
                for i in range(TOPK):
                    to = hit if i else cw
                    then(dve.tensor_tensor(to[:, :, :], along(number[:, :].unsqueeze(1), [NT, NE]),
                                           along(at_f[:, :, i:i + 1], [NT, NE]), ALU.is_equal))
                    then(dve.tensor_tensor(to[:, :, :], to[:, :, :], along(tw[:, :, i:i + 1], [NT, NE]), ALU.mult))
                    if i:
                        then(dve.tensor_tensor(cw[:, :, :], cw[:, :, :], hit[:, :, :], ALU.add))
                dve.sem_inc(z_ready, 2)
                dve.sem_inc(added, 4)

                def expert(e, par, shared):
                    if shared:
                        dve.memset(cwe[:, par, :], 1.0).then_inc(cwe_ready, 1)
                    else:
                        dve.tensor_copy(cwe[:, par, :].unsqueeze(2), cw[:, :, bass.ds(e, 1)]).then_inc(cwe_ready, 1)
                    for m in range(ITEMS):
                        dve.wait_ge(gate_ready, e * ITEMS + m + 1)
                        dve.wait_ge(z_split, e * ITEMS + m + 1)
                        dve.tensor_tensor(z[:, m % 2, :], gate[:, m % 2, :], g.pair[m % 2][:, HALF:2 * HALF], ALU.mult)\
                            .then_inc(z_ready, 1)
                    dve.wait_ge(cwe_ready, e + 1)
                    for t in range(NT):
                        dve.wait_ge(out_ready, e * NT + t + 1 + NT)
                        dve.scalar_tensor_tensor(out=g.x[:, t, :], in0=g.bank(4 + t % 4), scalar=cwe[:, par, t:t + 1],
                                                 in1=g.x[:, t, :], op0=ALU.mult, op1=ALU.add).then_inc(added, 1)

                with dve.Fori(0, NE // 2) as pair:
                    for par in range(2):
                        expert(2 * pair + par, par, False)
                expert(NE, 0, True)


def build(nc, d, out):
    with ExitStack() as ctx:
        g = Shared(nc, ctx)
        constants(nc, g, d)
        steps = [
            lambda: attention16(nc, g, d, "L0a"),
            lambda: lora_ffn(nc, g, d, "L0f"),
            lambda: single_head(nc, g, d, "L0b"),
            lambda: lora_ffn(nc, g, d, "L0g"),
            lambda: attention128(nc, g, d, "L1a"),
            lambda: routed_ffn(nc, g, d, "L1f"),
            lambda: attention16(nc, g, d, "L1b"),
            lambda: routed_ffn(nc, g, d, "L1g"),
        ]
        for step in steps:
            step()
        store(nc, g, out)


def layouts(i):
    import numpy as np

    def chunks(w):
        w = np.asarray(w)
        return np.ascontiguousarray(w.reshape(-1, P, w.shape[1]).transpose(1, 0, 2))

    per = GH + 2
    order = [(g * per + j) * HD + e for g in range(NKV) for j in range(GH) for e in range(HD)]
    order += [(g * per + GH + s) * HD + e for s in range(2) for g in range(NKV) for e in range(HD)]
    a = {"x": np.ascontiguousarray(np.asarray(i["L0_attn_a_hidden_states"]).reshape(NT, P, H).transpose(1, 0, 2))}
    for name, src in (("L0a", "L0_attn_a"), ("L1b", "L1_attn_b")):
        a[name + "_wqkv"] = chunks(np.asarray(i[src + "_w_qkv"])[order].T)
        a[name + "_bqkv"] = np.asarray(i[src + "_b_qkv"])[order]
        a[name + "_wd"] = chunks(np.asarray(i[src + "_w_dense"]).T)
        a[name + "_bd"] = np.asarray(i[src + "_b_dense"])
    inv = (1.0 / np.float32(1000000.0) ** (np.arange(0, HD, 2, dtype=np.float32) / np.float32(HD))).astype(np.float32)
    ang = np.outer(np.arange(T, dtype=np.float32), inv).astype(np.float32)
    cos, sin = np.cos(ang), np.sin(ang)
    cos2 = np.concatenate([cos, cos], 1)
    sin2 = np.concatenate([-sin, sin], 1)
    scale = np.float32(-1.0 / HD)
    for name, tab in (("cos16", cos2), ("sin16", sin2)):
        both = np.stack([tab * scale, tab], 1).astype(np.float32)
        a[name] = np.ascontiguousarray(both.reshape(NT, P, 2, HD).transpose(1, 0, 2, 3))

    a["L0f_w"] = chunks(np.asarray(i["L0_ffn_W_up"]).T)
    lora_a = np.asarray(i["L0_ffn_lora_A"]).reshape(ZR, H)
    a["L0f_ga"] = chunks(np.concatenate([np.asarray(i["L0_ffn_gate_w"]), lora_a], 0).T)
    a["L0f_b"] = np.ascontiguousarray(np.asarray(i["L0_ffn_lora_B"]).transpose(0, 2, 1).reshape(ZR, H))
    a["L0f_bias"] = np.asarray(i["L0_ffn_expert_bias"])

    a["L0b_w"] = chunks(i["L0_attn_b_Wqkv"])
    b = np.asarray(i["L0_attn_b_bqkv"])
    a["L0b_bqk"] = np.ascontiguousarray(b[:2 * D].reshape(2, D).T)
    a["L0b_bv"] = b[2 * D:]
    a["L0b_wo"] = np.asarray(i["L0_attn_b_Wo"])
    a["L0b_bo"] = np.asarray(i["L0_attn_b_bo"])

    wq, wk, wv, wo = (np.asarray(i["L1_attn_a_" + s]) for s in ("Wq", "Wk", "Wv", "Wo"))
    a["L1a_w"] = np.empty((NKV * PIECES, P, H), wq.dtype)
    for grp in range(NKV):
        for pos, piece in enumerate(SPLIT_ORDER):
            if piece >= O_:
                h = grp * GH + piece - O_
                w = wo[h * D:(h + 1) * D]
            else:
                src, h = {K_: (wk, grp), V_: (wv, grp)}.get(piece, (wq, grp * GH + piece - Q_))
                w = chunks(src[:, h * D:(h + 1) * D]).reshape(P, H)
            a["L1a_w"][grp * PIECES + pos] = w
    bq, bk, bv = (np.asarray(i["L1_attn_a_" + s]) for s in ("bq", "bk", "bv"))
    a["L1a_bias"] = np.ascontiguousarray(np.concatenate(
        [bk.reshape(NKV, 1, D), bv.reshape(NKV, 1, D), bq.reshape(NKV, GH, D)], 1).transpose(2, 1, 0))
    a["L1a_bo"] = np.asarray(i["L1_attn_a_bo"])
    inv = (1.0 / np.float32(10000.0) ** (np.arange(0, D // 2, dtype=np.float32) / np.float32(D // 2))).astype(np.float32)
    ang = (inv[:, None] * np.arange(T, dtype=np.float32)[None, :]).astype(np.float32)
    a["cos128"] = np.concatenate([np.cos(ang), np.cos(ang)], 0)
    a["sin128"] = np.concatenate([-np.sin(ang), np.sin(ang)], 0)

    wg, wu, wd, sg, su, sd = (np.asarray(i["L1_ffn_" + s]) for s in ("Wg", "Wu", "Wd", "Sg", "Su", "Sd"))
    a["L1f_w"] = np.empty(((NE + 1) * WP, P, H), wg.dtype)
    for e in range(NE + 1):
        gg, uu, dd = (wg[e], wu[e], wd[e]) if e < NE else (sg, su, sd)
        a["L1f_w"][e * WP:e * WP + GU, :, 0:INNER] = gg.T.reshape(KC, P, INNER)
        a["L1f_w"][e * WP:e * WP + GU, :, INNER:H] = uu.T.reshape(KC, P, INNER)
        a["L1f_w"][e * WP + GU:(e + 1) * WP] = dd.T.reshape(IC, P, H)
    a["L1f_gate"] = chunks(np.asarray(i["L1_ffn_gate_w"]).T)
    a["L1f_bias"] = np.asarray(i["L1_ffn_bias"])
    return a


def kernel(**inputs):
    import numpy as np
    import concourse.bacc as bacc
    from concourse.bass_utils import run_bass_kernel_spmd

    nc = bacc.Bacc("TRN2", target_bir_lowering=False, num_devices=1)
    arrays, aps = {}, {}
    for name, v in layouts(inputs).items():
        arrays["in_" + name] = np.ascontiguousarray(v)
        aps[name] = nc.dram_tensor("in_" + name, v.shape, mybir.dt.from_np(v.dtype), kind="ExternalInput").ap()
    out = nc.dram_tensor("out", (P, NT, H), F32, kind="ExternalOutput").ap()
    build(nc, aps, out)
    got = run_bass_kernel_spmd(nc, [arrays], core_ids=[0]).results[0]["out"]
    return np.ascontiguousarray(got.transpose(1, 0, 2)).reshape(1, T, H)
```

```python
from contextlib import ExitStack, contextmanager

import concourse.bass as bass
from concourse import mybir

ALU = mybir.AluOpType
ACT = mybir.ActivationFunctionType
F32 = mybir.dt.float32
F32R = mybir.dt.float32r
BF16 = mybir.dt.bfloat16
U32 = mybir.dt.uint32
AX_X = mybir.AxisListType.X

P = 128
T = 1024
NT = T // P
H = 512
KC = H // P
HALF = T // 2
BLK = HALF // P
EPS = 1e-5
BIG = 1e30
LOWEST = -3e38

NH, NKV, HD = 32, 8, 16
GH = NH // NKV
QKV = (NH + 2 * NKV) * HD
NQK = NH + NKV
SLOTS = P // HD

D = 128
SCALE = float(D) ** -0.5

NE0, RANK = 4, 8
ZR = NE0 * RANK

NE, INNER, TOPK = 16, 256, 4
IC = INNER // P


def banks_of(qt):
    return qt // BLK + 1


BANKS_BEFORE = [sum(banks_of(q) for q in range(qt)) for qt in range(NT + 1)]


@contextmanager
def stage(nc, name):
    sems = []
    with ExitStack() as scope:
        def sb(n, shape, dt=F32, at=scope):
            return at.enter_context(nc.sbuf_tensor(f"{name}_{n}", shape, dt))

        def sem(n):
            sems.append(nc.alloc_semaphore(f"{name}_{n}"))
            return sems[-1]

        yield sb, sem
    nc.clear_and_free_semaphores(sems)
    nc.all_engine_barrier()


class Shared:

    def __init__(self, nc, ctx):
        def sb(name, shape, dt=F32):
            return ctx.enter_context(nc.sbuf_tensor(name, shape, dt))

        self.x = sb("x", [P, NT, H])
        self.ident, self.ident_b = sb("ident", [P, P]), sb("ident_b", [P, P], BF16)
        self.ones = sb("ones", [P, H])
        self.mask_b = sb("mask_b", [P, P], BF16)
        self.pair = [ctx.enter_context(nc.psum_tensor(f"pair{i}", [P, 2 * HALF], F32)) for i in range(2)]
        self.single = [ctx.enter_context(nc.psum_tensor(f"single{i}", [P, HALF], F32)) for i in range(4)]

    def bank(self, i):
        return self.pair[i // 2][:, (i % 2) * HALF:(i % 2 + 1) * HALF] if i < 4 else self.single[i - 4][:, :]


class Normalisation:

    def __init__(self, sb, sem):
        self.xn = sb("xn", [P, 2, H])
        self.stats, self.mv = sb("stats", [P, NT, 6]), sb("mv", [P, NT, 2])
        self.veps, self.std, self.rstd = sb("veps", [P, NT]), sb("std", [P, NT]), sb("rstd", [P, NT])
        self.step, self.std_ready = sem("ln_step"), sem("std_ready")
        self.row_ready, self.turned = sem("row_ready"), sem("row_turned")


def ln_stats(dve, g, n):
    for t in range(NT):
        dve.bn_stats(n.stats[:, t, :], g.x[:, t, :]).then_inc(n.step, 1)
    for t in range(NT):
        dve.wait_ge(n.step, NT)
        dve.bn_aggr(n.mv[:, t, :], n.stats[:, t, :]).then_inc(n.step, 1)
    dve.wait_ge(n.step, 2 * NT)
    dve.tensor_scalar_add(n.veps[:, :], n.mv[:, :, 1], EPS).then_inc(n.step, 1)
    dve.wait_ge(n.std_ready, 1)
    dve.reciprocal(n.rstd[:, :], n.std[:, :]).then_inc(n.step, 1)
    dve.wait_ge(n.step, 2 * NT + 2)


def ln_root(act, n):
    act.wait_ge(n.step, 2 * NT + 1)
    act.activation(n.std[:, :], n.veps[:, :], ACT.Sqrt).then_inc(n.std_ready, 1)


def ln_row(dve, g, n, t):
    if t >= 2:
        dve.wait_ge(n.turned, t - 1)
    dve.tensor_scalar(n.xn[:, t % 2, :], g.x[:, t, :], n.mv[:, t, 0:1], n.rstd[:, t:t + 1],
                      ALU.subtract, ALU.mult).then_inc(n.row_ready, 1)


def ln_turn(pe, g, n, t):
    pe.wait_ge(n.row_ready, t + 1)
    for k in range(KC):
        mm = pe.transpose(g.bank(4 + t % 2)[:, k * P:(k + 1) * P], n.xn[:, t % 2, k * P:(k + 1) * P], g.ident[:, :])
    mm.then_inc(n.turned, 1)


def turned_row(g, t):
    return g.bank(4 + t % 2).rearrange("p (k t) -> p k t", k=KC)


def output_bias(pool, g, n, bd, loaded, count, biased):
    pool.wait_ge(loaded, count)
    for t in range(NT):
        pool.wait_ge(n.row_ready, t + 1)
        pool.tensor_tensor(g.x[:, t, :], g.x[:, t, :], bd[:, :], ALU.add).then_inc(biased, 1)


def constants(nc, g, d):
    with stage(nc, "const") as (sb, sem):
        done = sem("done")
        loaded = sem("loaded")
        with nc.Block() as block:
            @block.sync
            def _(sp):
                sp.dma_start(g.x[:, :, :], d["x"]).then_inc(loaded, 16)
                sp.wait_ge(loaded, 16)

            @block.gpsimd
            def _(pool):
                pool.memset(g.ident[:, :], 0.0).then_inc(done, 1)
                pool.memset(g.mask_b[:, :], 0.0).then_inc(done, 1)
                pool.memset(g.ones[:, :], 1.0).then_inc(done, 1)
                pool.wait_ge(done, 3)
                pool.affine_select(out=g.ident[:, :], in_=g.ident[:, :], compare_op=ALU.not_equal, fill=1.0,
                                   base=0, pattern=[[-1, P]], channel_multiplier=1).then_inc(done, 1)
                pool.affine_select(out=g.mask_b[:, :], in_=g.mask_b[:, :], compare_op=ALU.is_ge, fill=BIG,
                                   base=0, pattern=[[-1, P]], channel_multiplier=1).then_inc(done, 1)
                pool.wait_ge(done, 5)
                pool.tensor_copy(g.ident_b[:, :], g.ident[:, :]).then_inc(done, 1)
                pool.wait_ge(done, 6)


def store(nc, g, out):
    with stage(nc, "store") as (sb, sem):
        stored = sem("stored")
        with nc.Block() as block:
            @block.sync
            def _(sp):
                sp.dma_start(out, g.x[:, :, :]).then_inc(stored, 16)
                sp.wait_ge(stored, 16)


def fills():
    out = []
    for qt in range(NT):
        for part in range(banks_of(qt)):
            w = min(HALF, (qt + 1) * P - part * HALF)
            n = max(1, min(GH, HALF // w))
            out += [(qt, part, j, n, w) for j in range(0, GH, n)]
    return out


def groups():
    return [(c, kt) for c in range(2) for kt in range(0, BLK * (c + 1), 2)]


FILLS, GROUPS = fills(), groups()
NF, NG = len(FILLS), len(GROUPS)
NF0 = sum(f[0] < BLK for f in FILLS)
NU = NG * GH
GROUPS_BEFORE = (0, sum(c == 0 for c, _ in GROUPS), NG)


def first_query(c, kt):
    return max(0, kt - BLK * c) * P


def heads16_plan():
    plan, f = [], 0
    elements = sum(n * w for _, _, _, n, w in FILLS)
    spread = 0
    for g, (c, kt) in enumerate(GROUPS):
        for j in range(GH):
            plan.append(("seen", g, j))
            spread += elements / NU
            while f < NF - 2 and sum(n * w for _, _, _, n, w in FILLS[:f + 1]) <= spread:
                plan.append(("fill", f))
                f += 1
            if g == 0 and j == 2:
                plan.append(("values",))
            if GH - 1 <= g * GH + j < GH - 1 + BLK:
                plan.append(("row", 1, g * GH + j - GH + 1))
            if 13 <= g * GH + j < 13 + BLK:
                plan.append(("row", 0, g * GH + j - 13))
            if g and j == 1:
                plan.append(("weigh", g - 1))
                if g == GROUPS_BEFORE[1]:
                    plan.append(("copy", 0))
            if g == GROUPS_BEFORE[1] and j == 3:
                plan.append(("turn", 0))
    return plan + [("fill", NF - 2), ("weigh", NG - 1), ("copy", 1), ("fill", NF - 1), ("turn", 1)]


PLAN16 = heads16_plan()
ROWS = 2 * BLK
KS = 6 * HD


def row_number(kv, c, i):
    return kv * ROWS + c * BLK + i


class Heads16:

    def __init__(self, sb, sem):
        self.xT = sb("xT", [P, KC, T])
        self.w = sb("w", [P, KC, QKV])
        self.bias = sb("bias", [P, QKV])
        self.cos = sb("cos", [P, NT, 2, HD])
        self.sin = sb("sin", [P, NT, 2, HD])
        self.wd = sb("wd", [P, KC, H])
        self.bd = sb("bd", [P, H])
        self.v = sb("v", [P, NT, NKV, HD])
        self.vg = sb("vg", [P, NT, 32])
        self.parts = sb("parts", [P, NT, GH, 32], BF16)
        self.zero = sb("zero", [P, BLK * GH])
        self.qkT = sb("qkT", [P, NQK, T], BF16)
        with ExitStack() as proj:
            def c(n, shape, dt=F32):
                return sb(n, shape, dt, proj)
            self.qks = c("qk", [P, 2, NQK, HD])
            self.rcs = c("rc", [P, 2, NQK, HD])
            self.rs = c("rs", [P, NQK, HD])
            self.rest1s = c("rest1", [P, 2, NQK, HD])
            self.stacks = c("stack", [P, 2, NQK, SLOTS, HD], BF16)
        self.least = sb("least", [P, 2, NT, GH])
        self.most, self.most_rest = sb("most", [P, BLK, GH]), sb("most_rest", [P, BLK, GH])
        self.probsT = sb("probsT", [P, 2, GH, 2 * HALF])
        self.ctxT = sb("ctxT", [P, HALF])
        self.rsum = sb("rsum", [P, BLK, GH])
        self.oT = sb("oT", [P, KC, P])
        self.ctx = self.xT[:, :, :].rearrange("p k t -> p (k t)").rearrange("p (n h) -> p n h", n=NT)
        self.w_loaded, self.xT_ready, self.qkv_ready = sem("w_loaded"), sem("xT_ready"), sem("qkv_ready")
        self.qkv_read, self.rope_step, self.split1 = sem("qkv_read"), sem("rope_step"), sem("split1")
        self.rest1_ready, self.rest2_ready, self.stack_ready = sem("rest1_ready"), sem("rest2_ready"), sem("stack_ready")
        self.stackT_ready, self.stackT_copied, self.vg_ready = sem("stackT_ready"), sem("stackT_copied"), sem("vg_ready")
        self.fill_ready, self.fill_read, self.least_ready = sem("fill_ready"), sem("fill_read"), sem("least_ready")
        self.parts_ready, self.seen_ready, self.probs_ready = sem("parts_ready"), sem("seen_ready"), sem("probs_ready")
        self.parts_step, self.most_turned, self.most_copied = sem("parts_step"), sem("most_turned"), sem("most_copied")
        self.most_awaited, self.slots_ready = sem("most_awaited"), sem("slots_ready")
        self.pv_ready, self.ctxT_ready, self.ctx_turned = sem("pv_ready"), sem("ctxT_ready"), sem("ctx_turned")
        self.rsum_ready, self.ctx_ready, self.ctxT2_ready = sem("rsum_ready"), sem("ctx_ready"), sem("ctxT2_ready")
        self.oT_ready, self.out_ready, self.biased = sem("oT_ready"), sem("out_ready"), sem("biased")
        self.added = sem("added")


def attention16(nc, g, d, name):
    with stage(nc, name) as (sb, sem):
        ln = Normalisation(sb, sem)
        a = Heads16(sb, sem)

        with nc.Block() as block:
            @block.sync
            def _(sp):
                sp.dma_start(a.w[:, :, :], d[name + "_wqkv"]).then_inc(a.w_loaded, 16)
                sp.dma_start(a.bias[:, :], d[name + "_bqkv"].partition_broadcast(P)).then_inc(a.w_loaded, 16)
                sp.dma_start(a.cos[:, :, :, :], d["cos16"]).then_inc(a.w_loaded, 16)
                sp.dma_start(a.sin[:, :, :, :], d["sin16"]).then_inc(a.w_loaded, 16)
                sp.dma_start(a.wd[:, :, :], d[name + "_wd"]).then_inc(a.w_loaded, 16)
                sp.dma_start(a.bd[:, :], d[name + "_bd"].partition_broadcast(P)).then_inc(a.w_loaded, 16)

            @block.gpsimd
            def _(pool):
                pool.memset(a.vg[:, :, :], 0.0).then_inc(a.vg_ready, 1)
                pool.wait_ge(a.vg_ready, 1)
                pool.memset(a.vg[:, :, HD:HD + 1], 1.0).then_inc(a.vg_ready, 1)
                pool.memset(a.stacks[:, :, :, 6:8, :], 0.0).then_inc(a.slots_ready, 1)
                pool.memset(a.parts[:, :, :, :], 0.0).then_inc(a.slots_ready, 1)
                pool.memset(a.zero[:, :], 0.0).then_inc(a.slots_ready, 1)
                pool.wait_ge(a.slots_ready, 3)
                pool.memset(a.stacks[:, :, NH:NQK, 6, 0:3], 1.0).then_inc(a.slots_ready, 1)
                for t in range(NT):
                    pool.wait_ge(a.split1, t + 1)
                    if t >= 2:
                        pool.wait_ge(a.stack_ready, 2 * (t - 1))
                    pool.tensor_tensor(a.rest1s[:, t % 2, :, :], a.rcs[:, t % 2, :, :], a.stacks[:, t % 2, :, 1, :],
                                       ALU.subtract).then_inc(a.rest1_ready, 1)
                output_bias(pool, g, ln, a.bd, a.w_loaded, 96, a.biased)
                pool.sem_inc(a.parts_ready, 2)

                def split_most(kv, c):
                    tiles = slice(c * BLK, (c + 1) * BLK)
                    first = 5 * (2 * kv + c)
                    ones = g.ones[:, 0:BLK * GH].rearrange("p (t j) -> p t j", t=BLK)
                    pool.wait_ge(a.least_ready, kv * 2 + c + 1)
                    pool.wait_ge(a.most_turned, row_number(kv, c, BLK - 1) + 1)
                    pool.tensor_tensor(a.most[:, :, :], a.zero[:, :].rearrange("p (t j) -> p t j", t=BLK),
                                       a.least[:, 0, tiles, :], ALU.subtract).then_inc(a.parts_step, 1)
                    pool.wait_ge(a.parts_step, first + 1)
                    pool.tensor_tensor(a.parts[:, tiles, :, 0], a.most[:, :, :], ones, ALU.mult).then_inc(a.parts_step, 1)
                    pool.wait_ge(a.parts_step, first + 2)
                    pool.tensor_tensor(a.most_rest[:, :, :], a.most[:, :, :], a.parts[:, tiles, :, 0], ALU.subtract)\
                        .then_inc(a.parts_step, 1)
                    pool.wait_ge(a.parts_step, first + 3)
                    pool.tensor_tensor(a.parts[:, tiles, :, 1], a.most_rest[:, :, :], ones, ALU.mult)\
                        .then_inc(a.parts_step, 1)
                    pool.wait_ge(a.parts_step, first + 4)
                    pool.tensor_tensor(a.parts[:, tiles, :, 2], a.most_rest[:, :, :], a.parts[:, tiles, :, 1], ALU.subtract)\
                        .then_inc(a.parts_step, 1)
                    pool.wait_ge(a.parts_step, first + 5)
                    pool.sem_inc(a.parts_ready, 1)

                with pool.Fori(0, NKV) as kv:
                    for c in range(2):
                        split_most(kv, c)

            @block.scalar
            def _(act):
                def row_copy(t):
                    act.wait_ge(ln.turned, t + 1)
                    act.activation(a.xT[:, :, t * P:(t + 1) * P], turned_row(g, t), ACT.Copy).then_inc(a.xT_ready, 1)

                def row_evac(kv, c, i):
                    qt = c * BLK + i
                    act.wait_ge(a.most_turned, ROWS + row_number(kv, c, i) + 1)
                    act.sem_inc(a.most_awaited, 1)
                    act.activation(a.qkT[KS:P, bass.ds(kv * GH, GH), qt * P:(qt + 1) * P],
                                   g.bank(7)[KS:P, :].rearrange("p (j q) -> p j q", j=GH), ACT.Copy)\
                        .then_inc(a.most_copied, 1)

                def group(kv, ahead):
                    for s in PLAN16:
                        if s[0] == "row" and (s[1] or ahead):
                            row_evac(kv if s[1] else kv + 1, s[1], s[2])
                        elif s[0] == "seen":
                            _, i, j = s
                            c, kt = GROUPS[i]
                            u = i * GH + j
                            n = sum(HALF - first_query(c, k) for k in (kt, kt + 1))
                            act.wait_ge(a.seen_ready, kv * NU + u + 1)
                            act.wait_ge(a.pv_ready, kv * NG + i + 1)
                            act.activation(a.probsT[:, i % 2, j, 0:n], g.pair[u % 2][:, 0:n], ACT.Exp, scale=-1.0)\
                                .then_inc(a.probs_ready, 1)
                        elif s[0] == "copy":
                            act.wait_ge(a.pv_ready, kv * NG + GROUPS_BEFORE[s[1] + 1] + 2)
                            act.wait_ge(a.ctx_turned, kv * 2 + s[1] + 1)
                            act.activation(a.ctxT[:, :], g.bank(6), ACT.Copy).then_inc(a.ctxT_ready, 1)

                ln_root(act, ln)
                def first_parts(t):
                    stack, rc = a.stacks[:, t % 2, :, :, :], a.rcs[:, t % 2, :, :]
                    act.wait_ge(a.rope_step, 4 * t + 4)
                    if t >= 2:
                        act.wait_ge(a.stackT_ready, 5 * (t - 1))
                    act.activation(stack[:, 0:NH, 0:3, :], rc[:, 0:NH, :].unsqueeze(2).to_broadcast([P, NH, 3, HD]), ACT.Copy)
                    act.activation(stack[:, NH:NQK, 1:6:2, :],
                                   rc[:, NH:NQK, :].unsqueeze(2).to_broadcast([P, NKV, 3, HD]), ACT.Copy)\
                        .then_inc(a.split1, 1)

                def stack_copy(t):
                    for n in range(5):
                        act.wait_ge(a.stackT_ready, 5 * t + n + 1)
                        act.activation(a.qkT[:, 8 * n:8 * n + 8, t * P:(t + 1) * P],
                                       g.bank(6 + (5 * t + n) % 2).bitcast(BF16).rearrange("p (h t) -> p h t", h=8),
                                       ACT.Copy).then_inc(a.stackT_copied, 1)

                row_copy(0)
                row_copy(1)
                for t in range(NT):
                    if t + 2 < NT:
                        row_copy(t + 2)
                    first_parts(t)
                    if t >= 1:
                        stack_copy(t - 1)
                stack_copy(NT - 1)
                act.sem_inc(a.ctxT_ready, 1)
                act.sem_inc(a.probs_ready, 2)
                for i in range(BLK):
                    row_evac(0, 0, i)
                with act.Fori(0, NKV - 1) as kv:
                    group(kv, True)
                group(NKV - 1, False)
                for t in range(NT):
                    act.wait_ge(a.ctxT2_ready, t + 1)
                    if t >= 1:
                        act.wait_ge(a.out_ready, t)
                    act.activation(a.oT[:, :, :], g.bank(4 + t % 2).rearrange("p (k t) -> p k t", k=KC),
                                   ACT.Copy).then_inc(a.oT_ready, 1)


            @block.tensor
            def _(pe):
                def qkv(t):
                    pe.wait_ge(a.xT_ready, t + 1)
                    if t >= 2:
                        pe.wait_ge(a.qkv_read, 2 * (t - 1))
                    for lo, hi, b in ((0, H, 0), (H, QKV, 1)):
                        for k in range(KC):
                            mm = pe.matmul(g.bank(2 * (t % 2) + b)[:, 0:hi - lo], a.xT[:, k, t * P:(t + 1) * P],
                                           a.w[:, k, lo:hi], start=(k == 0), stop=(k == KC - 1))
                    mm.then_inc(a.qkv_ready, 1)

                def turn_stack(t):
                    if t == 0:
                        pe.wait_ge(a.slots_ready, 4)
                    pe.wait_ge(a.stack_ready, 2 * t + 2)
                    for n in range(5):
                        if 5 * t + n >= 2:
                            pe.wait_ge(a.stackT_copied, 5 * t + n - 1)
                        for i in range(8):
                            mm = pe.transpose(g.bank(6 + (5 * t + n) % 2).bitcast(BF16)[:, i * P:(i + 1) * P],
                                              a.stacks[:, t % 2, 8 * n + i, :, :].rearrange("p s d -> p (s d)"),
                                              g.ident_b[:, :])
                        mm.then_inc(a.stackT_ready, 1)

                def turn_row(t):
                    if t >= 2:
                        pe.wait_ge(a.xT_ready, t - 1)
                    ln_turn(pe, g, ln, t)

                turn_row(0)
                turn_row(1)
                pe.wait_ge(a.w_loaded, 96)
                for t in range(2):
                    qkv(t)
                    turn_row(t + 2)
                for t in range(NT):
                    if t + 2 < NT:
                        qkv(t + 2)
                    turn_stack(t)
                    if t + 4 < NT:
                        turn_row(t + 4)
                pe.wait_ge(a.stackT_copied, 5 * NT)
                pe.wait_ge(a.qkv_read, 2 * NT)

                pe.sem_inc(a.most_turned, ROWS)
                pe.sem_inc(a.pv_ready, 2)
                pe.sem_inc(a.ctx_turned, 1)

                def fill(kv, f):
                    qt, part, first, heads, w = FILLS[f]
                    pe.wait_ge(a.fill_read, kv * NF + f + 1)
                    for i in range(heads):
                        o, k = i * w, part * HALF
                        masked = part == banks_of(qt) - 1
                        mm = pe.matmul(g.bank(4 + f % 2)[:, o:o + w],
                                       a.qkT[0:KS, bass.ds(kv * GH + first + i, 1), qt * P:(qt + 1) * P].squeeze(1),
                                       a.qkT[0:KS, bass.ds(kv + NH, 1), k:k + w].squeeze(1), start=True, stop=not masked)
                        if masked:
                            mm = pe.matmul(g.bank(4 + f % 2)[:, o + w - P:o + w], g.ident_b[:, :], g.mask_b[:, :],
                                           start=False, stop=True)
                    mm.then_inc(a.fill_ready, 1)

                def seen(kv, i, j):
                    c, pair = GROUPS[i]
                    u = i * GH + j
                    pe.wait_ge(a.probs_ready, kv * NU + u + 1)
                    pe.wait_ge(a.most_copied, row_number(kv, c, BLK - 1) + 1)
                    o = 0
                    for kt in (pair, pair + 1):
                        q = first_query(c, kt)
                        out = g.pair[u % 2][:, o:o + HALF - q]
                        diagonal = kt >= BLK * c
                        mm = pe.matmul(out, a.qkT[:, bass.ds(kv + NH, 1), kt * P:(kt + 1) * P].squeeze(1),
                                  a.qkT[:, bass.ds(kv * GH + j, 1), c * HALF + q:(c + 1) * HALF].squeeze(1),
                                  start=True, stop=not diagonal)
                        if diagonal:
                            mm = pe.matmul(out[:, 0:P], g.mask_b[:, :], g.ident_b[:, :], start=False, stop=True)
                        o += HALF - q
                    mm.then_inc(a.seen_ready, 1)

                def row(kv, c, i):
                    qt = c * BLK + i
                    pe.wait_ge(a.parts_ready, kv * 2 + c + 3)
                    if i or c or not isinstance(kv, int) or kv:
                        pe.wait_ge(a.most_copied, row_number(kv, c, i))
                    if i == 0 and c:
                        pe.wait_ge(a.ctx_ready, kv * 2 + 1)
                    elif i == 0 and not isinstance(kv, int):
                        pe.wait_ge(a.ctx_ready, kv * 2)
                    for j in range(GH):
                        mm = pe.matmul(g.bank(7)[KS:P, j * P:(j + 1) * P], a.parts[:, qt, j, :], g.ident_b[:, :],
                                       start=True, stop=True)
                    mm.then_inc(a.most_turned, 1)

                def weigh(kv, i):
                    c, pair = GROUPS[i]
                    pe.wait_ge(a.probs_ready, kv * NU + (i + 1) * GH + 2)
                    if i == 0:
                        pe.wait_ge(a.vg_ready, kv + 3)
                    if i in GROUPS_BEFORE:
                        pe.wait_ge(a.ctxT_ready, kv * 2 + c + 1)
                    o = 0
                    for kt in (pair, pair + 1):
                        q = first_query(c, kt)
                        for j in range(GH):
                            mm = pe.matmul(g.bank(6)[32 * j:32 * j + 32, q:HALF], a.vg[:, kt, :],
                                           a.probsT[:, i % 2, j, o:o + HALF - q], start=kt == 0,
                                           stop=kt == BLK * (c + 1) - 1)
                        o += HALF - q
                    mm.then_inc(a.pv_ready, 1)

                def turn_ctx(kv, c, ahead):
                    pe.wait_ge(a.ctxT_ready, kv * 2 + c + 2)
                    pe.wait_ge(a.ctx_ready, kv * 2 + c + 1)
                    if c == 0 or ahead:
                        pe.wait_ge(a.most_copied, kv * ROWS + (c + 2) * BLK)
                    for t in range(BLK):
                        mm = pe.transpose(g.bank(7)[:, t * P:(t + 1) * P], a.ctxT[:, t * P:(t + 1) * P], g.ident[:, :])
                    mm.then_inc(a.ctx_turned, 1)

                def group(kv, ahead):
                    for s in PLAN16:
                        if s[0] == "seen":
                            seen(kv, s[1], s[2])
                        elif s[0] == "row" and (s[1] or ahead):
                            row(kv if s[1] else kv + 1, s[1], s[2])
                        elif s[0] == "fill" and ahead:
                            fill(kv + 1, s[1])
                        elif s[0] == "weigh":
                            weigh(kv, s[1])
                        elif s[0] == "turn":
                            turn_ctx(kv, s[1], ahead)

                for f in range(NF):
                    fill(0, f)
                    if f >= NF - 2 * BLK and f % 2:
                        row(0, 0, (f - NF + 2 * BLK) // 2)
                with pe.Fori(0, NKV - 1) as kv:
                    group(kv, True)
                group(NKV - 1, False)

                def turn_o(t):
                    pe.wait_ge(a.ctx_ready, NKV * 2 + 1)
                    if t >= 2:
                        pe.wait_ge(a.oT_ready, t - 1)
                    for k in range(KC):
                        mm = pe.transpose(g.bank(4 + t % 2)[:, k * P:(k + 1) * P], a.ctx[:, t, k * P:(k + 1) * P],
                                          g.ident[:, :])
                    mm.then_inc(a.ctxT2_ready, 1)

                turn_o(0)
                for t in range(NT):
                    if t + 1 < NT:
                        turn_o(t + 1)
                    pe.wait_ge(a.oT_ready, t + 1)
                    if t >= 2:
                        pe.wait_ge(a.added, t - 1)
                    for k in range(KC):
                        mm = pe.matmul(g.bank(t % 2), a.oT[:, k, :], a.wd[:, k, :], start=(k == 0), stop=(k == KC - 1))
                    mm.then_inc(a.out_ready, 1)


            @block.vector
            def _(dve):
                ln_stats(dve, g, ln)
                ln_row(dve, g, ln, 0)
                ln_row(dve, g, ln, 1)
                dve.wait_ge(a.w_loaded, 96)
                def rotate(t):
                    b = 2 * (t % 2)
                    qk, rc = a.qks[:, t % 2, :, :], a.rcs[:, t % 2, :, :]
                    dve.wait_ge(a.qkv_ready, t + 1)
                    if t >= 2:
                        dve.wait_ge(a.rope_step, 4 * (t - 1))
                    dve.tensor_tensor(qk[:, 0:NH, :].rearrange("p h d -> p (h d)"), g.bank(b), a.bias[:, 0:H],
                                      ALU.add).then_inc(a.qkv_read, 1)
                    dve.tensor_tensor(qk[:, NH:NQK, :].rearrange("p h d -> p (h d)"), g.bank(b + 1)[:, 0:P],
                                      a.bias[:, H:H + P], ALU.add).then_inc(a.rope_step, 1)
                    dve.tensor_tensor(a.v[:, t, :, :].rearrange("p h d -> p (h d)"), g.bank(b + 1)[:, P:2 * P],
                                      a.bias[:, H + P:QKV], ALU.add).then_inc(a.qkv_read, 1)
                    dve.wait_ge(a.qkv_read, 2 * t + 2)
                    dve.wait_ge(a.rope_step, 4 * t + 1)
                    if t >= 2:
                        dve.wait_ge(a.split1, t - 1)
                        dve.wait_ge(a.rest1_ready, t - 1)
                    for n, (lo, hi) in enumerate(((0, NH), (NH, NQK))):
                        m = hi - lo
                        dve.tensor_tensor(rc[:, lo:hi, :], qk[:, lo:hi, :],
                                          a.cos[:, t, n:n + 1, :].to_broadcast([P, m, HD]), ALU.mult)
                        for c in range(2):
                            o = c * HD // 2
                            q = HD // 2 - o
                            mm = dve.tensor_tensor(a.rs[:, lo:hi, o:o + HD // 2], qk[:, lo:hi, q:q + HD // 2],
                                                   a.sin[:, t, n:n + 1, o:o + HD // 2].to_broadcast([P, m, HD // 2]),
                                                   ALU.mult)
                    mm.then_inc(a.rope_step, 2)
                    dve.wait_ge(a.rope_step, 4 * t + 3)
                    dve.tensor_tensor(rc, rc, a.rs[:, :, :], ALU.add).then_inc(a.rope_step, 1)

                def later_parts(t):
                    stack, rest1 = a.stacks[:, t % 2, :, :, :], a.rest1s[:, t % 2, :, :]
                    dve.wait_ge(a.rest1_ready, t + 1)
                    dve.tensor_copy(stack[:, 0:NH, 3:5, :],
                                    rest1[:, 0:NH, :].unsqueeze(2).to_broadcast([P, NH, 2, HD])).then_inc(a.rest2_ready, 1)
                    dve.tensor_copy(stack[:, NH:NQK, 2:5:2, :],
                                    rest1[:, NH:NQK, :].unsqueeze(2).to_broadcast([P, NKV, 2, HD])).then_inc(a.rest2_ready, 1)
                    dve.wait_ge(a.rest2_ready, 2 * t + 2)
                    dve.tensor_tensor(stack[:, 0:NH, 5, :], rest1[:, 0:NH, :], stack[:, 0:NH, 3, :],
                                      ALU.subtract).then_inc(a.stack_ready, 1)
                    dve.tensor_tensor(stack[:, NH:NQK, 0, :], rest1[:, NH:NQK, :], stack[:, NH:NQK, 2, :],
                                      ALU.subtract).then_inc(a.stack_ready, 1)

                for t in range(NT):
                    if t + 2 < NT:
                        ln_row(dve, g, ln, t + 2)
                    rotate(t)
                    if t >= 1:
                        later_parts(t - 1)
                later_parts(NT - 1)

                dve.sem_inc(a.ctx_ready, 1)
                dve.sem_inc(a.fill_read, 2)
                dve.wait_ge(a.vg_ready, 2)

                def lowest(kv, f):
                    qt, part, first, heads, w = FILLS[f]
                    if f in (0, NF0):
                        dve.wait_ge(a.parts_ready, kv * 2 + qt // BLK + 1)
                    dve.wait_ge(a.fill_ready, kv * NF + f + 1)
                    dve.tensor_reduce(a.least[:, part, qt, first:first + heads],
                                      g.bank(4 + f % 2)[:, 0:heads * w].rearrange("p (j k) -> p j k", j=heads),
                                      AX_X, ALU.min).then_inc(a.fill_read, 1)
                    if f == NF0 - 1:
                        dve.wait_ge(a.fill_read, kv * NF + f + 3)
                        dve.sem_inc(a.least_ready, 1)
                    if f == NF - 1:
                        dve.wait_ge(a.fill_read, kv * NF + f + 3)
                        dve.tensor_tensor(a.least[:, 0, BLK:NT, :], a.least[:, 0, BLK:NT, :], a.least[:, 1, BLK:NT, :],
                                          ALU.min).then_inc(a.least_ready, 1)

                def normalise(kv, c):
                    dve.wait_ge(a.ctx_turned, kv * 2 + c + 2)
                    v = g.bank(7).rearrange("p (t j d) -> p t j d", t=BLK, j=GH)
                    dve.reciprocal(a.rsum[:, :, :], v[:, :, :, HD]).then_inc(a.rsum_ready, 1)
                    dve.wait_ge(a.rsum_ready, kv * 2 + c + 1)
                    for t in range(BLK):
                        o = a.ctx[:, c * BLK + t, :].rearrange("p (g d) -> p g d", g=NKV)[:, bass.ds(kv, 1), :].squeeze(1)
                        mm = dve.tensor_tensor(o.rearrange("p (j d) -> p j d", j=GH), v[:, t, :, 0:HD],
                                               a.rsum[:, t, :].unsqueeze(2).to_broadcast([P, GH, HD]), ALU.mult)
                    mm.then_inc(a.ctx_ready, 1)

                def group(kv, ahead):
                    for s in PLAN16:
                        if s[0] == "fill" and ahead:
                            lowest(kv + 1, s[1])
                        elif s[0] == "values":
                            dve.wait_ge(a.pv_ready, kv * NG + 2)
                            dve.tensor_scalar(a.vg[:, :, 0:HD].unsqueeze(2), a.v[:, :, bass.ds(kv, 1), :], 1.0, None,
                                              ALU.mult).then_inc(a.vg_ready, 1)
                        elif s[0] == "turn":
                            normalise(kv, s[1])

                for f in range(NF):
                    lowest(0, f)
                with dve.Fori(0, NKV - 1) as kv:
                    group(kv, True)
                group(NKV - 1, False)
                for t in range(NT):
                    dve.wait_ge(a.out_ready, t + 1)
                    dve.wait_ge(a.biased, t + 1)
                    dve.tensor_tensor(g.x[:, t, :], g.bank(t % 2), g.x[:, t, :], ALU.add).then_inc(a.added, 1)



def lora_ffn(nc, g, d, name):
    with stage(nc, name) as (sb, sem):
        ln = Normalisation(sb, sem)
        xT = sb("xT", [P, KC, T])
        w = sb("w", [P, KC, H])
        ga = sb("ga", [P, KC, NE0 + ZR])
        bm = sb("bm", [P, H])
        ebias = sb("ebias", [P, NE0])
        number = sb("number", [P, ZR])
        logits = sb("logits", [P, NT, 8])
        top = sb("top", [P, NT, 8])
        at = sb("at", [P, NT, 8], U32)
        pick = sb("pick", [P, NT])
        z = sb("z", [P, 2, P])
        zT = sb("zT", [P, 2, P])
        loaded, b_loaded = sem("w_loaded"), sem("b_loaded")
        filled, b_filled, xT_ready = sem("filled"), sem("b_filled"), sem("xT_ready")
        gz_ready, pick_step, z_ready = sem("gz_ready"), sem("pick_step"), sem("z_ready")
        z_turned, zT_ready, out_ready, added = sem("z_turned"), sem("zT_ready"), sem("out_ready"), sem("added")

        with nc.Block() as block:
            @block.sync
            def _(sp):
                sp.dma_start(ga[:, :, :], d["L0f_ga"]).then_inc(loaded, 16)
                sp.dma_start(w[:, :, :], d["L0f_w"]).then_inc(loaded, 16)
                sp.dma_start(ebias[:, :], d["L0f_bias"].partition_broadcast(P)).then_inc(loaded, 16)
                sp.wait_ge(b_filled, 1)
                sp.dma_start(bm[0:ZR, :], d["L0f_b"]).then_inc(b_loaded, 16)

            @block.gpsimd
            def _(pool):
                pool.memset(bm[:, :], 0.0).then_inc(b_filled, 1)
                for e in range(NE0):
                    pool.memset(number[:, e * RANK:(e + 1) * RANK], float(e)).then_inc(filled, 1)
                pool.memset(z[:, :, :], 0.0).then_inc(filled, 1)
                pool.memset(logits[:, :, :], LOWEST).then_inc(filled, 1)

            @block.scalar
            def _(act):
                ln_root(act, ln)
                for t in range(NT + 2):
                    if t < NT:
                        act.wait_ge(ln.turned, t + 1)
                        act.activation(xT[:, :, t * P:(t + 1) * P], turned_row(g, t), ACT.Copy).then_inc(xT_ready, 1)
                    if t >= 2:
                        act.wait_ge(z_turned, t - 1)
                        if t >= 4:
                            act.wait_ge(out_ready, t - 3)
                        act.activation(zT[:, t % 2, :], g.bank(3)[:, 0:P], ACT.Copy).then_inc(zT_ready, 1)

            @block.tensor
            def _(pe):
                ln_turn(pe, g, ln, 0)
                pe.wait_ge(loaded, 48)
                for t in range(NT + 2):
                    if t + 1 < NT:
                        ln_turn(pe, g, ln, t + 1)
                    if t < NT:
                        pe.wait_ge(xT_ready, t + 1)
                        if t >= 2:
                            pe.wait_ge(z_ready, t - 1)
                        for k in range(KC):
                            mm = pe.matmul(g.bank(6 + t % 2)[:, 0:NE0 + ZR], xT[:, k, t * P:(t + 1) * P], ga[:, k, :],
                                           start=(k == 0), stop=(k == KC - 1))
                        mm.then_inc(gz_ready, 1)
                        if t >= 3:
                            pe.wait_ge(added, t - 2)
                        for k in range(KC):
                            pe.matmul(g.bank(t % 3), xT[:, k, t * P:(t + 1) * P], w[:, k, :],
                                      start=(k == 0), stop=False)
                    if t >= 2:
                        pe.wait_ge(zT_ready, t - 1)
                        pe.wait_ge(b_loaded, 16)
                        pe.matmul(g.bank((t - 2) % 3), zT[:, t % 2, :], bm[:, :], start=False, stop=True)\
                            .then_inc(out_ready, 1)
                    if 1 <= t <= NT:
                        pe.wait_ge(z_ready, t)
                        if t >= 2:
                            pe.wait_ge(zT_ready, t - 1)
                        pe.transpose(g.bank(3)[:, 0:P], z[:, (t - 1) % 2, :], g.ident[:, :]).then_inc(z_turned, 1)

            @block.vector
            def _(dve):
                ln_stats(dve, g, ln)
                ln_row(dve, g, ln, 0)
                ln_row(dve, g, ln, 1)
                dve.wait_ge(filled, NE0 + 2)
                dve.wait_ge(loaded, 48)
                for t in range(NT + 2):
                    if t + 2 < NT:
                        ln_row(dve, g, ln, t + 2)
                    if t < NT:
                        gz = g.bank(6 + t % 2)
                        dve.wait_ge(gz_ready, t + 1)
                        dve.tensor_tensor(logits[:, t, 0:NE0], gz[:, 0:NE0], ebias[:, :], ALU.add).then_inc(pick_step, 1)
                        dve.wait_ge(pick_step, 4 * t + 1)
                        dve.max(top[:, t, :], logits[:, t, :]).then_inc(pick_step, 1)
                        dve.wait_ge(pick_step, 4 * t + 2)
                        dve.max_index(at[:, t, :], top[:, t, :], logits[:, t, :]).then_inc(pick_step, 1)
                        dve.wait_ge(pick_step, 4 * t + 3)
                        dve.tensor_copy(pick[:, t:t + 1], at[:, t, 0:1]).then_inc(pick_step, 1)
                        dve.wait_ge(pick_step, 4 * t + 4)
                        if t >= 2:
                            dve.wait_ge(z_turned, t - 1)
                        dve.scalar_tensor_tensor(out=z[:, t % 2, 0:ZR], in0=number[:, :], scalar=pick[:, t:t + 1],
                                                 in1=gz[:, NE0:NE0 + ZR], op0=ALU.is_equal, op1=ALU.mult)\
                            .then_inc(z_ready, 1)
                    if t >= 2:
                        dve.wait_ge(out_ready, t - 1)
                        dve.tensor_tensor(g.x[:, t - 2, :], g.bank((t - 2) % 3), g.x[:, t - 2, :], ALU.add)\
                            .then_inc(added, 1)


def single_head(nc, g, d, name):
    with stage(nc, name) as (sb, sem):
        ln = Normalisation(sb, sem)
        xT = sb("xT", [P, KC, T])
        w = sb("w", [P, KC, 3 * D])
        wo = sb("wo", [P, H])
        bq = sb("bq", [P, 2])
        bqs = sb("bqs", [P, 1])
        bv = sb("bv", [P, D])
        bo = sb("bo", [P, H])
        qT, kT = sb("qT", [P, T]), sb("kT", [P, T])
        v = sb("v", [P, NT, D])
        probs, probsT = sb("probs", [P, 2, T]), sb("probsT", [P, 2, NT, P])
        least, rsum, rinv = sb("least", [P, NT]), sb("rsum", [P, NT]), sb("rinv", [P, NT])
        ctxT = sb("ctxT", [P, 2, P])
        loaded, xT_ready, bias_ready, biased = sem("loaded"), sem("xT_ready"), sem("bias_ready"), sem("biased")
        qk_ready, qk_copied = sem("qk_ready"), sem("qk_copied")
        v_ready, v_copied = sem("v_ready"), sem("v_copied")
        scores_ready, least_ready, probs_ready = sem("scores_ready"), sem("least_ready"), sem("probs_ready")
        turned, evac_dve, evac_act = sem("probs_turned"), sem("evac_dve"), sem("evac_act")
        pv_ready, ctxT_ready = sem("pv_ready"), sem("ctxT_ready")
        out_ready, rinv_ready, added = sem("out_ready"), sem("rinv_ready"), sem("added")

        with nc.Block() as block:
            @block.sync
            def _(sp):
                sp.dma_start(w[:, :, :], d["L0b_w"]).then_inc(loaded, 16)
                sp.dma_start(bq[:, :], d["L0b_bqk"]).then_inc(loaded, 16)
                sp.dma_start(bv[:, :], d["L0b_bv"].partition_broadcast(P)).then_inc(loaded, 16)
                sp.dma_start(wo[:, :], d["L0b_wo"]).then_inc(loaded, 16)
                sp.dma_start(bo[:, :], d["L0b_bo"].partition_broadcast(P)).then_inc(loaded, 16)

            @block.gpsimd
            def _(pool):
                output_bias(pool, g, ln, bo, loaded, 80, biased)

            @block.scalar
            def _(act):
                ln_root(act, ln)
                for t in range(NT):
                    act.wait_ge(ln.turned, t + 1)
                    act.activation(xT[:, :, t * P:(t + 1) * P], turned_row(g, t), ACT.Copy).then_inc(xT_ready, 1)
                act.wait_ge(bias_ready, 1)
                for h in range(2):
                    s = slice(h * HALF, (h + 1) * HALF)
                    act.wait_ge(qk_ready, 2 * h + 1)
                    act.activation(qT[:, s], g.bank(2 * h), ACT.Identity, bias=bqs[:, 0:1], scale=-SCALE)\
                        .then_inc(qk_copied, 1)
                    act.wait_ge(qk_ready, 2 * h + 2)
                    act.activation(kT[:, s], g.bank(2 * h + 1), ACT.Identity, bias=bq[:, 1:2]).then_inc(qk_copied, 1)

                def ctx_copy(qt):
                    act.wait_ge(pv_ready, qt + 1)
                    if qt >= 2:
                        act.wait_ge(out_ready, qt - 1)
                    act.activation(ctxT[:, qt % 2, :], g.bank(6)[:, 0:P], ACT.Copy).then_inc(ctxT_ready, 1)

                def exps(qt):
                    act.wait_ge(least_ready, qt + 1)
                    if qt >= 2:
                        act.wait_ge(turned, 2 * (qt - 1))
                    act.activation(probs[:, qt % 2, :], g.pair[qt % 2][:, :], ACT.Exp, bias=least[:, qt:qt + 1],
                                   scale=-1.0, accum_out=rsum[:, qt:qt + 1]).then_inc(probs_ready, 1)

                exps(0)
                for qt in range(NT):
                    if qt + 1 < NT:
                        exps(qt + 1)
                    act.wait_ge(turned, 2 * qt + 2)
                    if qt >= 2:
                        act.wait_ge(pv_ready, qt - 1)
                    act.activation(probsT[:, qt % 2, BLK:NT, :], g.bank(5).rearrange("p (k q) -> p k q", k=BLK),
                                   ACT.Copy).then_inc(evac_act, 1)
                    if qt >= 1:
                        ctx_copy(qt - 1)
                ctx_copy(NT - 1)

            @block.tensor
            def _(pe):
                pe.wait_ge(loaded, 80)
                for t in range(NT):
                    if t >= 2:
                        pe.wait_ge(xT_ready, t - 1)
                    ln_turn(pe, g, ln, t)
                for h in range(2):
                    pe.wait_ge(xT_ready, (h + 1) * BLK)
                    for c in range(2):
                        for k in range(KC):
                            mm = pe.matmul(g.bank(2 * h + c), w[:, k, c * D:(c + 1) * D],
                                           xT[:, k, h * HALF:(h + 1) * HALF], start=(k == 0), stop=(k == KC - 1))
                        mm.then_inc(qk_ready, 1)
                for t in range(NT):
                    if t >= 2:
                        pe.wait_ge(v_copied, t - 1)
                    for k in range(KC):
                        mm = pe.matmul(g.bank(6 + t % 2)[:, 0:D], xT[:, k, t * P:(t + 1) * P], w[:, k, 2 * D:3 * D],
                                       start=(k == 0), stop=(k == KC - 1))
                    mm.then_inc(v_ready, 1)

                def scores(qt):
                    pe.wait_ge(qk_copied, 4)
                    if qt >= 2:
                        pe.wait_ge(probs_ready, qt - 1)
                    for h in range(2):
                        mm = pe.matmul(g.pair[qt % 2][:, h * HALF:(h + 1) * HALF], qT[:, qt * P:(qt + 1) * P],
                                       kT[:, h * HALF:(h + 1) * HALF], start=True, stop=True)
                    mm.then_inc(scores_ready, 1)

                def weigh(qt):
                    pe.wait_ge(v_copied, NT)
                    pe.wait_ge(evac_dve, qt + 1)
                    pe.wait_ge(evac_act, qt + 1)
                    if qt >= 1:
                        pe.wait_ge(ctxT_ready, qt)
                    for kt in range(NT):
                        mm = pe.matmul(g.bank(6)[:, 0:P], v[:, kt, :], probsT[:, qt % 2, kt, :],
                                       start=(kt == 0), stop=(kt == NT - 1))
                    mm.then_inc(pv_ready, 1)

                def project(qt):
                    pe.wait_ge(ctxT_ready, qt + 1)
                    if qt >= 1:
                        pe.wait_ge(added, qt)
                    pe.matmul(g.bank(7), ctxT[:, qt % 2, :], wo[:, :], start=True, stop=True).then_inc(out_ready, 1)

                scores(0)
                scores(1)
                for qt in range(NT):
                    if qt + 2 < NT:
                        scores(qt + 2)
                    pe.wait_ge(probs_ready, qt + 1)
                    for b in range(2):
                        if qt >= 1:
                            pe.wait_ge((evac_dve, evac_act)[b], qt)
                        for i in range(BLK):
                            kt = BLK * b + i
                            mm = pe.transpose(g.bank(4 + b)[:, i * P:(i + 1) * P], probs[:, qt % 2, kt * P:(kt + 1) * P],
                                              g.ident[:, :])
                        mm.then_inc(turned, 1)
                    if qt >= 1:
                        weigh(qt - 1)
                    if qt >= 2:
                        project(qt - 2)
                weigh(NT - 1)
                project(NT - 2)
                project(NT - 1)

            @block.vector
            def _(dve):
                ln_stats(dve, g, ln)
                dve.wait_ge(loaded, 80)
                dve.tensor_scalar(bqs[:, :], bq[:, 0:1], -SCALE, None, ALU.mult).then_inc(bias_ready, 1)
                for t in range(NT):
                    ln_row(dve, g, ln, t)
                for t in range(NT):
                    dve.wait_ge(v_ready, t + 1)
                    dve.tensor_tensor(v[:, t, :], g.bank(6 + t % 2)[:, 0:D], bv[:, :], ALU.add).then_inc(v_copied, 1)

                def low(qt):
                    dve.wait_ge(scores_ready, qt + 1)
                    dve.tensor_reduce(least[:, qt:qt + 1], g.pair[qt % 2][:, :], AX_X, ALU.min).then_inc(least_ready, 1)

                def add(qt):
                    dve.wait_ge(probs_ready, qt + 1)
                    dve.reciprocal(rinv[:, qt:qt + 1], rsum[:, qt:qt + 1]).then_inc(rinv_ready, 1)
                    dve.wait_ge(rinv_ready, qt + 1)
                    dve.wait_ge(out_ready, qt + 1)
                    dve.wait_ge(biased, qt + 1)
                    dve.scalar_tensor_tensor(out=g.x[:, qt, :], in0=g.bank(7), scalar=rinv[:, qt:qt + 1],
                                             in1=g.x[:, qt, :], op0=ALU.mult, op1=ALU.add).then_inc(added, 1)

                low(0)
                low(1)
                for qt in range(NT):
                    if qt + 2 < NT:
                        low(qt + 2)
                    dve.wait_ge(turned, 2 * qt + 1)
                    if qt >= 2:
                        dve.wait_ge(pv_ready, qt - 1)
                    dve.tensor_copy(probsT[:, qt % 2, 0:BLK, :], g.bank(4).rearrange("p (k q) -> p k q", k=BLK))\
                        .then_inc(evac_dve, 1)
                    if qt >= 2:
                        add(qt - 2)
                add(NT - 2)
                add(NT - 1)


def turned_rows_high(act, g, ln, xh, ready):
    for t in range(NT):
        act.wait_ge(ln.turned, t + 1)
        act.activation(xh[:, :, t * P:(t + 1) * P], turned_row(g, t), ACT.Copy).then_inc(ready, 1)


def turned_rows_low(dve, g, t, xh, xl, ready, split):
    dve.wait_ge(ready, t + 1)
    s = slice(t * P, (t + 1) * P)
    dve.tensor_tensor(xl[:, :, s], turned_row(g, t), xh[:, :, s].bitcast(F32), ALU.subtract).then_inc(split, 1)


def product(pe, out, wh, wl, xh, xl, start, stop):
    pe.matmul(out, wh, xh, start=start, stop=False)
    pe.matmul(out, wh, xl, start=False, stop=False)
    return pe.matmul(out, wl, xh, start=False, stop=stop)


K_, V_, Q_, O_ = 0, 1, 2, 2 + GH
PIECES = 2 + 2 * GH
SPLIT_ORDER = [K_, Q_, V_, Q_ + 1, O_, Q_ + 2, O_ + 1, Q_ + 3, O_ + 2, O_ + 3]
SLOTS_RAW = PIECES // 2
UNITS = GH * NT
BANKS_G = GH * BANKS_BEFORE[NT]


def group_plan():
    plan = [("proj", K_, 0), ("proj", Q_, 0), ("proj", V_, 0), ("proj", K_, 1), ("begin",), ("proj", Q_, 1)]
    for j in range(GH):
        if j == 0:
            between = [[("turn_v", 0)], [("proj", V_, 1)], [("turn_v", 1)], [("proj", Q_ + 1, 0)],
                       [("weigh", 0, 0), ("proj", Q_ + 1, 1)]]
        else:
            more = [("proj", Q_ + j + 1, h) for h in range(2)] if j + 1 < GH else [None, None]
            between = [[], [("weigh", j - 1, 1), more[0]], [("out", j - 1, 4), ("out", j - 1, 5)], [("out", j - 1, 6), ("out", j - 1, 7)], [("weigh", j, 0), more[1]]]
        between += [[], [("out", j, 0), ("out", j, 1)], [("out", j, 2), ("out", j, 3)]]
        for qt in range(NT):
            plan += [("unit", j, qt)] + [s for s in between[qt] if s]
    plan.append(("weigh", GH - 1, 1))
    return plan + [("out", GH - 1, t) for t in range(BLK, NT)]


PLAN = group_plan()


def numbered(*kinds):
    return {s: n for n, s in enumerate(s for s in PLAN if s[0] in kinds)}


AUX = numbered("proj", "turn_v", "out")
IN_BANK = numbered("proj", "turn_v", "out", "weigh")
ORDER = list(IN_BANK)
NAUX = len(AUX)
OF_KIND = {k: numbered(k) for k in ("proj", "turn_v", "out", "weigh")}
ROPE = {s: n for n, s in enumerate(s for s in PLAN if s[0] == "proj" and s[1] != V_)}
NROPE = len(ROPE)
NPROJ = len(OF_KIND["proj"])


def aux_bank(s):
    return 6 + IN_BANK[s] % 2


def rotated_before(j, qt):
    need = [("proj", K_, h) for h in range(qt // BLK + 1)] + [("proj", Q_ + j, h) for h in range(qt // BLK + 1)]
    return max(ROPE[s] for s in need) + 1


def turned_of_group(u):
    if u < 0:
        return -banks_of(NT - 1)
    j, qt = divmod(u, NT)
    return j * BANKS_BEFORE[NT] + BANKS_BEFORE[qt]


def attention128(nc, g, d, name):
    with stage(nc, name) as (sb, sem):
        ln = Normalisation(sb, sem)
        xh, xl = sb("xh", [P, KC, T], F32R), sb("xl", [P, KC, T], F32R)
        raw = sb("raw", [P, SLOTS_RAW, H])
        wh, wl = sb("wh", [P, PIECES, H], F32R), sb("wl", [P, PIECES, H], F32R)
        cos, sin = sb("cos", [P, T]), sb("sin", [P, T])
        bias = sb("bias", [P, 2 + GH, NKV])
        own_bias = sb("own_bias", [P, 2 + GH])
        bo = sb("bo", [P, H])
        lin, swapped = sb("lin", [P, 2, HALF]), sb("swapped", [P, 2, HALF])
        by_cos, by_sin, rot = sb("by_cos", [P, HALF]), sb("by_sin", [P, HALF]), sb("rot", [P, HALF])
        kh, kl = sb("kh", [P, T], F32R), sb("kl", [P, T], F32R)
        qh, ql = sb("qh", [P, 2, T], F32R), sb("ql", [P, 2, T], F32R)
        vT = sb("vT", [P, HALF])
        vh, vl = sb("vh", [P, NT, D], F32R), sb("vl", [P, NT, D], F32R)
        probs = sb("probs", [P, 2, T])
        ph, pl = sb("ph", [P, NT, HALF], F32R), sb("pl", [P, NT, HALF], F32R)
        ch, cl = sb("ch", [P, HALF], F32R), sb("cl", [P, HALF], F32R)
        least = sb("least", [P, 4])
        rsum, rinv = sb("rsum", [P, 2, NT]), sb("rinv", [P, 2, NT])

        loaded, biased, scaled = sem("loaded"), sem("biased"), sem("scaled")
        own_bias_ready = sem("own_bias_ready")
        x_high, x_split = sem("x_high"), sem("x_split")
        raw_loaded = [sem(f"raw_loaded{i}") for i in range(SLOTS_RAW)]
        w_high, w_split = sem("w_high"), sem("w_split")
        aux_ready = sem("aux_ready")
        proj_read, v_split, added = sem("proj_read"), sem("v_split"), sem("added")
        by_cos_ready, by_sin_ready, summed = sem("by_cos_ready"), sem("by_sin_ready"), sem("summed")
        rot_high, rotated, v_high = sem("rot_high"), sem("rotated"), sem("v_high")
        scores_ready, least_ready, probs_ready = sem("scores_ready"), sem("least_ready"), sem("probs_ready")
        turned, p_high, p_split = sem("probs_turned"), sem("p_high"), sem("p_split")
        pv_ready, c_high, c_split, rinv_ready = sem("pv_ready"), sem("c_high"), sem("c_split"), sem("rinv_ready")

        with nc.Block() as block:
            @block.sync
            def _(sp):
                sp.dma_start(bias[:, :, :], d["L1a_bias"]).then_inc(loaded, 16)
                sp.dma_start(cos[:, :], d["cos128"]).then_inc(loaded, 16)
                sp.dma_start(sin[:, :], d["sin128"]).then_inc(loaded, 16)
                sp.dma_start(bo[:, :], d["L1a_bo"].partition_broadcast(P)).then_inc(loaded, 16)
                with sp.Fori(0, NKV) as kv:
                    for pos in range(PIECES):
                        sp.wait_ge(w_split, kv * PIECES + pos + 1)
                        sp.dma_start(raw[:, pos % SLOTS_RAW, :], d["L1a_w"][bass.ds(kv * PIECES + pos, 1), :, :].squeeze(0))\
                            .then_inc(raw_loaded[pos % SLOTS_RAW], 16)

            @block.gpsimd
            def _(pool):
                output_bias(pool, g, ln, bo, loaded, 64, biased)
                pool.sem_inc(w_split, SLOTS_RAW)
                pool.sem_inc(rotated, 2)
                with pool.Fori(0, NKV) as kv:
                    def split(pos):
                        piece = SPLIT_ORDER[pos]
                        if piece >= O_:
                            last = AUX["out", piece - O_, NT - 1]
                        else:
                            last = AUX["proj", piece, 1]
                        pool.wait_ge(raw_loaded[pos % SLOTS_RAW], kv * 32 + 16 * (pos // SLOTS_RAW) + 16)
                        pool.wait_ge(aux_ready, kv * NAUX + last + 1)
                        r = raw[:, pos % SLOTS_RAW, :]
                        pool.tensor_tensor(wh[:, piece, :], r, g.ones[:, :], ALU.mult).then_inc(w_high, 1)
                        pool.wait_ge(w_high, kv * PIECES + pos + 1)
                        pool.tensor_tensor(wl[:, piece, :], raw[:, pos % SLOTS_RAW, :], wh[:, piece, :].bitcast(F32),
                                           ALU.subtract).then_inc(w_split, 1)

                    def rotate(s):
                        _, piece, h = s
                        r, cols = ROPE[s], slice(h * HALF, (h + 1) * HALF)
                        pool.wait_ge(proj_read, (kv + 1) * NPROJ + OF_KIND["proj"][s] + 1)
                        pool.wait_ge(summed, kv * NROPE + r + 1)
                        pool.tensor_tensor(by_sin[:, :], swapped[:, r % 2, :], sin[:, cols], ALU.mult)\
                            .then_inc(by_sin_ready, 1)
                        to = kl[:, cols] if piece == K_ else ql[:, (piece - Q_) % 2, cols]
                        high = kh[:, cols] if piece == K_ else qh[:, (piece - Q_) % 2, cols]
                        pool.wait_ge(rot_high, kv * NROPE + r + 1)
                        pool.tensor_tensor(to, rot[:, :], high.bitcast(F32), ALU.subtract).then_inc(rotated, 1)

                    for pos in range(SLOTS_RAW):
                        split(pos)
                    for s, r in ROPE.items():
                        rotate(s)
                        if 3 <= r < 3 + SLOTS_RAW:
                            split(SLOTS_RAW + r - 3)

            @block.scalar
            def _(act):
                ln_root(act, ln)
                turned_rows_high(act, g, ln, xh, x_high)
                act.sem_inc(probs_ready, 2)
                act.sem_inc(proj_read, NPROJ)
                with act.Fori(0, NKV) as kv:
                    def exps(u):
                        j, qt = divmod(u, NT)
                        n = (qt + 1) * P
                        act.wait_ge(least_ready, kv * UNITS + u + 1)
                        act.wait_ge(turned, kv * BANKS_G + turned_of_group(u - 1) + 3)
                        act.activation(probs[:, u % 2, 0:n], g.pair[u % 2][:, 0:n], ACT.Exp,
                                       bias=least[:, u % 4:u % 4 + 1], scale=-1.0,
                                       accum_out=rsum[:, j % 2, qt:qt + 1]).then_inc(probs_ready, 1)

                    act.wait_ge(own_bias_ready, kv + 1)
                    for s in PLAN:
                        if s[0] == "proj":
                            piece, n = s[1], AUX[s]
                            act.wait_ge(aux_ready, (kv + 1) * NAUX + n + 1)
                            if piece == V_:
                                act.wait_ge(aux_ready, kv * NAUX + (AUX["turn_v", 1] + 1 if s[2] == 0 else
                                                                    NAUX + AUX["turn_v", 0] + 1))
                                act.activation(vT[:, :], g.bank(aux_bank(s)), ACT.Identity, bias=own_bias[:, 1:2])\
                                    .then_inc(proj_read, 1)
                                continue
                            r = ROPE[s]
                            act.wait_ge(rotated, kv * NROPE + r + 1)
                            b = own_bias[:, piece:piece + 1]
                            f = 1.0 if piece == K_ else -SCALE
                            act.activation(lin[:, r % 2, :], g.bank(aux_bank(s)), ACT.Identity, bias=b, scale=f)
                            for o in (0, P // 2):
                                q = P // 2 - o
                                mm = act.activation(swapped[o:o + P // 2, r % 2, :], g.bank(aux_bank(s))[q:q + P // 2, :],
                                                    ACT.Identity, bias=b[q:q + P // 2, :], scale=f)
                            mm.then_inc(proj_read, 1)
                        elif s[0] == "turn_v":
                            act.wait_ge(aux_ready, (kv + 1) * NAUX + AUX[s] + 1)
                            act.activation(vh[:, s[1] * BLK:(s[1] + 1) * BLK, :],
                                           g.bank(aux_bank(s)).rearrange("p (k e) -> p k e", k=BLK),
                                           ACT.Copy).then_inc(v_high, 1)
                        elif s[0] == "begin":
                            exps(0)
                        elif s[0] == "unit":
                            _, j, qt = s
                            u = j * NT + qt
                            if u + 1 < UNITS:
                                exps(u + 1)
                            for h in range(banks_of(qt)):
                                b = turned_of_group(u) + h
                                k = min(BLK, qt + 1 - BLK * h)
                                act.wait_ge(turned, kv * BANKS_G + b + 4)
                                act.wait_ge(pv_ready, kv * 2 * GH + 2 * j + qt // BLK + 1)
                                act.activation(ph[:, BLK * h:BLK * h + k, (qt % BLK) * P:(qt % BLK + 1) * P],
                                               g.bank(4 + b % 2)[:, 0:k * P].rearrange("p (k q) -> p k q", k=k),
                                               ACT.Copy).then_inc(p_high, 1)
                        elif s[0] == "weigh":
                            _, j, c = s
                            q = 2 * j + c
                            act.wait_ge(pv_ready, kv * 2 * GH + q + 2)
                            last = ("out", j, BLK - 1) if c else ("out", (j - 1) % GH, NT - 1)
                            act.wait_ge(aux_ready, kv * NAUX + AUX[last] + 1 + (NAUX if q else 0))
                            act.activation(ch[:, :], g.bank(aux_bank(s)), ACT.Copy).then_inc(c_high, 1)

            @block.tensor
            def _(pe):
                for t in range(NT):
                    if t >= 2:
                        pe.wait_ge(x_split, t - 1)
                    ln_turn(pe, g, ln, t)
                pe.wait_ge(x_split, NT)
                pe.sem_inc(turned, 3)
                pe.sem_inc(pv_ready, 1)
                pe.sem_inc(aux_ready, NAUX)
                with pe.Fori(0, NKV) as kv:
                    def scores(u):
                        j, qt = divmod(u, NT)
                        n = (qt + 1) * P
                        pe.wait_ge(rotated, kv * NROPE + rotated_before(j, qt) + 2)
                        pe.wait_ge(probs_ready, kv * UNITS + u + 1)
                        rows = slice(qt * P, (qt + 1) * P)
                        for c in range(0, n, HALF):
                            w = min(HALF, n - c)
                            product(pe, g.pair[u % 2][:, c:c + w], qh[:, j % 2, rows], ql[:, j % 2, rows],
                                    kh[:, c:c + w], kl[:, c:c + w], True, c + w < n)
                        pe.matmul(g.pair[u % 2][:, n - P:n], g.ident_b[:, :], g.mask_b[:, :], start=False, stop=True)\
                            .then_inc(scores_ready, 1)

                    for s in PLAN:
                        if s in IN_BANK:
                            n = IN_BANK[s] - 2
                            before = ORDER[n]
                            pe.wait_ge({"proj": proj_read, "turn_v": v_split, "out": added, "weigh": c_split}[before[0]],
                                       (kv + (n >= 0)) * len(OF_KIND[before[0]]) + OF_KIND[before[0]][before] + 1)
                        if s[0] == "proj":
                            _, piece, h = s
                            pe.wait_ge(w_split, kv * PIECES + SPLIT_ORDER.index(piece) + 1 + SLOTS_RAW)
                            for k in range(KC):
                                c, r = slice(k * P, (k + 1) * P), slice(h * HALF, (h + 1) * HALF)
                                mm = product(pe, g.bank(aux_bank(s)), wh[:, piece, c], wl[:, piece, c], xh[:, k, r], xl[:, k, r],
                                             k == 0, k == KC - 1)
                            mm.then_inc(aux_ready, 1)
                        elif s[0] == "turn_v":
                            pe.wait_ge(proj_read, (kv + 1) * NPROJ + OF_KIND["proj"]["proj", V_, s[1]] + 1)
                            for i in range(BLK):
                                mm = pe.transpose(g.bank(aux_bank(s))[:, i * P:(i + 1) * P], vT[:, i * P:(i + 1) * P], g.ident[:, :])
                            mm.then_inc(aux_ready, 1)
                        elif s[0] == "begin":
                            scores(0)
                            scores(1)
                        elif s[0] == "unit":
                            _, j, qt = s
                            u = j * NT + qt
                            if u + 2 < UNITS:
                                scores(u + 2)
                            pe.wait_ge(probs_ready, kv * UNITS + u + 3)
                            for h in range(banks_of(qt)):
                                b = turned_of_group(u) + h
                                pe.wait_ge(p_split, kv * BANKS_G + b + 1)
                                for i in range(min(BLK, qt + 1 - BLK * h)):
                                    kt = BLK * h + i
                                    mm = pe.transpose(g.bank(4 + b % 2)[:, i * P:(i + 1) * P],
                                                      probs[:, u % 2, kt * P:(kt + 1) * P], g.ident[:, :])
                                mm.then_inc(turned, 1)
                        elif s[0] == "weigh":
                            _, j, c = s
                            q = 2 * j + c
                            pe.wait_ge(p_split, kv * BANKS_G + j * BANKS_BEFORE[NT] + BANKS_BEFORE[BLK * (c + 1)] + 2)
                            pe.wait_ge(v_split, (kv + 1) * 2 + 2)
                            for kt in range(BLK * (c + 1)):
                                o = max(0, kt - BLK * c) * P
                                mm = product(pe, g.bank(aux_bank(s))[:, o:HALF], vh[:, kt, :], vl[:, kt, :],
                                             ph[:, kt, o:HALF], pl[:, kt, o:HALF], kt == 0, kt == BLK * (c + 1) - 1)
                            mm.then_inc(pv_ready, 1)
                        else:
                            _, j, t = s
                            pe.wait_ge(c_split, (kv + 1) * 2 * GH + 2 * j + t // BLK + 1)
                            pe.wait_ge(w_split, kv * PIECES + SPLIT_ORDER.index(O_ + j) + 1 + SLOTS_RAW)
                            c = slice((t % BLK) * P, (t % BLK + 1) * P)
                            product(pe, g.bank(aux_bank(s)), ch[:, c], cl[:, c], wh[:, O_ + j, :], wl[:, O_ + j, :], True, True)\
                                .then_inc(aux_ready, 1)

            @block.vector
            def _(dve):
                ln_stats(dve, g, ln)
                ln_row(dve, g, ln, 0)
                ln_row(dve, g, ln, 1)
                for t in range(NT):
                    if t + 2 < NT:
                        ln_row(dve, g, ln, t + 2)
                    turned_rows_low(dve, g, t, xh, xl, x_high, x_split)
                dve.wait_ge(loaded, 64)
                dve.tensor_scalar(bias[:, 2:2 + GH, :], bias[:, 2:2 + GH, :], -SCALE, None, ALU.mult).then_inc(scaled, 1)
                dve.wait_ge(biased, NT)
                dve.sem_inc(added, GH * NT)
                dve.sem_inc(v_split, 2)
                dve.sem_inc(summed, 1)
                dve.sem_inc(p_split, 2)
                dve.sem_inc(c_split, 2 * GH)
                dve.wait_ge(scaled, 1)
                with dve.Fori(0, NKV) as kv:
                    dve.wait_ge(proj_read, (kv + 1) * NPROJ)
                    dve.tensor_scalar(own_bias[:, :].unsqueeze(2), bias[:, :, bass.ds(kv, 1)], 1.0, None, ALU.mult)\
                        .then_inc(own_bias_ready, 1)

                    def low(u):
                        n = (u % NT + 1) * P
                        dve.wait_ge(scores_ready, kv * UNITS + u + 1)
                        dve.tensor_reduce(least[:, u % 4:u % 4 + 1], g.pair[u % 2][:, 0:n], AX_X, ALU.min)\
                            .then_inc(least_ready, 1)

                    def rotate(s):
                        _, piece, h = s
                        r, cols = ROPE[s], slice(h * HALF, (h + 1) * HALF)
                        dve.wait_ge(proj_read, (kv + 1) * NPROJ + OF_KIND["proj"][s] + 1)
                        dve.tensor_tensor(by_cos[:, :], lin[:, r % 2, :], cos[:, cols], ALU.mult).then_inc(by_cos_ready, 1)
                        dve.wait_ge(by_cos_ready, kv * NROPE + r + 1)
                        dve.wait_ge(by_sin_ready, kv * NROPE + r + 1)
                        dve.wait_ge(rotated, kv * NROPE + r + 2)
                        dve.tensor_tensor(rot[:, :], by_cos[:, :], by_sin[:, :], ALU.add).then_inc(summed, 1)
                        dve.wait_ge(summed, kv * NROPE + r + 2)
                        high = kh[:, cols] if piece == K_ else qh[:, (piece - Q_) % 2, cols]
                        dve.tensor_copy(high, rot[:, :]).then_inc(rot_high, 1)

                    started, projected = False, []
                    for s in PLAN:
                        if s in ROPE:
                            if started:
                                projected.append(s)
                            else:
                                rotate(s)
                        elif s[0] == "turn_v":
                            k = slice(s[1] * BLK, (s[1] + 1) * BLK)
                            dve.wait_ge(v_high, kv * 2 + s[1] + 1)
                            dve.tensor_tensor(vl[:, k, :], g.bank(aux_bank(s)).rearrange("p (k e) -> p k e", k=BLK),
                                              vh[:, k, :].bitcast(F32), ALU.subtract).then_inc(v_split, 1)
                        elif s[0] == "begin":
                            low(0)
                            low(1)
                        elif s[0] == "unit":
                            _, j, qt = s
                            u = j * NT + qt
                            if u + 2 < UNITS:
                                low(u + 2)
                            for h in range(banks_of(qt)):
                                b = turned_of_group(u) + h
                                k = min(BLK, qt + 1 - BLK * h)
                                to = (slice(None), slice(BLK * h, BLK * h + k), slice((qt % BLK) * P, (qt % BLK + 1) * P))
                                dve.wait_ge(p_high, kv * BANKS_G + b + 1)
                                dve.tensor_tensor(pl[to], g.bank(4 + b % 2)[:, 0:k * P].rearrange("p (k q) -> p k q", k=k),
                                                  ph[to].bitcast(F32), ALU.subtract).then_inc(p_split, 1)
                            for p in projected:
                                rotate(p)
                            started, projected = True, []
                        elif s[0] == "weigh":
                            _, j, c = s
                            q = 2 * j + c
                            tiles = slice(c * BLK, (c + 1) * BLK)
                            dve.wait_ge(probs_ready, kv * UNITS + j * NT + (c + 1) * BLK + 2)
                            dve.reciprocal(rinv[:, j % 2, tiles], rsum[:, j % 2, tiles]).then_inc(rinv_ready, 1)
                            dve.wait_ge(c_high, kv * 2 * GH + q + 1)
                            dve.tensor_tensor(cl[:, :], g.bank(aux_bank(s)), ch[:, :].bitcast(F32), ALU.subtract).then_inc(c_split, 1)
                        elif s[0] == "out":
                            _, j, t = s
                            dve.wait_ge(rinv_ready, kv * 2 * GH + 2 * j + t // BLK + 1)
                            dve.wait_ge(aux_ready, (kv + 1) * NAUX + AUX[s] + 1)
                            dve.scalar_tensor_tensor(out=g.x[:, t, :], in0=g.bank(aux_bank(s)), scalar=rinv[:, j % 2, t:t + 1],
                                                     in1=g.x[:, t, :], op0=ALU.mult, op1=ALU.add).then_inc(added, 1)


GU = KC
WP = GU + IC
ITEMS = 2 * IC


def routed_ffn(nc, g, d, name):
    with stage(nc, name) as (sb, sem):
        ln = Normalisation(sb, sem)
        xh, xl = sb("xh", [P, KC, T], F32R), sb("xl", [P, KC, T], F32R)
        gw = sb("gw", [P, KC, NE])
        gwh, gwl = sb("gwh", [P, KC, NE], F32R), sb("gwl", [P, KC, NE], F32R)
        gb = sb("gb", [P, NE])
        number = sb("number", [P, NE])
        sigT = sb("sigT", [NE, T])
        score, top = sb("score", [P, NT, NE]), sb("top", [P, NT, 8])
        at, at_f = sb("at", [P, NT, 8], U32), sb("at_f", [P, NT, 8])
        wsum, winv = sb("wsum", [P, NT]), sb("winv", [P, NT])
        tw = sb("tw", [P, NT, TOPK])
        hit, cw = sb("hit", [P, NT, NE]), sb("cw", [P, NT, NE])
        cwe = sb("cwe", [P, 2, NT])
        raw = sb("raw", [P, WP, H])
        wh, wl = sb("wh", [P, 2, WP, H], F32R), sb("wl", [P, 2, WP, H], F32R)
        gate = sb("gate", [P, 2, HALF])
        z = sb("z", [P, 2, HALF])
        zh, zl = sb("zh", [P, IC, T], F32R), sb("zl", [P, IC, T], F32R)

        loaded, filled, gw_high, gw_split = sem("loaded"), sem("filled"), sem("gw_high"), sem("gw_split")
        x_high, x_split = sem("x_high"), sem("x_split")
        logits_ready, score_ready, score_turned = sem("logits_ready"), sem("score_ready"), sem("score_turned")
        pick_step, cwe_ready = sem("pick_step"), sem("cwe_ready")
        raw_loaded = [sem(f"raw_loaded{i}") for i in range(WP)]
        w_high, w_split = sem("w_high"), sem("w_split")
        items_ready, gate_ready, z_ready = sem("items_ready"), sem("gate_ready"), sem("z_ready")
        z_high, z_split, out_ready, added = sem("z_high"), sem("z_split"), sem("out_ready"), sem("added")

        with nc.Block() as block:
            @block.sync
            def _(sp):
                sp.dma_start(gw[:, :, :], d["L1f_gate"]).then_inc(loaded, 16)
                sp.dma_start(gb[:, :], d["L1f_bias"].partition_broadcast(P)).then_inc(loaded, 16)

                def load(e):
                    for p in range(WP):
                        sp.wait_ge(w_split, e * WP + p + 1)
                        src = d["L1f_w"][e * WP + p] if isinstance(e, int) else \
                            d["L1f_w"][bass.ds(e * WP + p, 1), :, :].squeeze(0)
                        sp.dma_start(raw[:, p, :], src).then_inc(raw_loaded[p], 16)

                with sp.Fori(0, NE) as e:
                    load(e)
                load(NE)

            @block.gpsimd
            def _(pool):
                for e in range(NE):
                    pool.memset(number[:, e:e + 1], float(e)).then_inc(filled, 1)
                pool.sem_inc(w_split, WP)
                pool.sem_inc(z_split, 2)

                def split(e, par, p):
                    pool.wait_ge(raw_loaded[p], e * 16 + 16)
                    if not isinstance(e, int) or e:
                        if p < GU:
                            pool.wait_ge(items_ready, e * ITEMS)
                        else:
                            pool.wait_ge(out_ready, e * NT)
                    pool.tensor_tensor(wh[:, par, p, :], raw[:, p, :], g.ones[:, :], ALU.mult).then_inc(w_high, 1)
                    pool.wait_ge(w_high, e * WP + p + 1)
                    pool.tensor_tensor(wl[:, par, p, :], raw[:, p, :], wh[:, par, p, :].bitcast(F32), ALU.subtract)\
                        .then_inc(w_split, 1)

                def z_low(e, m):
                    c, h = m % IC, m // IC
                    s = slice(h * HALF, (h + 1) * HALF)
                    pool.wait_ge(z_high, e * ITEMS + m + 1)
                    pool.tensor_tensor(zl[:, c, s], z[:, m % 2, :], zh[:, c, s].bitcast(F32), ALU.subtract)\
                        .then_inc(z_split, 1)

                for p in range(WP):
                    split(0, 0, p)

                def expert(e, par, following):
                    for m in range(ITEMS):
                        z_low(e, m)
                        if following:
                            for p in ((0,), (1, 2), (3,), (4, 5))[m]:
                                split(e + 1, 1 - par, p)

                with pool.Fori(0, NE // 2) as pair:
                    for par in range(2):
                        expert(2 * pair + par, par, True)
                expert(NE, 0, False)

            @block.scalar
            def _(act):
                ln_root(act, ln)
                turned_rows_high(act, g, ln, xh, x_high)
                for h in range(2):
                    act.wait_ge(logits_ready, h + 1)
                    act.activation(sigT[:, h * HALF:(h + 1) * HALF], g.bank(6 + h)[0:NE, :], ACT.Sigmoid)\
                        .then_inc(score_ready, 1)

                def expert(e, par):
                    for m in range(ITEMS):
                        c, h = m % IC, m // IC
                        act.wait_ge(items_ready, e * ITEMS + m + 1 + ITEMS)
                        act.wait_ge(z_ready, e * ITEMS + m + 1)
                        act.activation(gate[:, m % 2, :], g.pair[m % 2][:, 0:HALF], ACT.Silu).then_inc(gate_ready, 1)
                        act.wait_ge(z_ready, e * ITEMS + m + 3)
                        act.activation(zh[:, c, h * HALF:(h + 1) * HALF], z[:, m % 2, :], ACT.Copy).then_inc(z_high, 1)

                with act.Fori(0, NE // 2) as pair:
                    for par in range(2):
                        expert(2 * pair + par, par)
                expert(NE, 0)

            @block.tensor
            def _(pe):
                for t in range(NT):
                    if t >= 2:
                        pe.wait_ge(x_split, t - 1)
                    ln_turn(pe, g, ln, t)
                pe.wait_ge(gw_split, 1)
                for h in range(2):
                    pe.wait_ge(x_split, (h + 1) * BLK)
                    for k in range(KC):
                        s = slice(h * HALF, (h + 1) * HALF)
                        mm = product(pe, g.bank(6 + h)[0:NE, :], gwh[:, k, :], gwl[:, k, :], xh[:, k, s], xl[:, k, s],
                                     k == 0, k == KC - 1)
                    mm.then_inc(logits_ready, 1)
                for t in range(NT):
                    if t % BLK == 0:
                        pe.wait_ge(score_ready, t // BLK + 1)
                    mm = pe.transpose(g.bank(4)[:, t * NE:(t + 1) * NE], sigT[:, t * P:(t + 1) * P], g.ident[0:NE, 0:NE])
                mm.then_inc(score_turned, 1)
                pe.sem_inc(items_ready, ITEMS)
                pe.sem_inc(out_ready, NT)

                def expert(e, par):
                    pe.wait_ge(w_split, e * WP + GU + WP)
                    for m in range(ITEMS):
                        c, h = m % IC, m // IC
                        pe.wait_ge(z_ready, e * ITEMS + m + 1)
                        for u in range(2):
                            cols = slice(u * INNER + c * P, u * INNER + (c + 1) * P)
                            toks = slice(h * HALF, (h + 1) * HALF)
                            for k in range(KC):
                                mm = product(pe, g.pair[m % 2][:, u * HALF:(u + 1) * HALF], wh[:, par, k, cols],
                                             wl[:, par, k, cols], xh[:, k, toks], xl[:, k, toks], k == 0, k == KC - 1)
                        mm.then_inc(items_ready, 1)
                    pe.wait_ge(w_split, e * WP + WP + WP)
                    for t in range(NT):
                        if t % BLK == 0:
                            pe.wait_ge(z_split, e * ITEMS + IC * (t // BLK + 1) + 2)
                        pe.wait_ge(added, e * NT + t + 1)
                        s = slice(t * P, (t + 1) * P)
                        for c in range(IC):
                            mm = product(pe, g.bank(4 + t % 4), zh[:, c, s], zl[:, c, s], wh[:, par, GU + c, :],
                                         wl[:, par, GU + c, :], c == 0, c == IC - 1)
                        mm.then_inc(out_ready, 1)

                with pe.Fori(0, NE // 2) as pair:
                    for par in range(2):
                        expert(2 * pair + par, par)
                expert(NE, 0)

            @block.vector
            def _(dve):
                ln_stats(dve, g, ln)
                ln_row(dve, g, ln, 0)
                ln_row(dve, g, ln, 1)
                dve.wait_ge(loaded, 32)
                dve.tensor_copy(gwh[:, :, :], gw[:, :, :]).then_inc(gw_high, 1)
                dve.wait_ge(gw_high, 1)
                dve.tensor_tensor(gwl[:, :, :], gw[:, :, :], gwh[:, :, :].bitcast(F32), ALU.subtract).then_inc(gw_split, 1)
                for t in range(NT):
                    if t + 2 < NT:
                        ln_row(dve, g, ln, t + 2)
                    turned_rows_low(dve, g, t, xh, xl, x_high, x_split)

                dve.sem_inc(z_ready, 2)

                step = [0]

                def then(i):
                    i.then_inc(pick_step, 1)
                    step[0] += 1
                    dve.wait_ge(pick_step, step[0])

                def along(v, shape):
                    return v.to_broadcast([P] + shape)

                dve.wait_ge(filled, NE)
                dve.wait_ge(score_turned, 1)
                then(dve.tensor_tensor(score[:, :, :], g.bank(4)[:, 0:NT * NE].rearrange("p (t e) -> p t e", t=NT), along(gb[:, :].unsqueeze(1), [NT, NE]), ALU.add))
                for t in range(NT):
                    dve.max(top[:, t, :], score[:, t, :]).then_inc(pick_step, 1)
                step[0] += NT
                dve.wait_ge(pick_step, step[0])
                for t in range(NT):
                    dve.max_index(at[:, t, :], top[:, t, :], score[:, t, :]).then_inc(pick_step, 1)
                step[0] += NT
                dve.wait_ge(pick_step, step[0])
                then(dve.tensor_copy(at_f[:, :, :], at[:, :, :]))
                then(dve.tensor_reduce(wsum[:, :], top[:, :, 0:TOPK], AX_X, ALU.add))
                then(dve.tensor_scalar_add(wsum[:, :], wsum[:, :], 1e-20))
                then(dve.reciprocal(winv[:, :], wsum[:, :]))
                then(dve.tensor_tensor(tw[:, :, :], top[:, :, 0:TOPK], along(winv[:, :].unsqueeze(2), [NT, TOPK]), ALU.mult))
                for i in range(TOPK):
                    to = hit if i else cw
                    then(dve.tensor_tensor(to[:, :, :], along(number[:, :].unsqueeze(1), [NT, NE]),
                                           along(at_f[:, :, i:i + 1], [NT, NE]), ALU.is_equal))
                    then(dve.tensor_tensor(to[:, :, :], to[:, :, :], along(tw[:, :, i:i + 1], [NT, NE]), ALU.mult))
                    if i:
                        then(dve.tensor_tensor(cw[:, :, :], cw[:, :, :], hit[:, :, :], ALU.add))
                dve.sem_inc(added, 4)

                def expert(e, par, shared):
                    if shared:
                        dve.memset(cwe[:, par, :], 1.0).then_inc(cwe_ready, 1)
                    else:
                        dve.tensor_copy(cwe[:, par, :].unsqueeze(2), cw[:, :, bass.ds(e, 1)]).then_inc(cwe_ready, 1)
                    for m in range(ITEMS):
                        dve.wait_ge(gate_ready, e * ITEMS + m + 1)
                        dve.wait_ge(z_split, e * ITEMS + m + 1)
                        dve.tensor_tensor(z[:, m % 2, :], gate[:, m % 2, :], g.pair[m % 2][:, HALF:2 * HALF], ALU.mult)\
                            .then_inc(z_ready, 1)
                    dve.wait_ge(cwe_ready, e + 1)
                    for t in range(NT):
                        dve.wait_ge(out_ready, e * NT + t + 1 + NT)
                        dve.scalar_tensor_tensor(out=g.x[:, t, :], in0=g.bank(4 + t % 4), scalar=cwe[:, par, t:t + 1],
                                                 in1=g.x[:, t, :], op0=ALU.mult, op1=ALU.add).then_inc(added, 1)

                with dve.Fori(0, NE // 2) as pair:
                    for par in range(2):
                        expert(2 * pair + par, par, False)
                expert(NE, 0, True)


def build(nc, d, out):
    with ExitStack() as ctx:
        g = Shared(nc, ctx)
        constants(nc, g, d)
        steps = [
            lambda: attention16(nc, g, d, "L0a"),
            lambda: lora_ffn(nc, g, d, "L0f"),
            lambda: single_head(nc, g, d, "L0b"),
            lambda: lora_ffn(nc, g, d, "L0g"),
            lambda: attention128(nc, g, d, "L1a"),
            lambda: routed_ffn(nc, g, d, "L1f"),
            lambda: attention16(nc, g, d, "L1b"),
            lambda: routed_ffn(nc, g, d, "L1g"),
        ]
        for step in steps:
            step()
        store(nc, g, out)


def layouts(i):
    import numpy as np

    def chunks(w):
        w = np.asarray(w)
        return np.ascontiguousarray(w.reshape(-1, P, w.shape[1]).transpose(1, 0, 2))

    per = GH + 2
    order = [(g * per + j) * HD + e for g in range(NKV) for j in range(GH) for e in range(HD)]
    order += [(g * per + GH + s) * HD + e for s in range(2) for g in range(NKV) for e in range(HD)]
    a = {"x": np.ascontiguousarray(np.asarray(i["L0_attn_a_hidden_states"]).reshape(NT, P, H).transpose(1, 0, 2))}
    for name, src in (("L0a", "L0_attn_a"), ("L1b", "L1_attn_b")):
        a[name + "_wqkv"] = chunks(np.asarray(i[src + "_w_qkv"])[order].T)
        a[name + "_bqkv"] = np.asarray(i[src + "_b_qkv"])[order]
        a[name + "_wd"] = chunks(np.asarray(i[src + "_w_dense"]).T)
        a[name + "_bd"] = np.asarray(i[src + "_b_dense"])
    inv = (1.0 / np.float32(1000000.0) ** (np.arange(0, HD, 2, dtype=np.float32) / np.float32(HD))).astype(np.float32)
    ang = np.outer(np.arange(T, dtype=np.float32), inv).astype(np.float32)
    cos, sin = np.cos(ang), np.sin(ang)
    cos2 = np.concatenate([cos, cos], 1)
    sin2 = np.concatenate([-sin, sin], 1)
    scale = np.float32(-1.0 / HD)
    for name, tab in (("cos16", cos2), ("sin16", sin2)):
        both = np.stack([tab * scale, tab], 1).astype(np.float32)
        a[name] = np.ascontiguousarray(both.reshape(NT, P, 2, HD).transpose(1, 0, 2, 3))

    a["L0f_w"] = chunks(np.asarray(i["L0_ffn_W_up"]).T)
    lora_a = np.asarray(i["L0_ffn_lora_A"]).reshape(ZR, H)
    a["L0f_ga"] = chunks(np.concatenate([np.asarray(i["L0_ffn_gate_w"]), lora_a], 0).T)
    a["L0f_b"] = np.ascontiguousarray(np.asarray(i["L0_ffn_lora_B"]).transpose(0, 2, 1).reshape(ZR, H))
    a["L0f_bias"] = np.asarray(i["L0_ffn_expert_bias"])

    a["L0b_w"] = chunks(i["L0_attn_b_Wqkv"])
    b = np.asarray(i["L0_attn_b_bqkv"])
    a["L0b_bqk"] = np.ascontiguousarray(b[:2 * D].reshape(2, D).T)
    a["L0b_bv"] = b[2 * D:]
    a["L0b_wo"] = np.asarray(i["L0_attn_b_Wo"])
    a["L0b_bo"] = np.asarray(i["L0_attn_b_bo"])

    wq, wk, wv, wo = (np.asarray(i["L1_attn_a_" + s]) for s in ("Wq", "Wk", "Wv", "Wo"))
    a["L1a_w"] = np.empty((NKV * PIECES, P, H), wq.dtype)
    for grp in range(NKV):
        for pos, piece in enumerate(SPLIT_ORDER):
            if piece >= O_:
                h = grp * GH + piece - O_
                w = wo[h * D:(h + 1) * D]
            else:
                src, h = {K_: (wk, grp), V_: (wv, grp)}.get(piece, (wq, grp * GH + piece - Q_))
                w = chunks(src[:, h * D:(h + 1) * D]).reshape(P, H)
            a["L1a_w"][grp * PIECES + pos] = w
    bq, bk, bv = (np.asarray(i["L1_attn_a_" + s]) for s in ("bq", "bk", "bv"))
    a["L1a_bias"] = np.ascontiguousarray(np.concatenate(
        [bk.reshape(NKV, 1, D), bv.reshape(NKV, 1, D), bq.reshape(NKV, GH, D)], 1).transpose(2, 1, 0))
    a["L1a_bo"] = np.asarray(i["L1_attn_a_bo"])
    inv = (1.0 / np.float32(10000.0) ** (np.arange(0, D // 2, dtype=np.float32) / np.float32(D // 2))).astype(np.float32)
    ang = (inv[:, None] * np.arange(T, dtype=np.float32)[None, :]).astype(np.float32)
    a["cos128"] = np.concatenate([np.cos(ang), np.cos(ang)], 0)
    a["sin128"] = np.concatenate([-np.sin(ang), np.sin(ang)], 0)

    wg, wu, wd, sg, su, sd = (np.asarray(i["L1_ffn_" + s]) for s in ("Wg", "Wu", "Wd", "Sg", "Su", "Sd"))
    a["L1f_w"] = np.empty(((NE + 1) * WP, P, H), wg.dtype)
    for e in range(NE + 1):
        gg, uu, dd = (wg[e], wu[e], wd[e]) if e < NE else (sg, su, sd)
        a["L1f_w"][e * WP:e * WP + GU, :, 0:INNER] = gg.T.reshape(KC, P, INNER)
        a["L1f_w"][e * WP:e * WP + GU, :, INNER:H] = uu.T.reshape(KC, P, INNER)
        a["L1f_w"][e * WP + GU:(e + 1) * WP] = dd.T.reshape(IC, P, H)
    a["L1f_gate"] = chunks(np.asarray(i["L1_ffn_gate_w"]).T)
    a["L1f_bias"] = np.asarray(i["L1_ffn_bias"])
    return a


def kernel(**inputs):
    import numpy as np
    import concourse.bacc as bacc
    from concourse.bass_utils import run_bass_kernel_spmd

    nc = bacc.Bacc("TRN2", target_bir_lowering=False, num_devices=1)
    arrays, aps = {}, {}
    for name, v in layouts(inputs).items():
        arrays["in_" + name] = np.ascontiguousarray(v)
        aps[name] = nc.dram_tensor("in_" + name, v.shape, mybir.dt.from_np(v.dtype), kind="ExternalInput").ap()
    out = nc.dram_tensor("out", (P, NT, H), F32, kind="ExternalOutput").ap()
    build(nc, aps, out)
    got = run_bass_kernel_spmd(nc, [arrays], core_ids=[0]).results[0]["out"]
    return np.ascontiguousarray(got.transpose(1, 0, 2)).reshape(1, T, H)
```
